# Optimizing a Trainium2 kernel written in Bass

```python
import numpy as np
import jax
import jax.numpy as jnp

def _softmax(x, axis=-1):
    return jax.nn.softmax(x, axis=axis)

def _gelu(x):
    return jax.nn.gelu(x, approximate=True)

def _silu(x):
    return jax.nn.silu(x)

def _sigmoid(x):
    return jax.nn.sigmoid(x)

def _layernorm(x, axis=-1, eps=1e-05):
    m = jnp.mean(x, axis=axis, keepdims=True)
    v = jnp.var(x, axis=axis, keepdims=True)
    return (x - m) / jnp.sqrt(v + eps)

def _scatter_add(tgt, idx, src, axis=0):
    return tgt.at[idx].add(src)

def _segment_sum(src, seg, n):
    return jax.ops.segment_sum(src, seg, n)
kernel_name = 'mk_xattn_ffn_d2_seqx_r8_f8cb85'

def setup_inputs(seed: int=0):
    np.random.seed(seed)
    _w = jnp.asarray

    def _rec_inputs():
        import jax
        import jax.numpy as jnp
        _rk = jax.random.key(seed)
        x = 7.22e-05 + 1 * jax.random.normal(jax.random.fold_in(_rk, 1), (16, 128, 128), jnp.float32)
        _lenS = 128 - jax.random.randint(jax.random.fold_in(_rk, 7), (16,), 0, max(1, 128 // 4) + 1, jnp.int32)
        _lenS2 = 77 - jax.random.randint(jax.random.fold_in(_rk, 8), (16,), 0, max(1, 77 // 4) + 1, jnp.int32)
        _ctx_1024P = jax.random.normal(jax.random.fold_in(_rk, 11), (16, 16, 128), jnp.float32)
        _ctx_1024c = jax.random.dirichlet(jax.random.fold_in(_rk, 511), 0.3 * jnp.ones((16,), jnp.float32), (16, 77))
        _ctx_1024t = jnp.einsum('bsk,bkd->bsd', _ctx_1024c, _ctx_1024P)
        _ctx_1024t = _ctx_1024t * jax.lax.rsqrt(jnp.mean(jnp.square(_ctx_1024t)) + 1e-12) * 0.953939
        ctx_1024 = 4.13588e-05 + 0.999923 * (_ctx_1024t + 0.3 * jax.random.normal(jax.random.fold_in(_rk, 611), (16, 77, 128), jnp.float32))
        _validS = jnp.arange(128)[None, :] < _lenS[:, None]
        _validS2 = jnp.arange(77)[None, :] < _lenS2[:, None]
        _causal = jnp.tril(jnp.ones((128, 128), dtype=bool))
        mask_BxSxS2_fk0 = jnp.where(jnp.broadcast_to(_validS2[:, None, :], (16, 128, 77)), 0.0, 1.0).astype(jnp.float32)
        mask_Bx1xSxS2_bf1 = jnp.ones((16, 1, 128, 77), dtype=bool)
        return (x, ctx_1024, mask_BxSxS2_fk0, mask_Bx1xSxS2_bf1)
    x, ctx_1024, mask_BxSxS2_fk0, mask_Bx1xSxS2_bf1 = _rec_inputs()

    def _L0_xattn_setup():
        import jax, jax.numpy as jnp
        import numpy as np
        INPUT_DIM, ATTN_DIM, OUTPUT_DIM = (128, 128, 128)
        B, LQ, LKV = (4, 256, 256)
        key = jax.random.key(seed)
        ks = jax.random.split(key, 10)
        s = 1.0 / np.sqrt(INPUT_DIM)
        return {'primary': jax.random.normal(ks[0], (B, LQ, INPUT_DIM), jnp.float32), 'context_sequence': jax.random.normal(ks[1], (B, LKV, INPUT_DIM), jnp.float32), 'mask': jax.random.randint(ks[2], (B, LQ, LKV), 0, 2).astype(jnp.float32), 'Wq': jax.random.uniform(ks[3], (INPUT_DIM, ATTN_DIM), jnp.float32, -s, s), 'bq': jax.random.uniform(ks[4], (ATTN_DIM,), jnp.float32, -s, s), 'Wk': jax.random.uniform(ks[5], (INPUT_DIM, ATTN_DIM), jnp.float32, -s, s), 'bk': jax.random.uniform(ks[6], (ATTN_DIM,), jnp.float32, -s, s), 'Wv': jax.random.uniform(ks[7], (INPUT_DIM, OUTPUT_DIM), jnp.float32, -s, s), 'bv': jax.random.uniform(ks[8], (OUTPUT_DIM,), jnp.float32, -s, s)}
    _L0_xattn_all = _L0_xattn_setup()
    _L0_xattn_in = {k: v for k, v in _L0_xattn_all.items() if k in ('Wq', 'bq', 'Wk', 'bk', 'Wv', 'bv')}
    del _L0_xattn_all

    def _L0_ffn_setup():
        import jax, jax.numpy as jnp
        import numpy as np
        B, S, D, H, M, E, K = (4, 256, 128, 256, 64, 8, 2)

        def _layernorm(x, g, b, eps=1e-05):
            mu = x.mean(-1, keepdims=True)
            var = ((x - mu) ** 2).mean(-1, keepdims=True)
            return (x - mu) * jax.lax.rsqrt(var + eps) * g + b

        def _forward(inputs_embeds, enc_W, enc_b, s2c_W, s2c_b, rW1, rb1, rW2, rb2, We1, be1, We2, be2, c2s_W, c2s_b, dec_W, dec_b, ln_g, ln_b):
            b, s, _ = inputs_embeds.shape
            spikes_enc = jax.nn.sigmoid(inputs_embeds @ enc_W + enc_b)
            flat = spikes_enc.reshape(b * s, H)
            cont = flat @ s2c_W + s2c_b
            logits = jnp.tanh(cont @ rW1 + rb1) @ rW2 + rb2
            probs = jax.nn.softmax(logits, axis=-1)
            topw, topi = jax.lax.top_k(probs, K)
            w = topw / topw.sum(-1, keepdims=True)
            gates = (jax.nn.one_hot(topi, E, dtype=cont.dtype) * w[..., None]).sum(1)
            h = jax.nn.relu(jnp.einsum('nm,emh->enh', cont, We1) + be1[:, None, :])
            expert_out = jnp.einsum('enh,ehm->enm', h, We2) + be2[:, None, :]
            output_flat = jnp.einsum('enm,ne->nm', expert_out, gates)
            spikes_moe = jax.nn.sigmoid(output_flat @ c2s_W + c2s_b).reshape(b, s, H)
            decoded = jax.nn.sigmoid(spikes_moe @ dec_W + dec_b)
            return _layernorm(decoded, ln_g, ln_b)
        key = jax.random.key(seed)
        ks = jax.random.split(key, 10)
        r = lambda k, shape: jax.random.normal(k, shape, dtype=jnp.float32) * 0.02
        return {'inputs_embeds': jax.random.normal(ks[0], (B, S, D), dtype=jnp.float32), 'enc_W': r(ks[1], (D, H)), 'enc_b': jnp.zeros((H,), jnp.float32), 's2c_W': r(ks[2], (H, M)), 's2c_b': jnp.zeros((M,), jnp.float32), 'rW1': r(ks[3], (M, 64)), 'rb1': jnp.zeros((64,), jnp.float32), 'rW2': r(ks[4], (64, E)), 'rb2': jnp.zeros((E,), jnp.float32), 'We1': r(ks[5], (E, M, H // 2)), 'be1': jnp.zeros((E, H // 2), jnp.float32), 'We2': r(ks[6], (E, H // 2, M)), 'be2': jnp.zeros((E, M), jnp.float32), 'c2s_W': r(ks[7], (M, H)), 'c2s_b': jnp.zeros((H,), jnp.float32), 'dec_W': r(ks[8], (H, D)), 'dec_b': jnp.zeros((D,), jnp.float32), 'ln_g': jnp.ones((D,), jnp.float32), 'ln_b': jnp.zeros((D,), jnp.float32)}
    _L0_ffn_all = _L0_ffn_setup()
    _L0_ffn_in = {k: v for k, v in _L0_ffn_all.items() if k in ('enc_W', 'enc_b', 's2c_W', 's2c_b', 'rW1', 'rb1', 'rW2', 'rb2', 'We1', 'be1', 'We2', 'be2', 'c2s_W', 'c2s_b', 'dec_W', 'dec_b', 'ln_g', 'ln_b')}
    del _L0_ffn_all

    def _L1_xattn_setup():
        import jax, jax.numpy as jnp
        import numpy as np
        D_MODEL = 128
        NUM_HEADS = 16
        D_K = D_MODEL // NUM_HEADS
        B, S = (4, 256)
        key = jax.random.key(seed)
        ks = jax.random.split(key, 11)
        scale = 1.0 / np.sqrt(D_MODEL)
        inp = {'q': jax.random.normal(ks[0], (B, S, D_MODEL), dtype=jnp.float32), 'k': jax.random.normal(ks[1], (B, S, D_MODEL), dtype=jnp.float32), 'v': jax.random.normal(ks[2], (B, S, D_MODEL), dtype=jnp.float32), 'mask': jnp.ones((B, 1, S, S), dtype=bool), 'Wq': jax.random.normal(ks[3], (D_MODEL, D_MODEL), dtype=jnp.float32) * scale, 'bq': jax.random.normal(ks[4], (D_MODEL,), dtype=jnp.float32) * scale, 'Wk': jax.random.normal(ks[5], (D_MODEL, D_MODEL), dtype=jnp.float32) * scale, 'bk': jax.random.normal(ks[6], (D_MODEL,), dtype=jnp.float32) * scale, 'Wv': jax.random.normal(ks[7], (D_MODEL, D_MODEL), dtype=jnp.float32) * scale, 'bv': jax.random.normal(ks[8], (D_MODEL,), dtype=jnp.float32) * scale, 'W0': jax.random.normal(ks[9], (D_MODEL, D_MODEL), dtype=jnp.float32) * scale, 'b0': jax.random.normal(ks[10], (D_MODEL,), dtype=jnp.float32) * scale}
        return inp
    _L1_xattn_all = _L1_xattn_setup()
    _L1_xattn_in = {k: v for k, v in _L1_xattn_all.items() if k in ('Wq', 'bq', 'Wk', 'bk', 'Wv', 'bv', 'W0', 'b0')}
    del _L1_xattn_all

    def _L1_ffn_setup():
        import jax, jax.numpy as jnp
        import numpy as np
        DIM = 128
        NUM_EXPERTS = 8
        TOP_K = 2
        HIDDEN = int(DIM * 1.5)
        key = jax.random.key(seed)
        k_x, k_r, k_w1, k_w2, k_w3 = jax.random.split(key, 5)
        B, T = (2, 512)
        s_in = 1.0 / np.sqrt(DIM)
        s_h = 1.0 / np.sqrt(HIDDEN)
        return {'x': jax.random.normal(k_x, (B, T, DIM), dtype=jnp.float32), 'Wr': jax.random.uniform(k_r, (DIM, NUM_EXPERTS), minval=-s_in, maxval=s_in, dtype=jnp.float32), 'W1': jax.random.uniform(k_w1, (NUM_EXPERTS, DIM, HIDDEN), minval=-s_in, maxval=s_in, dtype=jnp.float32), 'W2': jax.random.uniform(k_w2, (NUM_EXPERTS, HIDDEN, DIM), minval=-s_h, maxval=s_h, dtype=jnp.float32), 'W3': jax.random.uniform(k_w3, (NUM_EXPERTS, DIM, HIDDEN), minval=-s_in, maxval=s_in, dtype=jnp.float32)}
    _L1_ffn_all = _L1_ffn_setup()
    _L1_ffn_in = {k: v for k, v in _L1_ffn_all.items() if k in ('Wr', 'W1', 'W2', 'W3')}
    del _L1_ffn_all
    return {'x': x, 'ctx_1024': ctx_1024, 'mask_BxSxS2_fk0': mask_BxSxS2_fk0, 'mask_Bx1xSxS2_bf1': mask_Bx1xSxS2_bf1, 'L0_xattn_Wq': _L0_xattn_in['Wq'], 'L0_xattn_bq': _L0_xattn_in['bq'], 'L0_xattn_Wk': _L0_xattn_in['Wk'], 'L0_xattn_bk': _L0_xattn_in['bk'], 'L0_xattn_Wv': _L0_xattn_in['Wv'], 'L0_xattn_bv': _L0_xattn_in['bv'], 'L0_ffn_enc_W': _L0_ffn_in['enc_W'], 'L0_ffn_enc_b': _L0_ffn_in['enc_b'], 'L0_ffn_s2c_W': _L0_ffn_in['s2c_W'], 'L0_ffn_s2c_b': _L0_ffn_in['s2c_b'], 'L0_ffn_rW1': _L0_ffn_in['rW1'], 'L0_ffn_rb1': _L0_ffn_in['rb1'], 'L0_ffn_rW2': _L0_ffn_in['rW2'], 'L0_ffn_rb2': _L0_ffn_in['rb2'], 'L0_ffn_We1': _L0_ffn_in['We1'], 'L0_ffn_be1': _L0_ffn_in['be1'], 'L0_ffn_We2': _L0_ffn_in['We2'], 'L0_ffn_be2': _L0_ffn_in['be2'], 'L0_ffn_c2s_W': _L0_ffn_in['c2s_W'], 'L0_ffn_c2s_b': _L0_ffn_in['c2s_b'], 'L0_ffn_dec_W': _L0_ffn_in['dec_W'], 'L0_ffn_dec_b': _L0_ffn_in['dec_b'], 'L0_ffn_ln_g': _L0_ffn_in['ln_g'], 'L0_ffn_ln_b': _L0_ffn_in['ln_b'], 'L1_xattn_Wq': _L1_xattn_in['Wq'], 'L1_xattn_bq': _L1_xattn_in['bq'], 'L1_xattn_Wk': _L1_xattn_in['Wk'], 'L1_xattn_bk': _L1_xattn_in['bk'], 'L1_xattn_Wv': _L1_xattn_in['Wv'], 'L1_xattn_bv': _L1_xattn_in['bv'], 'L1_xattn_W0': _L1_xattn_in['W0'], 'L1_xattn_b0': _L1_xattn_in['b0'], 'L1_ffn_Wr': _L1_ffn_in['Wr'], 'L1_ffn_W1': _L1_ffn_in['W1'], 'L1_ffn_W2': _L1_ffn_in['W2'], 'L1_ffn_W3': _L1_ffn_in['W3']}

def reference(x, ctx_1024, mask_BxSxS2_fk0, mask_Bx1xSxS2_bf1, L0_xattn_Wq, L0_xattn_bq, L0_xattn_Wk, L0_xattn_bk, L0_xattn_Wv, L0_xattn_bv, L0_ffn_enc_W, L0_ffn_enc_b, L0_ffn_s2c_W, L0_ffn_s2c_b, L0_ffn_rW1, L0_ffn_rb1, L0_ffn_rW2, L0_ffn_rb2, L0_ffn_We1, L0_ffn_be1, L0_ffn_We2, L0_ffn_be2, L0_ffn_c2s_W, L0_ffn_c2s_b, L0_ffn_dec_W, L0_ffn_dec_b, L0_ffn_ln_g, L0_ffn_ln_b, L1_xattn_Wq, L1_xattn_bq, L1_xattn_Wk, L1_xattn_bk, L1_xattn_Wv, L1_xattn_bv, L1_xattn_W0, L1_xattn_b0, L1_ffn_Wr, L1_ffn_W1, L1_ffn_W2, L1_ffn_W3):
    import jax
    import jax.numpy as jnp

    def _L0_xattn_ref(primary, context_sequence, mask, Wq, bq, Wk, bk, Wv, bv):
        import jax, jax.numpy as jnp
        import numpy as np
        INPUT_DIM, ATTN_DIM, OUTPUT_DIM = (128, 128, 128)
        B, LQ, LKV = (4, 256, 256)
        q = primary @ Wq + bq
        k = context_sequence @ Wk + bk
        v = context_sequence @ Wv + bv
        score = jnp.einsum('bqd,bkd->bqk', q, k) / jnp.sqrt(jnp.float32(ATTN_DIM))
        score = score + mask * -1000000000.0
        attn = jax.nn.softmax(score, axis=-1)
        return jnp.einsum('bqk,bkd->bqd', attn, v)

    def _L0_ffn_ref(inputs_embeds, enc_W, enc_b, s2c_W, s2c_b, rW1, rb1, rW2, rb2, We1, be1, We2, be2, c2s_W, c2s_b, dec_W, dec_b, ln_g, ln_b):
        import jax, jax.numpy as jnp
        import numpy as np
        B, S, D, H, M, E, K = (4, 256, 128, 256, 64, 8, 2)

        def _layernorm(x, g, b, eps=1e-05):
            mu = x.mean(-1, keepdims=True)
            var = ((x - mu) ** 2).mean(-1, keepdims=True)
            return (x - mu) * jax.lax.rsqrt(var + eps) * g + b

        def _forward(inputs_embeds, enc_W, enc_b, s2c_W, s2c_b, rW1, rb1, rW2, rb2, We1, be1, We2, be2, c2s_W, c2s_b, dec_W, dec_b, ln_g, ln_b):
            b, s, _ = inputs_embeds.shape
            spikes_enc = jax.nn.sigmoid(inputs_embeds @ enc_W + enc_b)
            flat = spikes_enc.reshape(b * s, H)
            cont = flat @ s2c_W + s2c_b
            logits = jnp.tanh(cont @ rW1 + rb1) @ rW2 + rb2
            probs = jax.nn.softmax(logits, axis=-1)
            topw, topi = jax.lax.top_k(probs, K)
            w = topw / topw.sum(-1, keepdims=True)
            gates = (jax.nn.one_hot(topi, E, dtype=cont.dtype) * w[..., None]).sum(1)
            h = jax.nn.relu(jnp.einsum('nm,emh->enh', cont, We1) + be1[:, None, :])
            expert_out = jnp.einsum('enh,ehm->enm', h, We2) + be2[:, None, :]
            output_flat = jnp.einsum('enm,ne->nm', expert_out, gates)
            spikes_moe = jax.nn.sigmoid(output_flat @ c2s_W + c2s_b).reshape(b, s, H)
            decoded = jax.nn.sigmoid(spikes_moe @ dec_W + dec_b)
            return _layernorm(decoded, ln_g, ln_b)
        return _forward(inputs_embeds, enc_W, enc_b, s2c_W, s2c_b, rW1, rb1, rW2, rb2, We1, be1, We2, be2, c2s_W, c2s_b, dec_W, dec_b, ln_g, ln_b)

    def _L1_xattn_ref(q, k, v, mask, Wq, bq, Wk, bk, Wv, bv, W0, b0):
        import jax, jax.numpy as jnp
        import numpy as np
        D_MODEL = 128
        NUM_HEADS = 16
        D_K = D_MODEL // NUM_HEADS
        B, S = (4, 256)
        query = q @ Wq.T + bq
        key_ = k @ Wk.T + bk
        value = v @ Wv.T + bv

        def split_heads(x):
            b, s, _ = x.shape
            return x.reshape(b, s, NUM_HEADS, D_K).transpose(0, 2, 1, 3)
        qh, kh, vh = (split_heads(query), split_heads(key_), split_heads(value))
        scores = jnp.einsum('bhsd,bhtd->bhst', qh, kh) / np.sqrt(D_K)
        scores = jnp.where(mask, scores, jnp.float32(-1000000000.0))
        weights = jax.nn.softmax(scores, axis=-1)
        out = jnp.einsum('bhst,bhtd->bhsd', weights, vh)
        out = out.transpose(0, 2, 1, 3).reshape(q.shape[0], -1, D_MODEL)
        return out @ W0.T + b0

    def _L1_ffn_ref(x, Wr, W1, W2, W3):
        import jax, jax.numpy as jnp
        import numpy as np
        DIM = 128
        NUM_EXPERTS = 8
        TOP_K = 2
        HIDDEN = int(DIM * 1.5)
        B, T, C = x.shape
        xf = x.reshape(-1, C)
        gate_logits = xf @ Wr
        w, idx = jax.lax.top_k(gate_logits, TOP_K)
        w = jax.nn.softmax(w, axis=-1)
        comb = jnp.sum(w[:, :, None] * jax.nn.one_hot(idx, NUM_EXPERTS, dtype=w.dtype), axis=1)
        h = jnp.einsum('nc,ech->neh', xf, W1)
        g = jnp.einsum('nc,ech->neh', xf, W3)
        y = jnp.einsum('neh,ehc->nec', jax.nn.silu(h) * g, W2)
        out = jnp.einsum('nec,ne->nc', y, comb)
        return out.reshape(B, T, C)
    x = x + _L0_xattn_ref(_layernorm(x, axis=-1), ctx_1024, mask_BxSxS2_fk0, L0_xattn_Wq, L0_xattn_bq, L0_xattn_Wk, L0_xattn_bk, L0_xattn_Wv, L0_xattn_bv)
    x = x + _L0_ffn_ref(_layernorm(x, axis=-1), L0_ffn_enc_W, L0_ffn_enc_b, L0_ffn_s2c_W, L0_ffn_s2c_b, L0_ffn_rW1, L0_ffn_rb1, L0_ffn_rW2, L0_ffn_rb2, L0_ffn_We1, L0_ffn_be1, L0_ffn_We2, L0_ffn_be2, L0_ffn_c2s_W, L0_ffn_c2s_b, L0_ffn_dec_W, L0_ffn_dec_b, L0_ffn_ln_g, L0_ffn_ln_b)
    x = x + _L1_xattn_ref(_layernorm(x, axis=-1), ctx_1024, ctx_1024, mask_Bx1xSxS2_bf1, L1_xattn_Wq, L1_xattn_bq, L1_xattn_Wk, L1_xattn_bk, L1_xattn_Wv, L1_xattn_bv, L1_xattn_W0, L1_xattn_b0)
    x = x + _L1_ffn_ref(_layernorm(x, axis=-1), L1_ffn_Wr, L1_ffn_W1, L1_ffn_W2, L1_ffn_W3)
    return x

_drawn_inputs = setup_inputs


def setup_inputs(seed=0):
    import zlib

    import numpy as np

    out = dict(_drawn_inputs(seed))
    spreads = {'L0_ffn_enc_b': (0.0, 0.8),
     'L0_ffn_s2c_b': (0.0, 0.8),
     'L0_ffn_rb1': (0.0, 0.8),
     'L0_ffn_rb2': (0.0, 0.8),
     'L0_ffn_be1': (0.0, 0.8),
     'L0_ffn_be2': (0.0, 0.8),
     'L0_ffn_c2s_b': (0.0, 0.289),
     'L0_ffn_dec_b': (0.0, 0.1),
     'L0_ffn_ln_g': (1.0, 0.2),
     'L0_ffn_ln_b': (0.0, 0.1)}
    factors = {'L0_xattn_bq': 8.0,
     'L0_xattn_bk': 8.0,
     'L0_ffn_enc_W': 8.0,
     'L0_ffn_s2c_W': 8.0,
     'L0_ffn_rW1': 8.0,
     'L0_ffn_rW2': 8.0,
     'L0_ffn_We1': 8.0,
     'L0_ffn_We2': 8.0,
     'L0_ffn_c2s_W': 8.0,
     'L1_xattn_bq': 4.103,
     'L1_xattn_bk': 8.0}
    for name, (base, spread) in spreads.items():
        noise = np.random.default_rng([zlib.crc32(name.encode()), seed]).standard_normal(out[name].shape)
        drawn = base * np.exp(spread * noise) if base else spread * noise
        out[name] = jnp.asarray(drawn.astype(out[name].dtype))
    for name, factor in factors.items():
        out[name] = (out[name] * factor).astype(out[name].dtype)
    return out
```

```python
from contextlib import ExitStack

import concourse.bass as bass
import numpy as np
from concourse import mybir
from concourse.alu_op_type import AluOpType as ALU

F32 = mybir.dt.float32
BF16 = mybir.dt.bfloat16
ACT = mybir.ActivationFunctionType
AX = mybir.AxisListType
ds = bass.ds

P = 128
B, S, D = 16, 128, 128
SC = 77
TPG = 4
G = B // TPG
N = TPG * S
NH, DH = 16, 8
E = 8
H0, M0 = 256, 64
HX = H0 // 2
H1 = 192
NB = E * H1 // P
SA = 64
SB = SC - SA
NA = NH // 2
RB = E * SB
CA, CB = NH * SA, NH * SB
DV = DH + 1
CT = 2 * SA + RB
HIDDEN = -float(2 ** 100)
EPS = 1e-5
NEG_BIG = -1e38


def xattn_ffn_program(nc, a, out):
    ctx = ExitStack()
    with ctx:
        def sb(name, shape, dt=F32):
            return ctx.enter_context(nc.sbuf_tensor(name, shape, dt))

        def sem(name):
            return ctx.enter_context(nc.semaphore(name))

        x = sb("x", [P, B * D])
        room_a = sb("room_a", [P, B * D])
        room_b = sb("room_b", [P, B * D])
        room_c = sb("room_c", [P, 2, B * SC])
        room_d = sb("room_d", [P, B * D])
        ctx_a = room_a[:].rearrange("p (b d) -> p b d", b=B)
        ctx_b = room_b[0:RB, :].rearrange("p (b d) -> p b d", b=B)
        ctxT = sb("ctxT", [P, B, CT])
        k0T = room_c[:, 0, :]
        v0 = room_d[0:SC, :]
        k1T = sb("k1T", [P, B, SC])
        v1a = sb("v1a", [P, B * NA, 2, DV])
        v1b = sb("v1b", [RB, B * 2, E, DV])
        kblk = sb("kblk", [P, 4, CA + CB])
        mask0 = room_c[:, 1, :]
        mask1 = sb("mask1", [P, B, SC], mybir.dt.uint8)
        hide1 = sb("hide1", [P, B, SC], BF16)

        wq0 = sb("wq0", [P, D])
        wk0 = sb("wk0", [P, D])
        wv0 = sb("wv0", [P, D])
        bv0 = sb("bv0", [SC, D])
        enc_w = sb("enc_w", [P, H0])
        s2c_w = sb("s2c_w", [P, 2, 2, M0])
        r_w1 = sb("r_w1", [P, 2, M0])
        r_w2 = sb("r_w2", [M0 + 1, E])
        we1 = sb("we1", [P, E, HX])
        we2 = sb("we2", [P, E, M0])
        c2s_w = sb("c2s_w", [P, H0])
        dec_w = sb("dec_w", [P, 2, D])
        ln_g = sb("ln_g", [P, D])
        ln_b = sb("ln_b", [P, D])
        w1raw = sb("w1raw", [P, 4, D])
        w1T = sb("w1T", [P, 4, D])
        wr = sb("wr", [P, E])
        f_w1 = sb("f_w1", [P, E * H1])
        f_w3 = sb("f_w3", [P, E * H1])
        f_w2 = sb("f_w2", [P, NB, D])

        ROWS = ["bq0", "bk0", "enc0", "enc1", "rb1", "s2c"] + [f"be1_{e}" for e in range(E)] + \
               ["c2s0", "c2s1", "bq1", "bk1", "bv1"]
        NR = len(ROWS)
        vrows = sb("vrows", [NR, P])
        vcols = sb("vcols", [P, NR])

        def col(name, rows=P):
            i = ROWS.index(name)
            return vcols[0:rows, i:i + 1]

        NBE, NBD = E * M0, 2 * D
        brow = sb("brow", [3, NBE + NBD])
        NBR = NBE + NBD
        early = kblk[0:3, :, :].rearrange("p r c -> p (r c)")
        bres = early[:, 0:2 * NBR].rearrange("p (i n) -> p i n", i=2)
        bsel = early[:, 2 * NBR:4 * NBR].rearrange("p (i n) -> p i n", i=2)
        bpart = early[:, 4 * NBR:4 * NBR + 3 * NBR // 2].bitcast(BF16).rearrange("p (i n) -> p i n", i=3)
        bsplit = sb("bsplit", [3, NBE + NBD], BF16)
        ones3 = sb("ones3", [3, P], BF16)

        ident = sb("ident", [P, P])
        ident_h = sb("ident_h", [P, P], BF16)
        head_of = sb("head_of", [P, NH])
        slot_of = sb("slot_of", [RB, E])
        rank = sb("rank", [P, E])
        half = sb("half", [P, TPG])
        esel = sb("esel", [96, NB * P], BF16)

        stats = sb("stats", [P, TPG, 6])
        mom = sb("mom", [P, 6, TPG])
        rstd = sb("rstd", [P, TPG])
        xn = sb("xn", [P, TPG, D])
        xnT = sb("xnT", [P, N])
        wideT = sb("wideT", [P, G * N])
        q0T = sb("q0T", [P, N])
        e0 = sb("e0", [P, TPG, SC])
        m0 = sb("m0", [P, TPG])
        sum0 = sb("sum0", [P, TPG])
        r0 = sb("r0", [P, TPG])
        at0T = sb("at0T", [SC, N])
        spT = sb("spT", [P, 2, N])
        tT = sb("tT", [M0 + 1, N])
        hT = sb("hT", [P, 4, N])
        gy = sb("gy", [P, 2, N])
        gh = sb("gh", [P, 2, N // 2])
        oT = q0T
        sp2T = spT
        dc = sb("dc", [P, TPG, D])
        dn = sb("dn", [P, TPG, D])
        dg = sb("dg", [P, TPG, D])
        xb = sb("xb", [P, TPG * D])
        stats2 = sb("stats2", [P, TPG, 6])
        mom2 = sb("mom2", [P, 6, TPG])
        rstd2 = sb("rstd2", [P, TPG])
        lg = sb("lg", [P, B, E])
        lg2 = sb("lg2", [P, B, E])
        geq = sb("geq", [P, 2, B, E])
        gkey = sb("gkey", [P, 2, B, E])
        goh = sb("goh", [P, 2, B, E])
        gmx = sb("gmx", [P, 2, B])
        gkx = sb("gkx", [P, 2, B])
        gd = sb("gd", [P, B])
        gw = sb("gw", [P, 2, B])
        gwo = sb("gwo", [P, 2, B, E])
        gates = sb("gates", [P, B, E])
        gres = sb("gres", [P, 2, B, E])
        gsp = hT[:].rearrange("p i n -> p (i n)")[:, 0:B * 48].bitcast(BF16).rearrange("p (b c) -> p b c", b=B)
        gT = gy[0:96].rearrange("p i n -> p (i n)").bitcast(BF16)
        qt = sb("qt", [P, 2, P])
        e1 = room_c
        mxa = sb("mxa", [P, NH])
        mxb = sb("mxb", [P, NH])
        mx = sb("mx", [P, NH])
        pTa = room_a[:].rearrange("p (i n) -> p i n", i=2)
        pTb = sb("pTb", [RB, 2, 2 * P])
        rs1 = sb("rs1", [P, NH])
        at1 = sb("at1", [P, 2, NH, DH])
        at1T = sb("at1T", [P, P])
        sil = room_b[:, 0:2 * N].rearrange("p (i n) -> p i n", i=2)
        u1 = room_b[:, 2 * N:4 * N].rearrange("p (i n) -> p i n", i=2)
        act = room_d[:, 0:3 * N].rearrange("p (i n) -> p i n", i=3)

        bank = [ctx.enter_context(nc.psum_tensor(f"bank{i}", [P, 512], F32)) for i in range(8)]

        ld_x = sem("ld_x")
        ld_ctx = sem("ld_ctx")
        ld_rows = sem("ld_rows")
        ld_w0 = sem("ld_w0")
        ld_m0 = sem("ld_m0")
        ld_m1 = sem("ld_m1")
        ld_w1 = sem("ld_w1")
        ld_bias = sem("ld_bias")
        ld_f0 = sem("ld_f0")
        ld_f1 = sem("ld_f1")
        stored = sem("stored")
        c_id = sem("c_id")
        c_idh = sem("c_idh")
        c_sel = sem("c_sel")
        c_esel = sem("c_esel")
        c_zero = sem("c_zero")
        c_ones = sem("c_ones")
        c_misc = sem("c_misc")
        c_step = sem("c_step")
        c_split = sem("c_split")
        vc_ps = sem("vc_ps")
        vc_done = sem("vc_done")
        w1T_ps = sem("w1T_ps")
        w1T_done = sem("w1T_done")
        ctxT_ps = sem("ctxT_ps")
        ctxT_dve = sem("ctxT_dve")
        ctxT_act = sem("ctxT_act")
        k_ps = sem("k_ps")
        k0_done = sem("k0_done")
        k1_done = sem("k1_done")
        v0_ps = sem("v0_ps")
        v0_done = sem("v0_done")
        v1_ps = sem("v1_ps")
        v1_even = sem("v1_even")
        v1_odd = sem("v1_odd")
        v1_b = sem("v1_b")
        hide_done = sem("hide_done")
        kb_done = sem("kb_done")
        ln_stats = sem("ln_stats")
        ln_moments = sem("ln_moments")
        ln_steps = sem("ln_steps")
        ln_rstd = sem("ln_rstd")
        ln_applied = sem("ln_applied")
        xnT_ps = sem("xnT_ps")
        xnT_done = sem("xnT_done")
        q0_ps = sem("q0_ps")
        q0_done = sem("q0_done")
        s0_ps = sem("s0_ps")
        s0_masked = sem("s0_masked")
        m0_done = sem("m0_done")
        s0_shifted = sem("s0_shifted")
        e0_done = sem("e0_done")
        sum0_done = sem("sum0_done")
        r0_done = sem("r0_done")
        at0_ps = sem("at0_ps")
        at0_done = sem("at0_done")
        o0_ps = sem("o0_ps")
        x1_done = sem("x1_done")
        enc_ps = sem("enc_ps")
        sp_done = sem("sp_done")
        cont_ps = sem("cont_ps")
        cont_done = sem("cont_done")
        r1_ps = sem("r1_ps")
        t_done = sem("t_done")
        lg_ps = sem("lg_ps")
        g_step = sem("g_step")
        gd_done = sem("gd_done")
        gw_done = sem("gw_done")
        gates_done = sem("gates_done")
        h_ps = sem("h_ps")
        h_act = sem("h_act")
        h_dve = sem("h_dve")
        y_ps = sem("y_ps")
        gy_done = sem("gy_done")
        gh_done = sem("gh_done")
        acc_ps = sem("acc_ps")
        oT_done = sem("oT_done")
        c2s_ps = sem("c2s_ps")
        sp2_done = sem("sp2_done")
        dec_ps = sem("dec_ps")
        dc_done = sem("dc_done")
        lo_stats = sem("lo_stats")
        lo_moments = sem("lo_moments")
        lo_steps = sem("lo_steps")
        lo_rstd = sem("lo_rstd")
        dn_done = sem("dn_done")
        dg_done = sem("dg_done")
        xb_done = sem("xb_done")
        x2_done = sem("x2_done")
        q1_ps = sem("q1_ps")
        q1_done = sem("q1_done")
        qt_done = sem("qt_done")
        s1_ps = sem("s1_ps")
        mxab_done = sem("mxab_done")
        mx_done = sem("mx_done")
        s1_shifted = sem("s1_shifted")
        e1_done = sem("e1_done")
        pTa_ps = sem("pTa_ps")
        pTb_ps = sem("pTb_ps")
        pTa_done = sem("pTa_done")
        pTb_done = sem("pTb_done")
        o1_ps = sem("o1_ps")
        rs1_done = sem("rs1_done")
        at1_done = sem("at1_done")
        at1T_ps = sem("at1T_ps")
        at1T_done = sem("at1T_done")
        y1_ps = sem("y1_ps")
        x3_done = sem("x3_done")
        wide_done = sem("wide_done")
        gsp_done = sem("gsp_done")
        gT_ps = sem("gT_ps")
        gT_done = sem("gT_done")
        fh_ps = sem("fh_ps")
        fg_ps = sem("fg_ps")
        gb_ps = sem("gb_ps")
        sil_done = sem("sil_done")
        u1_done = sem("u1_done")
        act_done = sem("act_done")
        fy_ps = sem("fy_ps")
        res_done = sem("res_done")

        N_CTX = 2 + E
        N_ROWS = 12
        N_W0 = 4
        N_W1 = 4
        N_F0 = 14
        N_BIAS = 3
        N_F1 = 4
        LN_A, LN_B, LN_C, LN_D = 0, G, 2 * G, 3 * G

        block = ctx.enter_context(nc.Block())

        @block.sync
        def _(sp):
            ctx_d = a["ctx_1024"].rearrange("b s d -> s b d")
            for r in range(2):
                sp.dma_start(ctx_a[SA * r:SA * (r + 1)], ctx_d[0:SA]).then_inc(ld_ctx, 16)
            for r in range(E):
                sp.dma_start(ctx_b[SB * r:SB * (r + 1)], ctx_d[SA:SC]).then_inc(ld_ctx, 16)
            sp.dma_start(x[:, :].rearrange("p (b d) -> p b d", b=B),
                         a["x"].rearrange("b s d -> s b d")).then_inc(ld_x, 16)
            sp.dma_start(mask0[:, :].rearrange("p (b s) -> p b s", b=B),
                         a["mask_BxSxS2_fk0"].rearrange("b t s -> t b s")).then_inc(ld_m0, 16)
            sp.dma_start(mask1[:], a["mask_Bx1xSxS2_bf1"].rearrange("b o t s -> t (b o) s")).then_inc(ld_m1, 16)
            sp.dma_start(brow[:, 0:NBE], a["L0_ffn_be2"].rearrange("e m -> (e m)").unsqueeze(0)
                         .broadcast_to([3, NBE])).then_inc(ld_bias, 16)
            for i, name in enumerate(("L0_ffn_dec_b", "L1_xattn_b0")):
                sp.dma_start(brow[:, NBE + D * i:NBE + D * (i + 1)],
                             a[name].unsqueeze(0).broadcast_to([3, D])).then_inc(ld_bias, 16)
            sp.dma_start(enc_w[:], a["L0_ffn_enc_W"]).then_inc(ld_f0, 16)
            for r in range(2):
                sp.dma_start(s2c_w[:, :, r, :],
                             a["L0_ffn_s2c_W"].rearrange("(k p) m -> p k m", p=P)).then_inc(ld_f0, 16)
            for r in range(2):
                sp.dma_start(r_w1[0:M0, r, :], a["L0_ffn_rW1"]).then_inc(ld_f0, 16)
            sp.dma_start(r_w2[0:M0, :], a["L0_ffn_rW2"]).then_inc(ld_f0, 16)
            sp.dma_start(r_w2[M0:M0 + 1, :], a["L0_ffn_rb2"].unsqueeze(0)).then_inc(ld_f0, 16)
            sp.dma_start(we1[0:M0], a["L0_ffn_We1"].rearrange("e m h -> m e h")).then_inc(ld_f0, 16)
            sp.dma_start(we2[:], a["L0_ffn_We2"].rearrange("e h m -> h e m")).then_inc(ld_f0, 16)
            for r in range(2):
                sp.dma_start(c2s_w[M0 * r:M0 * (r + 1), :], a["L0_ffn_c2s_W"]).then_inc(ld_f0, 16)
            sp.dma_start(dec_w[:], a["L0_ffn_dec_W"].rearrange("(k p) m -> p k m", p=P)).then_inc(ld_f0, 16)
            sp.dma_start(ln_g[:], a["L0_ffn_ln_g"].unsqueeze(0).broadcast_to([P, D])).then_inc(ld_f0, 16)
            sp.dma_start(ln_b[:], a["L0_ffn_ln_b"].unsqueeze(0).broadcast_to([P, D])).then_inc(ld_f0, 16)
            sp.dma_start(wr[:], a["L1_ffn_Wr"]).then_inc(ld_f1, 16)
            sp.dma_start(f_w1[:, :].rearrange("p (e h) -> p e h", e=E),
                         a["L1_ffn_W1"].rearrange("e c h -> c e h")).then_inc(ld_f1, 16)
            sp.dma_start(f_w3[:, :].rearrange("p (e h) -> p e h", e=E),
                         a["L1_ffn_W3"].rearrange("e c h -> c e h")).then_inc(ld_f1, 16)
            sp.dma_start(f_w2[:], a["L1_ffn_W2"].rearrange("e h c -> (e h) c")
                         .rearrange("(j p) c -> p j c", p=P)).then_inc(ld_f1, 16)
            out_v = out.rearrange("b s d -> s b d")
            for g in range(G):
                sp.wait_ge(res_done, g + 1)
                sp.dma_start(out_v[:, TPG * g:TPG * (g + 1), :],
                             x[:, N * g:N * (g + 1)].rearrange("p (b d) -> p b d", d=D)).then_inc(stored, 16)
            sp.wait_ge(stored, 16 * G)

        @block.gpsimd
        def _(pool):
            pool.memset(ident[:], 0.0).then_inc(c_id, 1)
            pool.wait_ge(c_id, 1)
            pool.affine_select(out=ident[:], in_=ident[:], compare_op=ALU.not_equal, fill=1.0, base=0,
                               pattern=[[-1, P]], channel_multiplier=1).then_inc(c_id, 1)
            pool.memset(half[:], -0.5).then_inc(c_sel, 1)
            for e in range(E):
                pool.memset(rank[:, e:e + 1], float(E - e)).then_inc(c_sel, 1)
            pool.memset(head_of[:], 1.0).then_inc(c_sel, 1)
            pool.memset(slot_of[:], 1.0).then_inc(c_sel, 1)
            pool.wait_ge(c_sel, E + 3)
            pool.memset(tT[M0:M0 + 1, :], 1.0).then_inc(c_misc, 1)
            pool.wait_ge(c_misc, 1)
            pool.memset(ones3[:], 1.0).then_inc(c_misc, 1)
            pool.wait_ge(c_misc, 2)
            pool.memset(r_w1[M0:P], 0.0).then_inc(c_misc, 1)
            pool.memset(we1[M0:P], 0.0).then_inc(c_misc, 1)
            pool.wait_ge(c_misc, 4)
            for i, (m, w) in enumerate(((head_of, DH), (slot_of, SB))):
                n = NH if i == 0 else E
                pool.wait_ge(c_sel, E + 3 + 2 * i)
                pool.affine_select(out=m[:], in_=m[:], compare_op=ALU.is_ge, fill=0.0, base=0,
                                   pattern=[[-w, n]], channel_multiplier=1).then_inc(c_sel, 1)
                pool.wait_ge(c_sel, E + 4 + 2 * i)
                pool.affine_select(out=m[:], in_=m[:], compare_op=ALU.is_ge, fill=0.0, base=w - 1,
                                   pattern=[[w, n]], channel_multiplier=-1).then_inc(c_sel, 1)
            pool.memset(v1a[:], 0.0).then_inc(c_zero, 1)
            pool.wait_ge(c_zero, 1)
            pool.wait_ge(c_sel, E + 7)
            pool.memset(v1a[0:SA, :, 0, DH:DV], 1.0).then_inc(c_ones, 1)
            pool.wait_ge(c_ones, 1)
            pool.memset(v1a[SA:P, :, 1, DH:DV], 1.0).then_inc(c_ones, 1)
            pool.wait_ge(c_ones, 2)
            pool.tensor_copy(v1b[:, :, :, DH], slot_of[:].unsqueeze(1).broadcast_to([RB, 2 * B, E])).then_inc(c_ones, 1)

            pool.wait_ge(ld_m1, 16)
            pool.tensor_scalar(hide1[:], mask1[:], -HIDDEN, HIDDEN, ALU.mult, ALU.add).then_inc(hide_done, 1)

            def ln_scale(n):
                pool.wait_ge(ln_moments, n + 1)
                pool.wait_ge(ln_applied, n * TPG)
                pool.tensor_tensor(rstd[:], mom[:, 5, :], half[:], ALU.pow).then_inc(ln_rstd, 1)

            pool.wait_ge(c_sel, 1)
            with pool.Fori(LN_A, LN_B) as n:
                ln_scale(n)

            pool.memset(esel[0:32, :], 1.0).then_inc(c_esel, 1)
            pool.wait_ge(c_esel, 1)
            pool.affine_select(out=esel[0:32, :], in_=esel[0:32, :], compare_op=ALU.is_ge, fill=0.0, base=0,
                               pattern=[[1, NB * P]], channel_multiplier=-H1).then_inc(c_esel, 1)
            pool.wait_ge(c_esel, 2)
            pool.affine_select(out=esel[0:32, :], in_=esel[0:32, :], compare_op=ALU.is_ge, fill=0.0, base=H1 - 1,
                               pattern=[[-1, NB * P]], channel_multiplier=H1).then_inc(c_esel, 1)

            with pool.Fori(LN_B, LN_C) as n:
                ln_scale(n)

            def key_block(b, slot):
                for lo, n_s, off in ((0, SA, 0), (SA, SB, CA)):
                    pool.tensor_tensor(
                        kblk[:, slot, off:off + NH * n_s].rearrange("p (h s) -> p h s", h=NH),
                        k1T[:, ds(b, 1), lo:lo + n_s].broadcast_to([P, NH, n_s]),
                        head_of[:].unsqueeze(2).broadcast_to([P, NH, n_s]), ALU.mult).then_inc(kb_done, 1)

            def mix0_sums(g):
                for t in range(TPG):
                    pool.wait_ge(gy_done, TPG * g + t + 1)
                    pool.wait_ge(acc_ps, TPG * g + t - 1 if t >= 1 else TPG * g)
                    pool.tensor_tensor(gh[:, t % 2, :], gy[:, t % 2, 0:N // 2], gy[:, t % 2, N // 2:N],
                                       ALU.add).then_inc(gh_done, 1)

            def mix0_out(g):
                pool.wait_ge(x2_done, g)
                pool.tensor_tensor(xb[:].rearrange("p (t d) -> p t d", t=TPG),
                                   x[:, ds(g * N, N)].rearrange("p (t d) -> p t d", t=TPG),
                                   ln_b[:].unsqueeze(1).broadcast_to([P, TPG, D]), ALU.add).then_inc(xb_done, 1)
                pool.wait_ge(lo_moments, g + 1)
                pool.tensor_tensor(rstd2[:], mom2[:, 5, :], half[:], ALU.pow).then_inc(lo_rstd, 1)

            pool.wait_ge(ld_f0, 16 * N_F0)
            pool.wait_ge(k1_done, 3)
            pool.wait_ge(c_split, 1)
            for b in range(2):
                key_block(b, b)
            with pool.Fori(0, G) as g:
                mix0_sums(g)
                mix0_out(g)

            with pool.Fori(LN_C, LN_D) as n:
                ln_scale(n)

            def scores_inputs(b, j, more):
                since(pool, s1_ps, b, -1)
                pool.tensor_copy(qt[:, j % 2, :], wideT[:, ds(b * P, P)]).then_inc(qt_done, 1)
                if more:
                    key_block(b + 2, (j + 2) % 4)

            pool.wait_ge(y_ps, G * E)
            pool.memset(gsp[:], 0.0).then_inc(c_misc, 1)
            pool.wait_ge(q1_done, G)
            for b in range(4):
                scores_inputs(b, b, True)
            with pool.Fori(1, G - 1) as i:
                for j in range(4):
                    scores_inputs(i * 4 + j, j, True)
            for b in range(B - 4, B):
                scores_inputs(b, b % 4, b + 2 < B)

            with pool.Fori(LN_D, LN_D + G) as n:
                ln_scale(n)

        @block.tensor
        def _(pe):
            mm, tr = nc.tensor.matmul, nc.tensor.transpose
            pe.wait_ge(c_id, 2)
            pe.wait_ge(ld_rows, 16 * N_ROWS)
            tr(bank[7][:, 0:NR], vrows[:], ident[0:NR, 0:NR]).then_inc(vc_ps, 1)
            pe.wait_ge(ld_ctx, 16 * N_CTX)
            for i in range(B // 2):
                if i >= 4:
                    pe.wait_ge(ctxT_dve if i % 2 == 0 else ctxT_act, (i - 4) // 2 + 1)
                for r in range(2):
                    b, o = 2 * i + r, CT * r
                    tr(bank[i % 4][:, o:o + 2 * SA], ctx_a[:, b, :], ident[:])
                    last = tr(bank[i % 4][:, o + 2 * SA:o + CT], ctx_b[:, b, :], ident[0:RB, 0:RB])
                last.then_inc(ctxT_ps, 1)
            pe.wait_ge(ctxT_dve, B // 4)
            pe.wait_ge(ctxT_act, B // 4)
            pe.wait_ge(ld_w0, 16 * N_W0)

            def keys(w, i, bk):
                n = min(6, B - 6 * i)
                mm(bank[bk][:, 0:n * SC], w, ctxT[:, 6 * i:6 * i + n, SA:SA + SC],
                   start=True, stop=True).then_inc(k_ps, 1)

            for i in range(3):
                if i == 2:
                    pe.wait_ge(k0_done, 1)
                keys(wk0[:], i, 4 + i % 2)
            for i in range(G):
                for t in range(TPG):
                    last = mm(bank[i][0:SC, D * t:D * (t + 1)], ctxT[:, TPG * i + t, SA:SA + SC], wv0[:],
                              start=True, stop=True)
                last.then_inc(v0_ps, 1)

            def ln_transpose(n):
                pe.wait_ge(ln_applied, TPG * n + TPG)
                pe.wait_ge(xnT_done, n)
                for t in range(TPG):
                    last = tr(bank[7][:, P * t:P * (t + 1)], xn[:, t, :], ident[:])
                last.then_inc(xnT_ps, 1)

            def q0(g):
                pe.wait_ge(xnT_done, g + 1)
                pe.wait_ge(q0_done, g)
                mm(bank[1][:], wq0[:], xnT[:], start=True, stop=True).then_inc(q0_ps, 1)

            def attend0(g):
                pe.wait_ge(q0_done, g + 1)
                pe.wait_ge(s0_masked, g)
                for t in range(TPG):
                    last = mm(bank[2][:, SC * t:SC * (t + 1)], q0T[:, P * t:P * (t + 1)],
                              k0T[:, ds(g * (TPG * SC) + t * SC, SC)], start=True, stop=True)
                last.then_inc(s0_ps, 1)
                pe.wait_ge(e0_done, g + 1)
                pe.wait_ge(at0_done, g)
                for t in range(TPG):
                    last = tr(bank[3][0:SC, P * t:P * (t + 1)], e0[:, t, :], ident[:])
                last.then_inc(at0_ps, 1)
                pe.wait_ge(at0_done, g + 1)
                pe.wait_ge(x1_done, TPG * g)
                for t in range(TPG):
                    last = mm(bank[4][:, P * t:P * (t + 1)], at0T[:, P * t:P * (t + 1)],
                              v0[:, ds(g * N + t * P, P)], start=True, stop=True)
                last.then_inc(o0_ps, 1)

            pe.wait_ge(vc_done, 1)
            ln_transpose(LN_A)
            pe.wait_ge(v0_done, G)
            pe.wait_ge(k0_done, 3)
            q0(0)
            with pe.Fori(0, G - 1) as g:
                attend0(g)
                ln_transpose(g + 1)
                q0(g + 1)
            attend0(G - 1)

            pe.wait_ge(ld_w1, 16 * N_W1)
            for i in range(4):
                last = tr(bank[6][:, P * i:P * (i + 1)], w1raw[:, i, :], ident[:])
            last.then_inc(w1T_ps, 1)
            pe.wait_ge(w1T_done, 1)
            for i, bk in enumerate((5, 0, 5)):
                if i == 2:
                    pe.wait_ge(k1_done, 1)
                keys(w1T[:, 1, :], i, bk)
            pe.wait_ge(x1_done, B)
            pe.wait_ge(k1_done, 3)
            pe.wait_ge(xnT_done, G)
            for i in range(G):
                for t in range(TPG):
                    b, o = TPG * i + t, D * t
                    mm(bank[1 + i][:, o:o + D], ctxT[:, b, 0:2 * SA], w1T[:, 2, :], start=True, stop=True)
                    last = mm(bank[(0, 5, 6, 7)[i]][0:RB, o:o + D], ctxT[:, b, 2 * SA:CT], w1T[:, 2, :],
                              start=True, stop=True)
                last.then_inc(v1_ps, 1)
            pe.wait_ge(v1_b, G)
            pe.wait_ge(v1_odd, G)

            pe.wait_ge(ld_f0, 16 * N_F0)
            pe.wait_ge(c_misc, 4)

            def encode(g):
                pe.wait_ge(xnT_done, LN_B + g + 1)
                pe.wait_ge(sp_done, 2 * g)
                for k in range(2):
                    mm(bank[1 + k][:], enc_w[:, P * k:P * (k + 1)], xnT[:], start=True, stop=True).then_inc(enc_ps, 1)

            def route(g):
                pe.wait_ge(sp_done, 2 * g + 2)
                pe.wait_ge(cont_done, g)
                for k in range(2):
                    last = mm(bank[3][:], s2c_w[:, k, :, :].rearrange("p r m -> p (r m)"), spT[:, k, :],
                              start=(k == 0), stop=(k == 1))
                last.then_inc(cont_ps, 1)
                pe.wait_ge(cont_done, g + 1)
                pe.wait_ge(t_done, g)
                mm(bank[4][:], r_w1[:].rearrange("p r m -> p (r m)"), wideT[:, ds(g * N, N)], start=True, stop=True).then_inc(r1_ps, 1)
                pe.wait_ge(t_done, g + 1)
                for t in range(TPG):
                    last = mm(bank[5][:, ds(g * (TPG * E) + t * E, E)], tT[:, P * t:P * (t + 1)], r_w2[:],
                              start=True, stop=True)
                last.then_inc(lg_ps, 1)

            ln_transpose(LN_B)
            with pe.Fori(0, G - 1) as g:
                encode(g)
                ln_transpose(g + (LN_B + 1))
                route(g)
            encode(G - 1)
            route(G - 1)

            def hidden0(g, e):
                pe.wait_ge(h_act if e % 2 == 0 else h_dve, g * 4 + e // 2)
                mm(bank[4 + e % 2][:], we1[:, e, :], wideT[:, ds(g * N, N)], start=True, stop=True).then_inc(h_ps, 1)

            def expert0(g, e):
                if e == 0:
                    pe.wait_ge(gy_done, g * TPG)
                    for t in range(TPG):
                        mm(bank[t][:], ones3[:], bsplit[:, 0:NBE], start=True, stop=False, skip_group_check=True)
                if e % 2 == 0:
                    pe.wait_ge(h_act, g * 4 + e // 2 + 1)
                else:
                    pe.wait_ge(h_dve, g * 4 + e // 2 + 1)
                for t in range(TPG):
                    last = mm(bank[t][:, M0 * e:M0 * (e + 1)], hT[:, e % 4, P * t:P * (t + 1)], we2[:, e, :],
                              start=False, stop=(e == E - 1), skip_group_check=True)
                last.then_inc(y_ps, 1)

            def mix_sum(g):
                pe.wait_ge(sp2_done, g * 2)
                for t in range(TPG):
                    pe.wait_ge(gh_done, g * TPG + t + 1)
                    for k in range(2):
                        last = mm(bank[6][:, P * t:P * (t + 1)], gh[:, t % 2, P * k:P * (k + 1)], ident[:],
                                  start=(k == 0), stop=(k == 1))
                    last.then_inc(acc_ps, 1)

            def spikes(g):
                pe.wait_ge(oT_done, g + 1)
                pe.wait_ge(dc_done, g)
                for k in range(2):
                    mm(bank[7 - k][:], c2s_w[:, P * k:P * (k + 1)], oT[:], start=True, stop=True).then_inc(c2s_ps, 1)

            def decode(g):
                pe.wait_ge(sp2_done, g * 2 + 2)
                mm(bank[7][:], ones3[:], bsplit[:, NBE:NBE + D].unsqueeze(1).broadcast_to([3, TPG, D]),
                   start=True, stop=False, skip_group_check=True)
                for t in range(TPG):
                    for k in range(2):
                        last = mm(bank[7][:, D * t:D * (t + 1)], sp2T[:, k, P * t:P * (t + 1)], dec_w[:, k, :],
                                  start=False, stop=(k == 1), skip_group_check=True)
                last.then_inc(dec_ps, 1)

            def mixture0(g, before):
                for e in range(E):
                    hidden0(g, e)
                    if e >= 2:
                        expert0(g, e - 2)
                    if before and e == 1:
                        mix_sum(g - 1)
                    if before and e == 4:
                        spikes(g - 1)
                    if before and e == 6:
                        decode(g - 1)
                expert0(g, E - 2)
                expert0(g, E - 1)

            pe.wait_ge(c_split, 1)
            pe.wait_ge(t_done, G)
            pe.wait_ge(g_step, 1)
            mixture0(0, False)
            with pe.Fori(1, G) as g:
                mixture0(g, True)
            mix_sum(G - 1)
            spikes(G - 1)
            decode(G - 1)

            def q1(g):
                pe.wait_ge(xnT_done, LN_C + g + 1)
                pe.wait_ge(q1_done, g)
                mm(bank[6][:], w1T[:, 0, :], xnT[:], start=True, stop=True).then_inc(q1_ps, 1)

            pe.wait_ge(dc_done, G)
            ln_transpose(LN_C)
            with pe.Fori(0, G - 1) as g:
                q1(g)
                ln_transpose(g + (LN_C + 1))
            q1(G - 1)

            pe.wait_ge(hide_done, 1)
            pe.wait_ge(c_idh, 1)
            pe.wait_ge(c_ones, 3)
            pe.wait_ge(xnT_done, LN_D)

            def scores1(b, j):
                pe.wait_ge(s1_shifted, b * 2)
                hide = hide1[:, ds(b, 1), :]
                for bk, lo, n_s, nh in ((0, 0, SA, NH // 2), (1, 0, SA, NH // 2), (2, SA, SB, NH)):
                    mm(bank[bk][:, 0:nh * n_s], ident_h[:], hide[:, :, lo:lo + n_s].broadcast_to([P, nh, n_s]),
                       start=True, stop=False, skip_group_check=True)
                pe.wait_ge(qt_done, b + 1)
                pe.wait_ge(kb_done, b * 2 + 2)
                for bk, o, n in ((0, 0, 512), (1, 512, 512), (2, CA, CB)):
                    last = mm(bank[bk][:, 0:n], qt[:, j % 2, :], kblk[:, j % 4, o:o + n],
                              start=False, stop=True, skip_group_check=True)
                last.then_inc(s1_ps, 1)

            def weights_T(b, j):
                pe.wait_ge(e1_done, b + 1)
                pe.wait_ge(pTa_done, b)
                for c in range(NA):
                    last = tr(bank[3 + c // 4][:, P * (c % 4):P * (c % 4 + 1)], e1[:, j % 2, P * c:P * (c + 1)], ident[:])
                last.then_inc(pTa_ps, 1)
                pe.wait_ge(pTb_done, b)
                for c in range(2):
                    last = tr(bank[5][0:RB, P * c:P * (c + 1)], e1[:, j % 2, CA + RB * c:CA + RB * (c + 1)], ident[:])
                last.then_inc(pTb_ps, 1)

            def values1(b, j):
                pe.wait_ge(at1_done, b)
                pe.wait_ge(pTb_done, b + 1)
                for c in range(2):
                    mm(bank[6][:, E * DV * c:E * DV * (c + 1)], pTb[:, j % 2, P * c:P * (c + 1)],
                       v1b[:, ds(b * 2 + c, 1), :, :].rearrange("p o e v -> p (o e v)"),
                       start=(c == 0), stop=False, skip_group_check=True)
                pe.wait_ge(pTa_done, b + 1)
                for c in range(NA):
                    last = mm(bank[6][:, 2 * DV * c:2 * DV * (c + 1)], pTa[:, j % 2, P * c:P * (c + 1)],
                              v1a[:, ds(b * NA + c, 1), :, :].rearrange("p o e v -> p (o e v)"),
                              start=False, stop=True, skip_group_check=True)
                last.then_inc(o1_ps, 1)

            def heads_T(b, j):
                pe.wait_ge(at1_done, b + 1)
                pe.wait_ge(x3_done, b)
                tr(bank[7][:, 0:P], at1[:, j % 2, :, :].rearrange("p h d -> p (h d)"), ident[:]).then_inc(at1T_ps, 1)

            def project1(b):
                pe.wait_ge(at1T_done, b + 1)
                mm(bank[7][:, P:2 * P], ones3[:], bsplit[:, NBE + D:NBE + 2 * D], start=True, stop=False,
                   skip_group_check=True)
                mm(bank[7][:, P:2 * P], at1T[:], w1T[:, 3, :], start=False, stop=True,
                   skip_group_check=True).then_inc(y1_ps, 1)

            def attention1(b, j, first=0):
                if first < B:
                    scores1(b, j)
                if first >= 1 and first <= B:
                    weights_T(b - 1, j - 1)
                if first >= 2:
                    heads_T(b - 2, j - 2)
                if first >= 1 and first <= B:
                    values1(b - 1, j - 1)
                if first >= 2:
                    project1(b - 2)

            for b in range(4):
                attention1(b, b, b)
            with pe.Fori(1, G) as i:
                for j in range(4):
                    attention1(i * 4 + j, j, 4)
            for b in range(B, B + 2):
                attention1(b, b, b)

            def logits1(g):
                pe.wait_ge(xnT_done, LN_D + g + 1)
                for t in range(TPG):
                    last = mm(bank[5][:, ds(g * (TPG * E) + t * E, E)], xnT[:, P * t:P * (t + 1)], wr[:],
                              start=True, stop=True)
                last.then_inc(lg_ps, 1)

            pe.wait_ge(ld_f1, 16 * N_F1)
            pe.wait_ge(pTb_done, B)
            pe.wait_ge(x3_done, B)
            with pe.Fori(0, G) as g:
                ln_transpose(g + LN_D)
                logits1(g)
            pe.wait_ge(gsp_done, 3)
            for b in range(B):
                last = tr(bank[3 + b // 8][:].bitcast(BF16)[0:96, P * (b % 8):P * (b % 8 + 1)], gsp[:, b, :], ident_h[:])
                if b % 8 == 7:
                    last.then_inc(gT_ps, 1)
            pe.wait_ge(gT_done, 2)

            def hidden1(g, j):
                since(pe, sil_done, g * NB, j - 1)
                mm(bank[j % 2][:], f_w1[:, P * j:P * (j + 1)], wideT[:, ds(g * N, N)],
                   start=True, stop=True).then_inc(fh_ps, 1)
                since(pe, u1_done, g * NB, j - 1)
                mm(bank[2 + j % 2][:], f_w3[:, P * j:P * (j + 1)], wideT[:, ds(g * N, N)],
                   start=True, stop=True).then_inc(fg_ps, 1)
                since(pe, act_done, g * NB, j - 1)
                mm(bank[4 + j % 2][:], esel[:, P * j:P * (j + 1)], gT[:, ds(g * N, N)],
                   start=True, stop=True).then_inc(gb_ps, 1)

            def output1(g, j):
                pe.wait_ge(act_done, g * NB + j + 1)
                if j == 0:
                    pe.wait_ge(res_done, g)
                for t in range(TPG):
                    last = mm(bank[6][:, D * t:D * (t + 1)], act[:, j % 3, P * t:P * (t + 1)], f_w2[:, j, :],
                              start=(j == 0 and t == 0), stop=(j == NB - 1), skip_group_check=True)
                last.then_inc(fy_ps, 1)

            def mixture1(g, before):
                for j in range(NB):
                    hidden1(g, j)
                    if j >= 2:
                        output1(g, j - 2)
                    elif before:
                        output1(g - 1, NB - 2 + j)

            mixture1(0, False)
            with pe.Fori(1, G) as g:
                mixture1(g, True)
            output1(G - 1, NB - 2)
            output1(G - 1, NB - 1)

        @block.scalar
        def _(act_e):
            fn = nc.scalar.activation
            v = a
            for i, name in enumerate(("L0_xattn_bq", "L0_xattn_bk")):
                act_e.dma_start(vrows[i:i + 1, :], v[name].unsqueeze(0)).then_inc(ld_rows, 16)
            act_e.dma_start(vrows[2:4, :], v["L0_ffn_enc_b"].rearrange("(k p) -> k p", k=2)).then_inc(ld_rows, 16)
            for r in range(2):
                act_e.dma_start(vrows[4:5, M0 * r:M0 * (r + 1)], v["L0_ffn_rb1"].unsqueeze(0)).then_inc(ld_rows, 16)
                act_e.dma_start(vrows[5:6, M0 * r:M0 * (r + 1)], v["L0_ffn_s2c_b"].unsqueeze(0)).then_inc(ld_rows, 16)
            act_e.dma_start(vrows[6:6 + E, :], v["L0_ffn_be1"]).then_inc(ld_rows, 16)
            act_e.dma_start(vrows[14:16, :], v["L0_ffn_c2s_b"].rearrange("(k p) -> k p", k=2)).then_inc(ld_rows, 16)
            for i, name in enumerate(("L1_xattn_bq", "L1_xattn_bk", "L1_xattn_bv")):
                act_e.dma_start(vrows[16 + i:17 + i, :], v[name].unsqueeze(0)).then_inc(ld_rows, 16)
            act_e.dma_start(wk0[:], v["L0_xattn_Wk"]).then_inc(ld_w0, 16)
            act_e.dma_start(wv0[:], v["L0_xattn_Wv"]).then_inc(ld_w0, 16)
            act_e.dma_start(wq0[:], v["L0_xattn_Wq"]).then_inc(ld_w0, 16)
            act_e.dma_start(bv0[:], v["L0_xattn_bv"].unsqueeze(0).broadcast_to([SC, D])).then_inc(ld_w0, 16)
            for i, name in enumerate(("L1_xattn_Wq", "L1_xattn_Wk", "L1_xattn_Wv", "L1_xattn_W0")):
                act_e.dma_start(w1raw[:, i, :], v[name]).then_inc(ld_w1, 16)

            for i in range(1, B // 2, 2):
                act_e.wait_ge(ctxT_ps, i + 1)
                nc.scalar.copy(ctxT[:, 2 * i:2 * i + 2, :].rearrange("p b c -> p (b c)"),
                               bank[i % 4][:, 0:2 * CT]).then_inc(ctxT_act, 1)

            def ln_copy(n, read, count):
                act_e.wait_ge(xnT_ps, n + 1)
                act_e.wait_ge(read, count)
                nc.scalar.copy(xnT[:], bank[7][:]).then_inc(xnT_done, 1)

            def exp0(g):
                act_e.wait_ge(s0_shifted, g + 1)
                fn(e0[:], e0[:], ACT.Exp).then_inc(e0_done, 1)
                act_e.wait_ge(at0_ps, g + 1)
                act_e.wait_ge(o0_ps, g)
                nc.scalar.copy(at0T[:], bank[3][0:SC, :]).then_inc(at0_done, 1)

            ln_copy(0, q0_ps, 0)
            with act_e.Fori(0, G - 1) as g:
                exp0(g)
                ln_copy(g + 1, q0_ps, g + 1)
            exp0(G - 1)

            act_e.wait_ge(w1T_ps, 1)
            nc.scalar.copy(w1T[:].rearrange("p i d -> p (i d)"), bank[6][:]).then_inc(w1T_done, 1)
            act_e.wait_ge(vc_done, 1)
            for i, bk in enumerate((5, 0, 5)):
                n = min(6, B - 6 * i)
                act_e.wait_ge(k_ps, 4 + i)
                fn(k1T[:, 6 * i:6 * i + n, :].rearrange("p b s -> p (b s)"), bank[bk][:, 0:n * SC], ACT.Identity,
                   bias=col("bk1")).then_inc(k1_done, 1)
            act_e.wait_ge(c_zero, 1)
            for i in range(G):
                act_e.wait_ge(v1_ps, i + 1)
                src = bank[1 + i][SA:P, :].rearrange("p (c r d) -> p c r d", r=2, d=DH)
                nc.scalar.copy(v1a[SA:P, 4 * NA * i:4 * NA * (i + 1), 1, 0:DH], src[:, :, 1, :]).then_inc(v1_odd, 1)
            act_e.wait_ge(c_esel, 3)
            for r in (32, 64):
                nc.scalar.copy(esel[r:r + 32, :], esel[0:32, :]).then_inc(c_esel, 1)

            def sigmoid_enc(g):
                for k in range(2):
                    act_e.wait_ge(enc_ps, 2 * g + k + 1)
                    act_e.wait_ge(cont_ps, g)
                    fn(spT[:, k, :], bank[1 + k][:], ACT.Sigmoid, bias=col(f"enc{k}")).then_inc(sp_done, 1)

            def tanh_router(g):
                act_e.wait_ge(r1_ps, g + 1)
                act_e.wait_ge(lg_ps, g)
                act_e.wait_ge(c_misc, 1)
                fn(tT[0:M0, :], bank[4][0:M0, :], ACT.Tanh, bias=col("rb1", M0)).then_inc(t_done, 1)

            def gate_weights(k):
                act_e.wait_ge(gd_done, k + 1)
                fn(gw[:, 0, :], gd[:], ACT.Sigmoid, scale=-1.0).then_inc(gw_done, 1)
                fn(gw[:, 1, :], gd[:], ACT.Sigmoid).then_inc(gw_done, 1)

            ln_copy(LN_B, q0_ps, G)
            with act_e.Fori(0, G - 1) as g:
                sigmoid_enc(g)
                ln_copy(g + (LN_B + 1), enc_ps, 2 * g + 2)
                tanh_router(g)
            sigmoid_enc(G - 1)
            tanh_router(G - 1)

            def relu0(g, e):
                act_e.wait_ge(h_ps, g * E + e + 1)
                since(act_e, y_ps, g * E, e - 3)
                fn(hT[:, e % 4, :], bank[4][:], ACT.Relu, bias=col(f"be1_{e}")).then_inc(h_act, 1)

            def mix_copy(g):
                act_e.wait_ge(acc_ps, g * TPG + TPG)
                act_e.wait_ge(c2s_ps, g * 2)
                nc.scalar.copy(oT[:], bank[6][:]).then_inc(oT_done, 1)

            def sigmoid_c2s(g):
                act_e.wait_ge(dec_ps, g)
                for k in range(2):
                    act_e.wait_ge(c2s_ps, g * 2 + k + 1)
                    fn(sp2T[:, k, :], bank[7 - k][:], ACT.Sigmoid, bias=col(f"c2s{k}")).then_inc(sp2_done, 1)

            def sigmoid_dec(g):
                act_e.wait_ge(dec_ps, g + 1)
                act_e.wait_ge(dn_done, g * TPG)
                fn(dc[:].rearrange("p t d -> p (t d)"), bank[7][:], ACT.Sigmoid).then_inc(dc_done, 1)

            def mixture0(g, before):
                for e in range(0, E, 2):
                    relu0(g, e)
                    if before and e == 2:
                        mix_copy(g - 1)
                    if before and e == 4:
                        sigmoid_c2s(g - 1)
                if before:
                    sigmoid_dec(g - 1)

            relu0(0, 0)
            relu0(0, 2)
            gate_weights(0)
            relu0(0, 4)
            relu0(0, 6)
            with act_e.Fori(1, G) as g:
                mixture0(g, True)
            mix_copy(G - 1)
            sigmoid_c2s(G - 1)
            sigmoid_dec(G - 1)

            ln_copy(LN_C, enc_ps, 2 * G)
            with act_e.Fori(1, G) as g:
                ln_copy(g + LN_C, q1_ps, g)

            def weights_copy(b, j):
                act_e.wait_ge(pTa_ps, b + 1)
                since(act_e, o1_ps, b, -1)
                for k in range(2):
                    last = nc.scalar.copy(pTa[:, j % 2, 512 * k:512 * (k + 1)], bank[3 + k][:])
                last.then_inc(pTa_done, 1)

            def heads_copy(b):
                act_e.wait_ge(at1T_ps, b + 1)
                act_e.wait_ge(y1_ps, b)
                fn(at1T[:], bank[7][:, 0:P], ACT.Identity, bias=col("bv1")).then_inc(at1T_done, 1)

            def exp1(b, j):
                act_e.wait_ge(s1_shifted, b * 2 + 2)
                fn(e1[:, j % 2, :], e1[:, j % 2, :], ACT.Exp).then_inc(e1_done, 1)

            def attention1(b, j, first):
                if first >= 1 and first <= B:
                    weights_copy(b - 1, j - 1)
                if first >= 2:
                    heads_copy(b - 2)
                if first < B:
                    exp1(b, j)

            for b in range(4):
                attention1(b, b, b)
            with act_e.Fori(1, G) as i:
                for j in range(4):
                    attention1(i * 4 + j, j, 4)
            for b in range(B, B + 2):
                attention1(b, b, b)

            with act_e.Fori(0, G) as g:
                act_e.wait_ge(wide_done, g)
                ln_copy(g + LN_D, lg_ps, g + G)
            gate_weights(1)

            def silu(g, j):
                act_e.wait_ge(fh_ps, g * NB + j + 1)
                since(act_e, u1_done, g * NB, j - 1)
                fn(sil[:, j % 2, :], bank[j % 2][:], ACT.Silu).then_inc(sil_done, 1)

            for j in range(NB):
                silu(0, j)
            with act_e.Fori(1, G) as g:
                for j in range(NB):
                    silu(g, j)

        @block.vector
        def _(dve):
            v = nc.vector
            dve.wait_ge(vc_ps, 1)
            v.tensor_copy(vcols[:], bank[7][:, 0:NR]).then_inc(vc_done, 1)
            dve.wait_ge(c_id, 2)
            v.tensor_copy(ident_h[:], ident[:]).then_inc(c_idh, 1)
            for i in range(0, B // 2, 2):
                dve.wait_ge(ctxT_ps, i + 1)
                v.tensor_copy(ctxT[:, 2 * i:2 * i + 2, :].rearrange("p b c -> p (b c)"),
                              bank[i % 4][:, 0:2 * CT]).then_inc(ctxT_dve, 1)
            dve.wait_ge(vc_done, 1)
            for i in range(3):
                n = min(6, B - 6 * i)
                dve.wait_ge(k_ps, i + 1)
                v.tensor_scalar(k0T[:, 6 * SC * i:6 * SC * i + n * SC], bank[4 + i % 2][:, 0:n * SC], col("bk0"),
                                None, ALU.add).then_inc(k0_done, 1)
            dve.wait_ge(ld_w0, 16 * N_W0)
            for i in range(G):
                dve.wait_ge(v0_ps, i + 1)
                v.tensor_tensor(v0[:, N * i:N * (i + 1)].rearrange("p (t d) -> p t d", d=D),
                                bank[i][0:SC, :].rearrange("p (t d) -> p t d", d=D),
                                bv0[:].unsqueeze(1).broadcast_to([SC, TPG, D]), ALU.add).then_inc(v0_done, 1)

            def moments(n, st, mom, read, steps, done, applied, scaled):
                half_mean = lambda k: st[:, :, k]
                dve.wait_ge(read, n * TPG + TPG)
                dve.wait_ge(done, n)
                v.tensor_tensor(mom[:, 0, :], half_mean(1), half_mean(4), ALU.add).then_inc(steps, 1)
                v.tensor_tensor(mom[:, 1, :], half_mean(1), half_mean(4), ALU.subtract).then_inc(steps, 1)
                v.scalar_tensor_tensor(out=mom[:, 2, :], in0=half_mean(2), scalar=D * EPS, in1=half_mean(5),
                                       op0=ALU.add, op1=ALU.add).then_inc(steps, 1)
                dve.wait_ge(applied, n * TPG)
                dve.wait_ge(steps, n * 5 + 3)
                v.tensor_scalar(mom[:, 3, :], mom[:, 0, :], 0.5, None, ALU.mult).then_inc(steps, 1)
                v.scalar_tensor_tensor(out=mom[:, 4, :], in0=mom[:, 1, :], scalar=0.25, in1=mom[:, 1, :],
                                       op0=ALU.mult, op1=ALU.mult).then_inc(steps, 1)
                dve.wait_ge(scaled, n)
                dve.wait_ge(steps, n * 5 + 5)
                v.scalar_tensor_tensor(out=mom[:, 5, :], in0=mom[:, 2, :], scalar=1.0 / D, in1=mom[:, 4, :],
                                       op0=ALU.mult, op1=ALU.add).then_inc(done, 1)

            def ln_moments_of(n, g):
                dve.wait_ge(ln_moments, n)
                for t in range(TPG):
                    v.bn_stats(stats[:, t, :], x[:, ds(g * N + t * D, D)]).then_inc(ln_stats, 1)
                moments(n, stats, mom, ln_stats, ln_steps, ln_moments, ln_applied, ln_rstd)

            def ln_apply(n, g):
                dve.wait_ge(ln_rstd, n + 1)
                dve.wait_ge(ln_steps, n * 5 + 4)
                dve.wait_ge(xnT_ps, n)
                for t in range(TPG):
                    v.tensor_scalar(xn[:, t, :], x[:, ds(g * N + t * D, D)], mom[:, 3, t:t + 1], rstd[:, t:t + 1],
                                    ALU.subtract, ALU.mult).then_inc(ln_applied, 1)

            def q0(g):
                dve.wait_ge(q0_ps, g + 1)
                dve.wait_ge(s0_ps, g)
                v.tensor_scalar(q0T[:], bank[1][:], col("bq0"), float(D) ** -0.5, ALU.add, ALU.mult).then_inc(q0_done, 1)

            def shift0(g):
                dve.wait_ge(s0_ps, g + 1)
                dve.wait_ge(at0_ps, g)
                dve.wait_ge(sum0_done, g)
                v.scalar_tensor_tensor(out=e0[:].rearrange("p t s -> p (t s)"),
                                       in0=mask0[:, ds(g * (TPG * SC), TPG * SC)], scalar=-1e9,
                                       in1=bank[2][:, 0:TPG * SC], op0=ALU.mult, op1=ALU.add).then_inc(s0_masked, 1)
                dve.wait_ge(s0_masked, g + 1)
                dve.wait_ge(s0_shifted, g)
                v.tensor_reduce(m0[:], e0[:], AX.X, ALU.max).then_inc(m0_done, 1)
                dve.wait_ge(m0_done, g + 1)
                v.tensor_tensor(e0[:], e0[:], m0[:].unsqueeze(2).broadcast_to([P, TPG, SC]),
                                ALU.subtract).then_inc(s0_shifted, 1)

            def add0(g):
                dve.wait_ge(e0_done, g + 1)
                dve.wait_ge(r0_done, g)
                v.tensor_reduce(sum0[:], e0[:], AX.X, ALU.add).then_inc(sum0_done, 1)
                dve.wait_ge(sum0_done, g + 1)
                dve.wait_ge(x1_done, g * TPG)
                v.reciprocal(r0[:], sum0[:]).then_inc(r0_done, 1)
                dve.wait_ge(r0_done, g + 1)
                dve.wait_ge(o0_ps, g + 1)
                for t in range(TPG):
                    xt = x[:, ds(g * N + t * D, D)]
                    v.scalar_tensor_tensor(out=xt, in0=bank[4][:, D * t:D * (t + 1)], scalar=r0[:, t:t + 1],
                                           in1=xt, op0=ALU.mult, op1=ALU.add).then_inc(x1_done, 1)

            dve.wait_ge(ld_x, 16)
            ln_moments_of(0, 0)
            ln_apply(0, 0)
            q0(0)
            dve.wait_ge(ld_m0, 16)
            with dve.Fori(0, G - 1) as g:
                shift0(g)
                ln_moments_of(g + 1, g + 1)
                add0(g)
                ln_apply(g + 1, g + 1)
                q0(g + 1)
            shift0(G - 1)
            add0(G - 1)

            dve.wait_ge(ld_bias, 16 * N_BIAS)
            left = [brow[:], bres[:, 0, :], bres[:, 1, :]]
            for i in range(3):
                v.tensor_copy(bpart[:, i, :], left[i]).then_inc(c_step, 1)
                dve.wait_ge(c_step, 2 * i + 1)
                if i < 2:
                    v.tensor_tensor(left[i + 1], left[i], bpart[:, i, :], ALU.subtract).then_inc(c_step, 1)
                    dve.wait_ge(c_step, 2 * i + 2)
            v.tensor_scalar(bsel[:, 0, :], bpart[:, 0, :], ident[0:3, 0:1], None, ALU.mult).then_inc(c_step, 1)
            dve.wait_ge(c_step, 6)
            v.scalar_tensor_tensor(out=bsel[:, 1, :], in0=bpart[:, 1, :], scalar=ident[0:3, 1:2], in1=bsel[:, 0, :],
                                   op0=ALU.mult, op1=ALU.add).then_inc(c_step, 1)
            dve.wait_ge(c_step, 7)
            v.scalar_tensor_tensor(out=bsplit[:], in0=bpart[:, 2, :], scalar=ident[0:3, 2:3], in1=bsel[:, 1, :],
                                   op0=ALU.mult, op1=ALU.add).then_inc(c_split, 1)

            dve.wait_ge(x1_done, B)
            ln_moments_of(LN_B, 0)
            dve.wait_ge(c_ones, 3)
            for i in range(G):
                dve.wait_ge(v1_ps, i + 1)
                src = bank[1 + i][0:SA, :].rearrange("p (c r d) -> p c r d", r=2, d=DH)
                v.tensor_copy(v1a[0:SA, 4 * NA * i:4 * NA * (i + 1), 0, 0:DH], src[:, :, 0, :]).then_inc(v1_even, 1)
                v.tensor_tensor(v1b[:, 2 * TPG * i:2 * TPG * (i + 1), :, 0:DH],
                                bank[(0, 5, 6, 7)[i]][0:RB, :].rearrange("p (c e d) -> p c e d", e=E, d=DH),
                                slot_of[:].unsqueeze(1).unsqueeze(3).broadcast_to([RB, 2 * TPG, E, DH]),
                                ALU.mult).then_inc(v1_b, 1)
            ln_apply(LN_B, 0)

            def continuous(g):
                dve.wait_ge(cont_ps, g + 1)
                v.tensor_scalar(wideT[:, ds(g * N, N)], bank[3][:], col("s2c"), None, ALU.add).then_inc(cont_done, 1)

            with dve.Fori(0, G - 1) as g:
                ln_moments_of(g + (LN_B + 1), g + 1)
                ln_apply(g + (LN_B + 1), g + 1)
                continuous(g)
            continuous(G - 1)

            def gate_tokens(k, between):
                n = [k * 13]

                def step(op):
                    n[0] += 1
                    op.then_inc(g_step, 1)
                    dve.wait_ge(g_step, n[0])

                dve.wait_ge(lg_ps, G * (k + 1))
                step(v.tensor_copy(lg[:].rearrange("p b e -> p (b e)"), bank[5][:, 0:B * E]))
                for i, l in enumerate((lg, lg2)):
                    wide = lambda y: y[:, i, :].unsqueeze(2).broadcast_to([P, B, E])
                    step(v.tensor_reduce(gmx[:, i, :], l[:], AX.X, ALU.max))
                    step(v.tensor_tensor(geq[:, i], l[:], wide(gmx), ALU.is_equal))
                    step(v.tensor_tensor(gkey[:, i], geq[:, i], rank[:].unsqueeze(1).broadcast_to([P, B, E]), ALU.mult))
                    step(v.tensor_reduce(gkx[:, i, :], gkey[:, i], AX.X, ALU.max))
                    step(v.tensor_tensor(goh[:, i], gkey[:, i], wide(gkx), ALU.is_equal))
                    if i == 0:
                        step(v.scalar_tensor_tensor(out=lg2[:], in0=goh[:, 0], scalar=NEG_BIG, in1=lg[:],
                                                    op0=ALU.mult, op1=ALU.add))
                v.tensor_tensor(gd[:], gmx[:, 1, :], gmx[:, 0, :], ALU.subtract).then_inc(gd_done, 1)
                between()
                for i in range(2):
                    dve.wait_ge(gw_done, 2 * k + i + 1)
                    last = v.tensor_tensor(gwo[:, i], goh[:, i], gw[:, i, :].unsqueeze(2).broadcast_to([P, B, E]), ALU.mult)
                step(last)
                v.tensor_tensor(gates[:], gwo[:, 0], gwo[:, 1], ALU.add).then_inc(gates_done, 1)

            def relu0(g, e):
                dve.wait_ge(h_ps, g * E + e + 1)
                since(dve, y_ps, g * E, e - 3)
                v.tensor_scalar(hT[:, e % 4, :], bank[5][:], col(f"be1_{e}"), 0.0, ALU.add, ALU.max).then_inc(h_dve, 1)

            def gate_outputs(g):
                dve.wait_ge(y_ps, g * E + E)
                for t in range(TPG):
                    since(dve, gh_done, g * TPG, t - 1)
                    v.tensor_tensor(gy[:, t % 2, :].rearrange("p (e m) -> p e m", e=E),
                                    bank[t][:].rearrange("p (e m) -> p e m", e=E),
                                    gates[:, ds(g * TPG + t, 1), :].rearrange("p o e -> p (o e)").unsqueeze(2)
                                    .broadcast_to([P, E, M0]), ALU.mult).then_inc(gy_done, 1)

            def decoded_moments(g):
                dve.wait_ge(dc_done, g + 1)
                dve.wait_ge(lo_moments, g)
                for t in range(TPG):
                    v.bn_stats(stats2[:, t, :], dc[:, t, :]).then_inc(lo_stats, 1)
                moments(g, stats2, mom2, lo_stats, lo_steps, lo_moments, dn_done, lo_rstd)

            def decoded_norm(g):
                dve.wait_ge(lo_rstd, g + 1)
                dve.wait_ge(lo_steps, g * 5 + 4)
                dve.wait_ge(dg_done, g)
                for t in range(TPG):
                    v.tensor_scalar(dn[:, t, :], dc[:, t, :], mom2[:, 3, t:t + 1], rstd2[:, t:t + 1],
                                    ALU.subtract, ALU.mult).then_inc(dn_done, 1)
                dve.wait_ge(dn_done, g * TPG + TPG)
                dve.wait_ge(x2_done, g)
                v.tensor_tensor(dg[:], dn[:], ln_g[:].unsqueeze(1).broadcast_to([P, TPG, D]), ALU.mult).then_inc(dg_done, 1)
                dve.wait_ge(dg_done, g + 1)
                dve.wait_ge(xb_done, g + 1)
                v.tensor_tensor(x[:, ds(g * N, N)], dg[:].rearrange("p t d -> p (t d)"), xb[:], ALU.add).then_inc(x2_done, 1)

            def mixture0(g, before):
                for e in range(1, E, 2):
                    relu0(g, e)
                if before:
                    decoded_moments(g - 1)
                gate_outputs(g)
                if before:
                    decoded_norm(g - 1)

            gate_tokens(0, lambda: relu0(0, 1))
            for e in range(3, E, 2):
                relu0(0, e)
            dve.wait_ge(gates_done, 1)
            gate_outputs(0)
            with dve.Fori(1, G) as g:
                mixture0(g, True)
            decoded_moments(G - 1)
            decoded_norm(G - 1)

            def q1(g):
                dve.wait_ge(q1_ps, g + 1)
                v.tensor_scalar(wideT[:, ds(g * N, N)], bank[6][:], col("bq1"), float(DH) ** -0.5,
                                ALU.add, ALU.mult).then_inc(q1_done, 1)

            dve.wait_ge(x2_done, G)
            ln_moments_of(LN_C, 0)
            ln_apply(LN_C, 0)
            with dve.Fori(0, G - 1) as g:
                ln_moments_of(g + (LN_C + 1), g + 1)
                ln_apply(g + (LN_C + 1), g + 1)
                q1(g)
            q1(G - 1)

            def shift1(b, j):
                dve.wait_ge(s1_ps, b + 1)
                dve.wait_ge(mx_done, b)
                v.tensor_reduce(mxb[:], bank[2][:, 0:CB].rearrange("p (h s) -> p h s", h=NH), AX.X, ALU.max).then_inc(mxab_done, 1)
                for k in range(2):
                    last = v.tensor_reduce(mxa[:, 8 * k:8 * (k + 1)], bank[k][:].rearrange("p (h s) -> p h s", s=SA),
                                           AX.X, ALU.max)
                last.then_inc(mxab_done, 1)
                dve.wait_ge(mxab_done, b * 2 + 2)
                dve.wait_ge(s1_shifted, b * 2)
                v.tensor_tensor(mx[:], mxa[:], mxb[:], ALU.max).then_inc(mx_done, 1)
                dve.wait_ge(mx_done, b + 1)
                since(dve, pTb_ps, b, -1)
                for k in range(2):
                    last = v.tensor_tensor(e1[:, j % 2, 512 * k:512 * (k + 1)].rearrange("p (h s) -> p h s", s=SA),
                                           bank[k][:].rearrange("p (h s) -> p h s", s=SA),
                                           mx[:, 8 * k:8 * (k + 1)].unsqueeze(2).broadcast_to([P, 8, SA]), ALU.subtract)
                last.then_inc(s1_shifted, 1)
                v.tensor_tensor(e1[:, j % 2, CA:CA + CB].rearrange("p (h s) -> p h s", s=SB),
                                bank[2][:, 0:CB].rearrange("p (h s) -> p h s", s=SB),
                                mx[:].unsqueeze(2).broadcast_to([P, NH, SB]), ALU.subtract).then_inc(s1_shifted, 1)

            def weights_copy(b, j):
                dve.wait_ge(pTb_ps, b + 1)
                since(dve, o1_ps, b, -1)
                v.tensor_copy(pTb[:, j % 2, :], bank[5][0:RB, 0:2 * P]).then_inc(pTb_done, 1)

            def normalize1(b, j):
                dve.wait_ge(o1_ps, b + 1)
                dve.wait_ge(at1_done, b)
                o = bank[6][:, 0:NH * DV].rearrange("p (h v) -> p h v", v=DV)
                v.reciprocal(rs1[:], o[:, :, DH]).then_inc(rs1_done, 1)
                dve.wait_ge(rs1_done, b + 1)
                since(dve, at1T_ps, b, -1)
                v.tensor_tensor(at1[:, j % 2, :, :], o[:, :, 0:DH], rs1[:].unsqueeze(2).broadcast_to([P, NH, DH]),
                                ALU.mult).then_inc(at1_done, 1)

            def add1(b):
                dve.wait_ge(y1_ps, b + 1)
                v.tensor_tensor(x[:, ds(b * D, D)], bank[7][:, P:2 * P], x[:, ds(b * D, D)], ALU.add).then_inc(x3_done, 1)

            def attention1(b, j, first):
                if first >= 2 and first <= B + 1:
                    normalize1(b - 2, j - 2)
                if first >= 3:
                    add1(b - 3)
                if first < B:
                    shift1(b, j)
                if first >= 1 and first <= B:
                    weights_copy(b - 1, j - 1)

            for b in range(4):
                attention1(b, b, b)
            with dve.Fori(1, G) as i:
                for j in range(4):
                    attention1(i * 4 + j, j, 4)
            for b in range(B, B + 3):
                attention1(b, b, b)

            dve.wait_ge(x3_done, B)
            with dve.Fori(0, G) as g:
                ln_moments_of(g + LN_D, g)
                ln_apply(g + LN_D, g)
                dve.wait_ge(xnT_done, g + (LN_D + 1))
                v.tensor_copy(wideT[:, ds(g * N, N)], xnT[:]).then_inc(wide_done, 1)
            dve.wait_ge(c_misc, 5)
            gate_tokens(1, lambda: None)
            dve.wait_ge(gates_done, 2)
            v.tensor_copy(gsp[:, :, 0:E], gates[:]).then_inc(gsp_done, 1)
            dve.wait_ge(gsp_done, 1)
            v.tensor_tensor(gres[:, 0], gates[:], gsp[:, :, 0:E], ALU.subtract).then_inc(c_split, 1)
            dve.wait_ge(c_split, 2)
            v.tensor_copy(gsp[:, :, 32:32 + E], gres[:, 0]).then_inc(gsp_done, 1)
            dve.wait_ge(gsp_done, 2)
            v.tensor_tensor(gres[:, 1], gres[:, 0], gsp[:, :, 32:32 + E], ALU.subtract).then_inc(c_split, 1)
            dve.wait_ge(c_split, 3)
            v.tensor_copy(gsp[:, :, 64:64 + E], gres[:, 1]).then_inc(gsp_done, 1)
            for i in range(2):
                dve.wait_ge(gT_ps, i + 1)
                v.tensor_copy(gT[:, 8 * P * i:8 * P * (i + 1)], bank[3 + i][:].bitcast(BF16)[0:96, :]).then_inc(gT_done, 1)

            def gated(g, j):
                dve.wait_ge(sil_done, g * NB + j + 1)
                dve.wait_ge(fg_ps, g * NB + j + 1)
                since(dve, act_done, g * NB, j - 1)
                v.tensor_tensor(u1[:, j % 2, :], bank[2 + j % 2][:], sil[:, j % 2, :], ALU.mult).then_inc(u1_done, 1)
                dve.wait_ge(u1_done, g * NB + j + 1)
                dve.wait_ge(gb_ps, g * NB + j + 1)
                since(dve, fy_ps, g * NB, j - 2)
                v.tensor_tensor(act[:, j % 3, :], bank[4 + j % 2][:], u1[:, j % 2, :], ALU.mult).then_inc(act_done, 1)

            def result(g):
                dve.wait_ge(fy_ps, g * NB + NB)
                v.tensor_tensor(x[:, ds(g * N, N)], bank[6][:], x[:, ds(g * N, N)], ALU.add).then_inc(res_done, 1)

            for j in range(NB):
                gated(0, j)
            with dve.Fori(1, G) as g:
                for j in range(NB):
                    if j == 2:
                        result(g - 1)
                    gated(g, j)
            result(G - 1)


def since(eng, signal, base, k):
    if not (isinstance(base, int) and base + k <= 0):
        eng.wait_ge(signal, base + k)


_INS = ["x", "ctx_1024", "mask_BxSxS2_fk0", "mask_Bx1xSxS2_bf1",
        "L0_xattn_Wq", "L0_xattn_bq", "L0_xattn_Wk", "L0_xattn_bk", "L0_xattn_Wv", "L0_xattn_bv",
        "L0_ffn_enc_W", "L0_ffn_enc_b", "L0_ffn_s2c_W", "L0_ffn_s2c_b", "L0_ffn_rW1", "L0_ffn_rb1",
        "L0_ffn_rW2", "L0_ffn_rb2", "L0_ffn_We1", "L0_ffn_be1", "L0_ffn_We2", "L0_ffn_be2",
        "L0_ffn_c2s_W", "L0_ffn_c2s_b", "L0_ffn_dec_W", "L0_ffn_dec_b", "L0_ffn_ln_g", "L0_ffn_ln_b",
        "L1_xattn_Wq", "L1_xattn_bq", "L1_xattn_Wk", "L1_xattn_bk", "L1_xattn_Wv", "L1_xattn_bv",
        "L1_xattn_W0", "L1_xattn_b0", "L1_ffn_Wr", "L1_ffn_W1", "L1_ffn_W2", "L1_ffn_W3"]


def kernel(**inputs):
    import concourse.bacc as _bacc
    from concourse.bass_utils import run_bass_kernel_spmd as _run

    nc = _bacc.Bacc("TRN2", target_bir_lowering=False, num_devices=1)
    arrays, aps = {}, {}
    for name in _INS:
        v = np.ascontiguousarray(inputs[name])
        if v.dtype == np.bool_:
            v = v.view(np.uint8)
        arrays[f"in_{name}"] = v
        aps[name] = nc.dram_tensor(f"in_{name}", v.shape, mybir.dt.from_np(v.dtype), kind="ExternalInput").ap()
    out = nc.dram_tensor("out", (B, S, D), F32, kind="ExternalOutput").ap()
    xattn_ffn_program(nc, aps, out)
    return _run(nc, [arrays], core_ids=[0]).results[0]["out"]
```

```python
from contextlib import ExitStack

import concourse.bass as bass
import numpy as np
from concourse import mybir
from concourse.alu_op_type import AluOpType as ALU

F32 = mybir.dt.float32
BF16 = mybir.dt.bfloat16
ACT = mybir.ActivationFunctionType
AX = mybir.AxisListType
ds = bass.ds

P = 128
B, S, D = 16, 128, 128
SC = 77
TPG = 4
G = B // TPG
N = TPG * S
NH, DH = 16, 8
E = 8
H0, M0 = 256, 64
HX = H0 // 2
H1 = 192
NB = E * H1 // P
SA = 64
SB = SC - SA
NA = NH // 2
RB = E * SB
CA, CB = NH * SA, NH * SB
DV = DH + 1
CT = 2 * SA + RB
HIDDEN = -float(2 ** 100)
EPS = 1e-5
NEG_BIG = -1e38


def xattn_ffn_program(nc, a, out):
    ctx = ExitStack()
    with ctx:
        def sb(name, shape, dt=F32):
            return ctx.enter_context(nc.sbuf_tensor(name, shape, dt))

        def sem(name):
            return ctx.enter_context(nc.semaphore(name))

        x = sb("x", [P, B * D])
        room_a = sb("room_a", [P, B * D])
        room_b = sb("room_b", [P, B * D])
        room_c = sb("room_c", [P, 2, B * SC])
        room_d = sb("room_d", [P, B * D])
        ctx_in = room_a[0:SC, :].rearrange("p (b d) -> p b d", b=B)
        ctxT = sb("ctxT", [P, B, CT])
        k0T = room_c[:, 0, :]
        v0 = room_d[0:SC, :]
        k1T = sb("k1T", [P, B, SC])
        v1 = sb("v1", [P, B, 2, NH * DV])
        v1a = v1[:, :, 0, :].rearrange("p b (c r v) -> p b c r v", r=2, v=DV)
        v1b = v1[0:RB, :, 1, :].rearrange("p b (h v) -> p b h v", v=DV)
        vt = sb("vt", [P, 2, 2, NH * DV])
        kblk = sb("kblk", [P, 4, CA + CB])
        mask0 = room_c[:, 1, :]
        mask1 = sb("mask1", [P, B, SC], mybir.dt.uint8)
        hide1 = sb("hide1", [P, B, SC], BF16)

        wq0 = sb("wq0", [P, D])
        wk0 = sb("wk0", [P, D])
        wv0 = sb("wv0", [P, D])
        bv0 = sb("bv0", [SC, D])
        enc_w = sb("enc_w", [P, H0])
        s2c_w = sb("s2c_w", [P, 2, 2, M0])
        r_w1 = sb("r_w1", [P, 2, M0])
        r_w2 = sb("r_w2", [M0 + 1, E])
        we1 = sb("we1", [P, E, HX])
        we2 = sb("we2", [P, E, M0])
        c2s_w = sb("c2s_w", [P, H0])
        dec_w = sb("dec_w", [P, 2, D])
        ln_g = sb("ln_g", [P, D])
        ln_b = sb("ln_b", [P, D])
        w1raw = sb("w1raw", [P, 4, D])
        w1T = sb("w1T", [P, 4, D])
        wr = sb("wr", [P, E])
        f_w1 = sb("f_w1", [P, E * H1])
        f_w3 = sb("f_w3", [P, E * H1])
        f_w2 = sb("f_w2", [P, NB, D])

        ROWS = ["bq0", "bk0", "enc0", "enc1", "rb1", "s2c"] + [f"be1_{e}" for e in range(E)] + \
               ["c2s0", "c2s1", "bq1", "bk1", "bv1"]
        NR = len(ROWS)
        vrows = sb("vrows", [NR, P])
        vcols = sb("vcols", [P, NR])

        def col(name, rows=P):
            i = ROWS.index(name)
            return vcols[0:rows, i:i + 1]

        NBE, NBD = E * M0, 2 * D
        brow = sb("brow", [3, NBE + NBD])
        NBR = NBE + NBD
        early = kblk[0:3, :, :].rearrange("p r c -> p (r c)")
        bres = early[:, 0:2 * NBR].rearrange("p (i n) -> p i n", i=2)
        bsel = early[:, 2 * NBR:4 * NBR].rearrange("p (i n) -> p i n", i=2)
        bpart = early[:, 4 * NBR:4 * NBR + 3 * NBR // 2].bitcast(BF16).rearrange("p (i n) -> p i n", i=3)
        bsplit = sb("bsplit", [3, NBE + NBD], BF16)
        ones3 = sb("ones3", [3, P], BF16)

        ident = sb("ident", [P, P])
        ident_h = sb("ident_h", [P, P], BF16)
        head_of = sb("head_of", [P, NH])
        slot_of = sb("slot_of", [RB, 2, E])
        rank = sb("rank", [P, E])
        half = sb("half", [P, TPG])
        esel = sb("esel", [96, NB * P], BF16)

        stats = sb("stats", [P, B, 6])
        mom = sb("mom", [P, 6, B])
        rstd = sb("rstd", [P, B])
        bqs = sb("bqs", [P, 2])
        xn = sb("xn", [P, TPG, D])
        xnT = sb("xnT", [P, N])
        wideT = sb("wideT", [P, G * N])
        q0T = sb("q0T", [P, N])
        e0 = sb("e0", [P, TPG, SC])
        m0 = sb("m0", [P, TPG])
        sum0 = sb("sum0", [P, TPG])
        r0 = sb("r0", [P, TPG])
        at0T = sb("at0T", [SC, N])
        spT = sb("spT", [P, 2, N])
        tT = sb("tT", [M0 + 1, N])
        hT = sb("hT", [P, 4, N])
        gy = sb("gy", [P, 2, N])
        gh = sb("gh", [P, 2, N // 2])
        oT = q0T
        sp2T = spT
        dc = sb("dc", [P, TPG, D])
        dn = sb("dn", [P, TPG, D])
        dg = sb("dg", [P, TPG, D])
        xb = sb("xb", [P, TPG * D])
        stats2 = sb("stats2", [P, TPG, 6])
        mom2 = sb("mom2", [P, 6, TPG])
        rstd2 = sb("rstd2", [P, TPG])
        lg = sb("lg", [P, B, E])
        lg2 = sb("lg2", [P, B, E])
        geq = sb("geq", [P, 2, B, E])
        gkey = sb("gkey", [P, 2, B, E])
        goh = sb("goh", [P, 2, B, E])
        gmx = sb("gmx", [P, 2, B])
        gkx = sb("gkx", [P, 2, B])
        gd = sb("gd", [P, B])
        gw = sb("gw", [P, 2, B])
        gwo = sb("gwo", [P, 2, B, E])
        gates = sb("gates", [P, B, E])
        gres = sb("gres", [P, 2, B, E])
        gsp = hT[:].rearrange("p i n -> p (i n)")[:, 0:B * 48].bitcast(BF16).rearrange("p (b c) -> p b c", b=B)
        gT = gy[0:96].rearrange("p i n -> p (i n)").bitcast(BF16)
        qt = sb("qt", [P, 2, P])
        e1 = room_c
        mxa = sb("mxa", [P, NH])
        mxb = sb("mxb", [P, NH])
        mx = sb("mx", [P, NH])
        pTa = room_a[:].rearrange("p (i n) -> p i n", i=2)
        pTb = sb("pTb", [RB, 2, 2 * P])
        rs1 = sb("rs1", [P, NH])
        at1 = sb("at1", [P, 2, NH, DH])
        at1T = sb("at1T", [P, P])
        sil = room_b[:, 0:2 * N].rearrange("p (i n) -> p i n", i=2)
        u1 = room_b[:, 2 * N:4 * N].rearrange("p (i n) -> p i n", i=2)
        act = room_d[:, 0:3 * N].rearrange("p (i n) -> p i n", i=3)

        bank = [ctx.enter_context(nc.psum_tensor(f"bank{i}", [P, 512], F32)) for i in range(8)]

        ld_x = [sem(f"ld_x{g}") for g in range(G)]
        ld_ctx = sem("ld_ctx")
        ld_rows = sem("ld_rows")
        ld_w0 = sem("ld_w0")
        ld_m0 = sem("ld_m0")
        ld_m1 = sem("ld_m1")
        ld_w1 = sem("ld_w1")
        ld_bias = sem("ld_bias")
        ld_f0 = sem("ld_f0")
        ld_f1 = sem("ld_f1")
        stored = sem("stored")
        c_id = sem("c_id")
        c_idh = sem("c_idh")
        c_sel = sem("c_sel")
        c_esel = sem("c_esel")
        c_zero = sem("c_zero")
        c_ones = sem("c_ones")
        c_misc = sem("c_misc")
        c_step = sem("c_step")
        c_split = sem("c_split")
        vc_ps = sem("vc_ps")
        vc_done = sem("vc_done")
        w1T_ps = sem("w1T_ps")
        w1T_done = sem("w1T_done")
        ctxT_ps = sem("ctxT_ps")
        ctxT_lo = sem("ctxT_lo")
        ctxT_hi = sem("ctxT_hi")
        bqs_done = sem("bqs_done")
        k_ps = sem("k_ps")
        k0_done = sem("k0_done")
        k1_done = sem("k1_done")
        v0_ps = sem("v0_ps")
        v0_done = sem("v0_done")
        v1_ps = sem("v1_ps")
        v1_even = sem("v1_even")
        v1_odd = sem("v1_odd")
        v1_b = sem("v1_b")
        hide_done = sem("hide_done")
        kb_done = sem("kb_done")
        ln_stats = sem("ln_stats")
        ln_moments = sem("ln_moments")
        ln_steps = sem("ln_steps")
        ln_rstd = sem("ln_rstd")
        ln_applied = sem("ln_applied")
        xnT_ps = sem("xnT_ps")
        xnT_done = sem("xnT_done")
        q0_ps = sem("q0_ps")
        q0_done = sem("q0_done")
        s0_ps = sem("s0_ps")
        s0_masked = sem("s0_masked")
        m0_done = sem("m0_done")
        s0_shifted = sem("s0_shifted")
        e0_done = sem("e0_done")
        sum0_done = sem("sum0_done")
        r0_done = sem("r0_done")
        at0_ps = sem("at0_ps")
        at0_done = sem("at0_done")
        o0_ps = sem("o0_ps")
        x1_done = sem("x1_done")
        enc_ps = sem("enc_ps")
        sp_done = sem("sp_done")
        cont_ps = sem("cont_ps")
        cont_done = sem("cont_done")
        r1_ps = sem("r1_ps")
        t_done = sem("t_done")
        lg_ps = sem("lg_ps")
        g_step = sem("g_step")
        gd_done = sem("gd_done")
        gw_done = sem("gw_done")
        gates_done = sem("gates_done")
        h_ps = sem("h_ps")
        h_act = sem("h_act")
        h_dve = sem("h_dve")
        y_ps = sem("y_ps")
        gy_done = sem("gy_done")
        gh_done = sem("gh_done")
        acc_ps = sem("acc_ps")
        oT_done = sem("oT_done")
        c2s_ps = sem("c2s_ps")
        sp2_done = sem("sp2_done")
        dec_ps = sem("dec_ps")
        dc_done = sem("dc_done")
        lo_stats = sem("lo_stats")
        lo_moments = sem("lo_moments")
        lo_steps = sem("lo_steps")
        lo_rstd = sem("lo_rstd")
        dn_done = sem("dn_done")
        dg_done = sem("dg_done")
        xb_done = sem("xb_done")
        x2_done = sem("x2_done")
        q1_ps = sem("q1_ps")
        q1_done = sem("q1_done")
        qt_done = sem("qt_done")
        vt_done = sem("vt_done")
        s1_ps = sem("s1_ps")
        mxab_done = sem("mxab_done")
        mx_done = sem("mx_done")
        s1_shifted = sem("s1_shifted")
        e1_done = sem("e1_done")
        pTa_ps = sem("pTa_ps")
        pTb_ps = sem("pTb_ps")
        pTa_done = sem("pTa_done")
        pTb_done = sem("pTb_done")
        o1_ps = sem("o1_ps")
        rs1_done = sem("rs1_done")
        at1_done = sem("at1_done")
        at1T_ps = sem("at1T_ps")
        at1T_done = sem("at1T_done")
        y1_ps = sem("y1_ps")
        x3_done = sem("x3_done")
        wide_done = sem("wide_done")
        gsp_done = sem("gsp_done")
        gT_ps = sem("gT_ps")
        gT_done = sem("gT_done")
        fh_ps = sem("fh_ps")
        fg_ps = sem("fg_ps")
        gb_ps = sem("gb_ps")
        sil_done = sem("sil_done")
        u1_done = sem("u1_done")
        act_done = sem("act_done")
        fy_ps = sem("fy_ps")
        res_done = sem("res_done")

        N_ROWS = 12
        N_W0 = 4
        N_W1 = 4
        N_F0 = 14
        N_BIAS = 3
        N_F1 = 4
        LG1 = 256
        LN_A, LN_B, LN_C, LN_D = 0, G, 2 * G, 3 * G

        block = ctx.enter_context(nc.Block())

        @block.sync
        def _(sp):
            sp.dma_start(ctx_in[:], a["ctx_1024"].rearrange("b s d -> s b d")).then_inc(ld_ctx, 16)
            for g in range(G):
                sp.dma_start(x[:, N * g:N * (g + 1)].rearrange("p (b d) -> p b d", b=TPG),
                             a["x"].rearrange("b s d -> s b d")[:, TPG * g:TPG * (g + 1), :]).then_inc(ld_x[g], 16)
            sp.dma_start(mask0[:, :].rearrange("p (b s) -> p b s", b=B),
                         a["mask_BxSxS2_fk0"].rearrange("b t s -> t b s")).then_inc(ld_m0, 16)
            sp.dma_start(mask1[:], a["mask_Bx1xSxS2_bf1"].rearrange("b o t s -> t (b o) s")).then_inc(ld_m1, 16)
            sp.dma_start(brow[:, 0:NBE], a["L0_ffn_be2"].rearrange("e m -> (e m)").unsqueeze(0)
                         .broadcast_to([3, NBE])).then_inc(ld_bias, 16)
            for i, name in enumerate(("L0_ffn_dec_b", "L1_xattn_b0")):
                sp.dma_start(brow[:, NBE + D * i:NBE + D * (i + 1)],
                             a[name].unsqueeze(0).broadcast_to([3, D])).then_inc(ld_bias, 16)
            sp.dma_start(enc_w[:], a["L0_ffn_enc_W"]).then_inc(ld_f0, 16)
            for r in range(2):
                sp.dma_start(s2c_w[:, :, r, :],
                             a["L0_ffn_s2c_W"].rearrange("(k p) m -> p k m", p=P)).then_inc(ld_f0, 16)
            for r in range(2):
                sp.dma_start(r_w1[0:M0, r, :], a["L0_ffn_rW1"]).then_inc(ld_f0, 16)
            sp.dma_start(r_w2[0:M0, :], a["L0_ffn_rW2"]).then_inc(ld_f0, 16)
            sp.dma_start(r_w2[M0:M0 + 1, :], a["L0_ffn_rb2"].unsqueeze(0)).then_inc(ld_f0, 16)
            sp.dma_start(we1[0:M0], a["L0_ffn_We1"].rearrange("e m h -> m e h")).then_inc(ld_f0, 16)
            sp.dma_start(we2[:], a["L0_ffn_We2"].rearrange("e h m -> h e m")).then_inc(ld_f0, 16)
            for r in range(2):
                sp.dma_start(c2s_w[M0 * r:M0 * (r + 1), :], a["L0_ffn_c2s_W"]).then_inc(ld_f0, 16)
            sp.dma_start(dec_w[:], a["L0_ffn_dec_W"].rearrange("(k p) m -> p k m", p=P)).then_inc(ld_f0, 16)
            sp.dma_start(ln_g[:], a["L0_ffn_ln_g"].unsqueeze(0).broadcast_to([P, D])).then_inc(ld_f0, 16)
            sp.dma_start(ln_b[:], a["L0_ffn_ln_b"].unsqueeze(0).broadcast_to([P, D])).then_inc(ld_f0, 16)
            sp.dma_start(wr[:], a["L1_ffn_Wr"]).then_inc(ld_f1, 16)
            sp.dma_start(f_w1[:, :].rearrange("p (e h) -> p e h", e=E),
                         a["L1_ffn_W1"].rearrange("e c h -> c e h")).then_inc(ld_f1, 16)
            sp.dma_start(f_w3[:, :].rearrange("p (e h) -> p e h", e=E),
                         a["L1_ffn_W3"].rearrange("e c h -> c e h")).then_inc(ld_f1, 16)
            sp.dma_start(f_w2[:], a["L1_ffn_W2"].rearrange("e h c -> (e h) c")
                         .rearrange("(j p) c -> p j c", p=P)).then_inc(ld_f1, 16)
            out_v = out.rearrange("b s d -> s b d")
            for g in range(G):
                sp.wait_ge(res_done, g + 1)
                sp.dma_start(out_v[:, TPG * g:TPG * (g + 1), :],
                             x[:, N * g:N * (g + 1)].rearrange("p (b d) -> p b d", d=D)).then_inc(stored, 16)
            sp.wait_ge(stored, 16 * G)

        @block.gpsimd
        def _(pool):
            pool.memset(ident[:], 0.0).then_inc(c_id, 1)
            pool.wait_ge(c_id, 1)
            pool.affine_select(out=ident[:], in_=ident[:], compare_op=ALU.not_equal, fill=1.0, base=0,
                               pattern=[[-1, P]], channel_multiplier=1).then_inc(c_id, 1)
            pool.memset(half[:], -0.5).then_inc(c_sel, 1)

            def ln_scale(n, g):
                pool.wait_ge(ln_moments, n + 1)
                since(pool, ln_applied, n * TPG, (1 - G) * TPG)
                pool.tensor_tensor(rstd[:, ds(g * TPG, TPG)], mom[:, 5, ds(g * TPG, TPG)], half[:],
                                   ALU.pow).then_inc(ln_rstd, 1)

            pool.wait_ge(c_sel, 1)
            for g in range(G):
                ln_scale(LN_A + g, g)
            for e in range(E):
                pool.memset(rank[:, e:e + 1], float(E - e)).then_inc(c_sel, 1)
            pool.memset(head_of[:], 1.0).then_inc(c_sel, 1)
            pool.memset(slot_of[:], 1.0).then_inc(c_sel, 1)
            pool.wait_ge(c_sel, E + 3)
            pool.memset(tT[M0:M0 + 1, :], 1.0).then_inc(c_misc, 1)
            pool.wait_ge(c_misc, 1)
            pool.memset(ones3[:], 1.0).then_inc(c_misc, 1)
            pool.wait_ge(c_misc, 2)
            pool.memset(r_w1[M0:P], 0.0).then_inc(c_misc, 1)
            pool.memset(we1[M0:P], 0.0).then_inc(c_misc, 1)
            pool.wait_ge(c_misc, 4)
            for i, (m, w) in enumerate(((head_of, DH), (slot_of, SB))):
                steps = lambda k: [[k, NH]] if i == 0 else [[0, 2], [k, E]]
                pool.wait_ge(c_sel, E + 3 + 2 * i)
                pool.affine_select(out=m[:], in_=m[:], compare_op=ALU.is_ge, fill=0.0, base=0,
                                   pattern=steps(-w), channel_multiplier=1).then_inc(c_sel, 1)
                pool.wait_ge(c_sel, E + 4 + 2 * i)
                pool.affine_select(out=m[:], in_=m[:], compare_op=ALU.is_ge, fill=0.0, base=w - 1,
                                   pattern=steps(w), channel_multiplier=-1).then_inc(c_sel, 1)
            pool.memset(v1[:].rearrange("p b k n -> p (b k n)"), 0.0).then_inc(c_zero, 1)
            pool.wait_ge(c_zero, 1)
            pool.wait_ge(c_sel, E + 7)
            pool.memset(v1a[0:SA, :, :, 0, DH], 1.0).then_inc(c_ones, 1)
            pool.wait_ge(c_ones, 1)
            pool.memset(v1a[SA:P, :, :, 1, DH], 1.0).then_inc(c_ones, 1)
            pool.wait_ge(c_ones, 2)
            pool.tensor_copy(v1b[:, :, :, DH], slot_of[:].rearrange("p c e -> p (c e)").unsqueeze(1)
                             .broadcast_to([RB, B, NH])).then_inc(c_ones, 1)

            pool.wait_ge(ld_m1, 16)
            pool.tensor_scalar(hide1[:], mask1[:], -HIDDEN, HIDDEN, ALU.mult, ALU.add).then_inc(hide_done, 1)

            for g in range(G):
                ln_scale(LN_B + g, g)

            pool.memset(esel[0:32, :], 1.0).then_inc(c_esel, 1)
            pool.wait_ge(c_esel, 1)
            pool.affine_select(out=esel[0:32, :], in_=esel[0:32, :], compare_op=ALU.is_ge, fill=0.0, base=0,
                               pattern=[[1, NB * P]], channel_multiplier=-H1).then_inc(c_esel, 1)
            pool.wait_ge(c_esel, 2)
            pool.affine_select(out=esel[0:32, :], in_=esel[0:32, :], compare_op=ALU.is_ge, fill=0.0, base=H1 - 1,
                               pattern=[[-1, NB * P]], channel_multiplier=H1).then_inc(c_esel, 1)

            def key_block(b, slot):
                for lo, n_s, off in ((0, SA, 0), (SA, SB, CA)):
                    pool.tensor_tensor(
                        kblk[:, slot, off:off + NH * n_s].rearrange("p (h s) -> p h s", h=NH),
                        k1T[:, ds(b, 1), lo:lo + n_s].broadcast_to([P, NH, n_s]),
                        head_of[:].unsqueeze(2).broadcast_to([P, NH, n_s]), ALU.mult).then_inc(kb_done, 1)

            def mix0_sums(g):
                for t in range(TPG):
                    pool.wait_ge(gy_done, TPG * g + t + 1)
                    since(pool, acc_ps, g * TPG, t - 1)
                    pool.tensor_tensor(gh[:, t % 2, :], gy[:, t % 2, 0:N // 2], gy[:, t % 2, N // 2:N],
                                       ALU.add).then_inc(gh_done, 1)

            def mix0_out(g):
                pool.wait_ge(x2_done, g)
                pool.tensor_tensor(xb[:].rearrange("p (t d) -> p t d", t=TPG),
                                   x[:, ds(g * N, N)].rearrange("p (t d) -> p t d", t=TPG),
                                   ln_b[:].unsqueeze(1).broadcast_to([P, TPG, D]), ALU.add).then_inc(xb_done, 1)
                pool.wait_ge(lo_moments, g + 1)
                pool.tensor_tensor(rstd2[:], mom2[:, 5, :], half[:], ALU.pow).then_inc(lo_rstd, 1)

            pool.wait_ge(ld_f0, 16 * N_F0)
            pool.wait_ge(k1_done, 3)
            pool.wait_ge(c_split, 1)
            for b in range(2):
                key_block(b, b)
            def mixture0(g):
                mix0_out(g - 1)
                mix0_sums(g)
                ln_scale(g + (LN_C - 1), g - 1)

            mix0_sums(0)
            mixture0(1)
            with pool.Fori(2, G) as g:
                mixture0(g)
            mix0_out(G - 1)

            def queries(b, j):
                since(pool, s1_ps, b * 3, -3)
                pool.tensor_copy(qt[:, j % 2, :], wideT[:, ds(b * P, P)]).then_inc(qt_done, 1)

            def values(b, j):
                since(pool, o1_ps, b, -1)
                pool.tensor_copy(vt[:, j % 2, :, :].rearrange("p k n -> p (k n)"),
                                 v1[:, ds(b, 1), :, :].rearrange("p o k n -> p (o k n)")).then_inc(vt_done, 1)

            def attention1(b, j, first):
                if first + 1 < B:
                    queries(b + 1, j + 1)
                if first + 2 < B:
                    key_block(b + 2, (j + 2) % 4)
                if first >= 1:
                    values(b - 1, j - 1)

            pool.wait_ge(y_ps, G * E)
            pool.memset(gsp[:], 0.0).then_inc(c_misc, 1)
            pool.wait_ge(q1_done, 1)
            queries(0, 0)
            attention1(0, 0, 0)
            ln_scale(LN_C + G - 1, G - 1)
            for b in range(1, 4):
                if b == 3:
                    pool.wait_ge(q1_done, G)
                attention1(b, b, b)
            with pool.Fori(1, G - 1) as i:
                for j in range(4):
                    attention1(i * 4 + j, j, 4)
                    if j == 2:
                        ln_scale(i + (LN_D - 1), i - 1)
            for b in range(B - 4, B + 1):
                attention1(b, b, b)
                if b == B - 2:
                    ln_scale(LN_D + G - 2, G - 2)
            ln_scale(LN_D + G - 1, G - 1)

        @block.tensor
        def _(pe):
            mm, tr = nc.tensor.matmul, nc.tensor.transpose
            pe.wait_ge(c_id, 2)
            pe.wait_ge(ld_rows, 16 * N_ROWS)
            tr(bank[7][:, 0:NR], vrows[:], ident[0:NR, 0:NR]).then_inc(vc_ps, 1)
            pe.wait_ge(ld_ctx, 16)
            for i in range(3):
                for r in range(min(6, B - 6 * i)):
                    last = tr(bank[i][:, SC * r:SC * (r + 1)], ctx_in[:, 6 * i + r, :], ident[0:SC, 0:SC])
                last.then_inc(ctxT_ps, 1)

            def keys(w, i, bk):
                n = min(6, B - 6 * i)
                mm(bank[bk][:, 0:n * SC], w, ctxT[:, 6 * i:6 * i + n, SA:SA + SC],
                   start=True, stop=True).then_inc(k_ps, 1)

            pe.wait_ge(ld_w0, 16 * N_W0)
            for i in range(3):
                pe.wait_ge(ctxT_lo, i + 1)
                pe.wait_ge(ctxT_hi, i + 1)
                keys(wk0[:], i, 4 + i)
            for i in range(G):
                for t in range(TPG):
                    last = mm(bank[i][0:SC, D * t:D * (t + 1)], ctxT[:, TPG * i + t, SA:SA + SC], wv0[:],
                              start=True, stop=True)
                last.then_inc(v0_ps, 1)

            def ln_transpose(n, bk=7):
                pe.wait_ge(ln_applied, n * TPG + TPG)
                since(pe, xnT_done, n, 0)
                for t in range(TPG):
                    last = tr(bank[bk][:, P * t:P * (t + 1)], xn[:, t, :], ident[:])
                last.then_inc(xnT_ps, 1)

            def q0(g):
                pe.wait_ge(xnT_done, g + 1)
                since(pe, q0_done, g, 0)
                mm(bank[1][:], wq0[:], xnT[:], start=True, stop=True).then_inc(q0_ps, 1)

            def scores0(g):
                pe.wait_ge(q0_done, g + 1)
                since(pe, s0_masked, g, 0)
                for t in range(TPG):
                    last = mm(bank[2][:, SC * t:SC * (t + 1)], q0T[:, P * t:P * (t + 1)],
                              k0T[:, SC * (TPG * g + t):SC * (TPG * g + t + 1)], start=True, stop=True)
                last.then_inc(s0_ps, 1)

            def weights0(g):
                pe.wait_ge(e0_done, g + 1)
                since(pe, at0_done, g, 0)
                for t in range(TPG):
                    last = tr(bank[3][0:SC, P * t:P * (t + 1)], e0[:, t, :], ident[:])
                last.then_inc(at0_ps, 1)

            def values0(g):
                pe.wait_ge(at0_done, g + 1)
                since(pe, x1_done, TPG * g, 0)
                for t in range(TPG):
                    last = mm(bank[4][:, P * t:P * (t + 1)], at0T[:, P * t:P * (t + 1)],
                              v0[:, N * g + P * t:N * g + P * (t + 1)], start=True, stop=True)
                last.then_inc(o0_ps, 1)

            for k in range(G + 2):
                if k == 1:
                    pe.wait_ge(k0_done, 3)
                    pe.wait_ge(v0_done, G)
                if 1 <= k <= G:
                    scores0(k - 1)
                if k == 0:
                    pe.wait_ge(vc_done, 1)
                if k < G:
                    ln_transpose(LN_A + k)
                if k >= 2:
                    values0(k - 2)
                if k == 0:
                    pe.wait_ge(v0_done, 2)
                if k < G:
                    q0(k)
                if 1 <= k <= G:
                    weights0(k - 1)

            pe.wait_ge(ld_w1, 16 * N_W1)
            for i in range(4):
                last = tr(bank[6][:, P * i:P * (i + 1)], w1raw[:, i, :], ident[:])
            last.then_inc(w1T_ps, 1)
            pe.wait_ge(w1T_done, 1)
            for i, bk in enumerate((5, 0, 6)):
                keys(w1T[:, 1, :], i, bk)
            pe.wait_ge(q0_done, G)
            pe.wait_ge(s0_masked, G)
            pe.wait_ge(at0_done, G)
            for i in range(G):
                if i == 3:
                    pe.wait_ge(x1_done, B)
                if i < 3:
                    pe.wait_ge(k1_done, (2, 1, 3)[i])
                else:
                    pe.wait_ge(xnT_done, G)
                for t in range(TPG):
                    b, o = TPG * i + t, D * t
                    mm(bank[1 + i][:, o:o + D], ctxT[:, b, 0:2 * SA], w1T[:, 2, :], start=True, stop=True)
                    last = mm(bank[(0, 5, 6, 7)[i]][0:RB, o:o + D], ctxT[:, b, 2 * SA:CT], w1T[:, 2, :],
                              start=True, stop=True)
                last.then_inc(v1_ps, 1)
            pe.wait_ge(v1_b, G)
            pe.wait_ge(v1_odd, G)

            pe.wait_ge(ld_f0, 16 * N_F0)
            pe.wait_ge(c_misc, 4)

            def encode(g):
                pe.wait_ge(xnT_done, g + (LN_B + 1))
                since(pe, sp_done, g * 2, 0)
                for k in range(2):
                    mm(bank[1 + k][:], enc_w[:, P * k:P * (k + 1)], xnT[:], start=True, stop=True).then_inc(enc_ps, 1)

            def to_continuous(g):
                pe.wait_ge(sp_done, g * 2 + 2)
                since(pe, cont_done, g, 0)
                for k in range(2):
                    last = mm(bank[3][:], s2c_w[:, k, :, :].rearrange("p r m -> p (r m)"), spT[:, k, :],
                              start=(k == 0), stop=(k == 1))
                last.then_inc(cont_ps, 1)

            def router_hidden(g):
                pe.wait_ge(cont_done, g + 1)
                since(pe, t_done, g, 0)
                mm(bank[4][:], r_w1[:].rearrange("p r m -> p (r m)"), wideT[:, ds(g * N, N)],
                   start=True, stop=True).then_inc(r1_ps, 1)

            def logits0(g):
                pe.wait_ge(t_done, g + 1)
                for t in range(TPG):
                    last = mm(bank[5][:, ds(g * (TPG * E) + t * E, E)], tT[:, P * t:P * (t + 1)], r_w2[:],
                              start=True, stop=True)
                last.then_inc(lg_ps, 1)

            def router0(k, first):
                if first >= 1:
                    to_continuous(k - 1)
                if first < G:
                    ln_transpose(k + LN_B)
                if first >= 1:
                    router_hidden(k - 1)
                if first < G:
                    encode(k)
                if first >= 1:
                    logits0(k - 1)

            router0(0, 0)
            router0(1, 1)
            with pe.Fori(2, G) as k:
                router0(k, 2)
            router0(G, G)

            def hidden0(g, e):
                since(pe, h_act if e % 2 == 0 else h_dve, g * 4, e // 2)
                mm(bank[4 + e % 2][:], we1[:, e, :], wideT[:, ds(g * N, N)], start=True, stop=True).then_inc(h_ps, 1)

            def expert0(g, e):
                if e == 0:
                    since(pe, gy_done, g * TPG, 0)
                    for t in range(TPG):
                        mm(bank[t][:], ones3[:], bsplit[:, 0:NBE], start=True, stop=False, skip_group_check=True)
                if e % 2 == 0:
                    pe.wait_ge(h_act, g * 4 + e // 2 + 1)
                else:
                    pe.wait_ge(h_dve, g * 4 + e // 2 + 1)
                for t in range(TPG):
                    last = mm(bank[t][:, M0 * e:M0 * (e + 1)], hT[:, e % 4, P * t:P * (t + 1)], we2[:, e, :],
                              start=False, stop=(e == E - 1), skip_group_check=True)
                last.then_inc(y_ps, 1)

            def mix_sum(g):
                since(pe, sp2_done, g * 2, 0)
                for t in range(TPG):
                    pe.wait_ge(gh_done, g * TPG + t + 1)
                    for k in range(2):
                        last = mm(bank[6][:, P * t:P * (t + 1)], gh[:, t % 2, P * k:P * (k + 1)], ident[:],
                                  start=(k == 0), stop=(k == 1))
                    last.then_inc(acc_ps, 1)

            def spikes(g):
                pe.wait_ge(oT_done, g + 1)
                since(pe, dc_done, g, 0)
                for k in range(2):
                    mm(bank[7 - k][:], c2s_w[:, P * k:P * (k + 1)], oT[:], start=True, stop=True).then_inc(c2s_ps, 1)

            def decode(g):
                pe.wait_ge(sp2_done, g * 2 + 2)
                mm(bank[7][:], ones3[:], bsplit[:, NBE:NBE + D].unsqueeze(1).broadcast_to([3, TPG, D]),
                   start=True, stop=False, skip_group_check=True)
                for t in range(TPG):
                    for k in range(2):
                        last = mm(bank[7][:, D * t:D * (t + 1)], sp2T[:, k, P * t:P * (t + 1)], dec_w[:, k, :],
                                  start=False, stop=(k == 1), skip_group_check=True)
                last.then_inc(dec_ps, 1)

            def mixture0(g, before):
                for e in range(E):
                    hidden0(g, e)
                    if e >= 2:
                        expert0(g, e - 2)
                    if before and e == 1:
                        mix_sum(g - 1)
                    if before and e == 4:
                        spikes(g - 1)
                    if before and e == 6:
                        decode(g - 1)
                expert0(g, E - 2)
                expert0(g, E - 1)

            pe.wait_ge(c_split, 1)
            pe.wait_ge(t_done, G)
            pe.wait_ge(g_step, 1)
            mixture0(0, False)
            mixture0(1, True)
            with pe.Fori(2, G) as g:
                mixture0(g, True)

            def q1(g, bank_t, bank_q):
                ln_transpose(LN_C + g, bank_t)
                pe.wait_ge(xnT_done, LN_C + g + 1)
                since(pe, q1_done, g, 0)
                mm(bank[bank_q][:], w1T[:, 0, :], xnT[:], start=True, stop=True).then_inc(q1_ps, 1)

            mix_sum(G - 1)
            pe.wait_ge(h_act, G * E // 2)
            pe.wait_ge(h_dve, G * E // 2)
            q1(0, 4, 5)
            spikes(G - 1)
            q1(1, 4, 5)
            decode(G - 1)
            q1(2, 4, 5)

            pe.wait_ge(hide_done, 1)
            pe.wait_ge(c_idh, 1)
            pe.wait_ge(c_ones, 3)
            pe.wait_ge(gy_done, G * TPG)
            pe.wait_ge(xnT_done, LN_C + G - 1)
            pe.wait_ge(q1_done, G - 1)

            def scores1(b, j, between):
                hide = hide1[:, ds(b, 1), :]
                for bk, lo, n_s, nh, o in ((0, 0, SA, NH // 2, 0), (1, 0, SA, NH // 2, CA // 2), (2, SA, SB, NH, CA)):
                    since(pe, s1_shifted, b * 3, bk - 2)
                    mm(bank[bk][:, 0:nh * n_s], ident_h[:], hide[:, :, lo:lo + n_s].broadcast_to([P, nh, n_s]),
                       start=True, stop=False, skip_group_check=True)
                    if bk == 0:
                        pe.wait_ge(qt_done, b + 1)
                        pe.wait_ge(kb_done, b * 2 + 2)
                    mm(bank[bk][:, 0:nh * n_s], qt[:, j % 2, :], kblk[:, j % 4, o:o + nh * n_s],
                       start=False, stop=True, skip_group_check=True).then_inc(s1_ps, 1)
                    if bk == 0:
                        between()

            def weights_T(b, j):
                pe.wait_ge(e1_done, b + 1)
                pe.wait_ge(pTa_done, b)
                for c in range(NA):
                    last = tr(bank[3 + c // 4][:, P * (c % 4):P * (c % 4 + 1)], e1[:, j % 2, P * c:P * (c + 1)], ident[:])
                last.then_inc(pTa_ps, 1)
                pe.wait_ge(pTb_done, b)
                for c in range(2):
                    last = tr(bank[5][0:RB, P * c:P * (c + 1)], e1[:, j % 2, CA + RB * c:CA + RB * (c + 1)], ident[:])
                last.then_inc(pTb_ps, 1)

            def values1(b, j):
                pe.wait_ge(at1_done, b)
                pe.wait_ge(vt_done, b + 1)
                pe.wait_ge(pTb_done, b + 1)
                for c in range(2):
                    mm(bank[6][:, E * DV * c:E * DV * (c + 1)], pTb[:, j % 2, P * c:P * (c + 1)],
                       vt[0:RB, j % 2, 1, E * DV * c:E * DV * (c + 1)], start=(c == 0), stop=False, skip_group_check=True)
                pe.wait_ge(pTa_done, b + 1)
                for c in range(NA):
                    last = mm(bank[6][:, 2 * DV * c:2 * DV * (c + 1)], pTa[:, j % 2, P * c:P * (c + 1)],
                              vt[:, j % 2, 0, 2 * DV * c:2 * DV * (c + 1)], start=False, stop=True, skip_group_check=True)
                last.then_inc(o1_ps, 1)

            def heads_T(b, j):
                pe.wait_ge(at1_done, b + 1)
                pe.wait_ge(x3_done, b)
                tr(bank[7][:, 0:P], at1[:, j % 2, :, :].rearrange("p h d -> p (h d)"), ident[:]).then_inc(at1T_ps, 1)

            def project1(b):
                pe.wait_ge(at1T_done, b + 1)
                mm(bank[7][:, P:2 * P], ones3[:], bsplit[:, NBE + D:NBE + 2 * D], start=True, stop=False,
                   skip_group_check=True)
                mm(bank[7][:, P:2 * P], at1T[:], w1T[:, 3, :], start=False, stop=True,
                   skip_group_check=True).then_inc(y1_ps, 1)

            def logits1(g):
                pe.wait_ge(xnT_done, g + (LN_D + 1))
                for t in range(TPG):
                    last = mm(bank[6][:, ds(g * (TPG * E) + (LG1 + t * E), E)], xnT[:, P * t:P * (t + 1)], wr[:],
                              start=True, stop=True)
                last.then_inc(lg_ps, 1)

            def router1(g, added, normalized):
                pe.wait_ge(x3_done, added)
                ln_transpose(g + LN_D)
                pe.wait_ge(at1_done, normalized)
                logits1(g)

            def attention1(b, j, first):
                turn = lambda: heads_T(b - 3, j - 3) if first >= 3 else None
                if first < B:
                    scores1(b, j, turn)
                else:
                    turn()
                if first >= 3:
                    project1(b - 3)
                if 2 <= first < B + 2:
                    values1(b - 2, j - 2)
                if 1 <= first < B + 1:
                    weights_T(b - 1, j - 1)

            for b in range(4):
                if b == 2:
                    pe.wait_ge(dc_done, G)
                    pe.wait_ge(sp2_done, 2 * G)
                    q1(G - 1, 7, 6)
                    pe.wait_ge(q1_done, G)
                if b == 3:
                    pe.wait_ge(ld_f1, 16 * N_F1)
                attention1(b, b, b)
            with pe.Fori(1, G) as i:
                for j in range(4):
                    attention1(i * 4 + j, j, 4)
                router1(i - 1, i * 4 + 1, i * 4 + 2)
            for b in range(B, B + 3):
                attention1(b, b, b)
            router1(G - 1, B, B)

            pe.wait_ge(gsp_done, 3)
            for b in range(B):
                last = tr(bank[3 + b // 8][:].bitcast(BF16)[0:96, P * (b % 8):P * (b % 8 + 1)], gsp[:, b, :], ident_h[:])
                if b % 8 == 7:
                    last.then_inc(gT_ps, 1)
            pe.wait_ge(gT_done, 2)

            def hidden1(g, j):
                since(pe, sil_done, g * NB, j - 1)
                mm(bank[j % 2][:], f_w1[:, P * j:P * (j + 1)], wideT[:, ds(g * N, N)],
                   start=True, stop=True).then_inc(fh_ps, 1)
                since(pe, u1_done, g * NB, j - 1)
                mm(bank[2 + j % 2][:], f_w3[:, P * j:P * (j + 1)], wideT[:, ds(g * N, N)],
                   start=True, stop=True).then_inc(fg_ps, 1)
                since(pe, act_done, g * NB, j - 1)
                mm(bank[4 + j % 2][:], esel[:, P * j:P * (j + 1)], gT[:, ds(g * N, N)],
                   start=True, stop=True).then_inc(gb_ps, 1)

            def output1(g, j):
                pe.wait_ge(act_done, g * NB + j + 1)
                if j == 0:
                    pe.wait_ge(res_done, g)
                for t in range(TPG):
                    last = mm(bank[6][:, D * t:D * (t + 1)], act[:, j % 3, P * t:P * (t + 1)], f_w2[:, j, :],
                              start=(j == 0 and t == 0), stop=(j == NB - 1), skip_group_check=True)
                last.then_inc(fy_ps, 1)

            def mixture1(g, before):
                for j in range(NB):
                    hidden1(g, j)
                    if j >= 2:
                        output1(g, j - 2)
                    elif before:
                        output1(g - 1, NB - 2 + j)

            mixture1(0, False)
            with pe.Fori(1, G) as g:
                mixture1(g, True)
            output1(G - 1, NB - 2)
            output1(G - 1, NB - 1)

        @block.scalar
        def _(act_e):
            fn = nc.scalar.activation
            v = a
            for i, name in enumerate(("L0_xattn_bq", "L0_xattn_bk")):
                act_e.dma_start(vrows[i:i + 1, :], v[name].unsqueeze(0)).then_inc(ld_rows, 16)
            act_e.dma_start(vrows[2:4, :], v["L0_ffn_enc_b"].rearrange("(k p) -> k p", k=2)).then_inc(ld_rows, 16)
            for r in range(2):
                act_e.dma_start(vrows[4:5, M0 * r:M0 * (r + 1)], v["L0_ffn_rb1"].unsqueeze(0)).then_inc(ld_rows, 16)
                act_e.dma_start(vrows[5:6, M0 * r:M0 * (r + 1)], v["L0_ffn_s2c_b"].unsqueeze(0)).then_inc(ld_rows, 16)
            act_e.dma_start(vrows[6:6 + E, :], v["L0_ffn_be1"]).then_inc(ld_rows, 16)
            act_e.dma_start(vrows[14:16, :], v["L0_ffn_c2s_b"].rearrange("(k p) -> k p", k=2)).then_inc(ld_rows, 16)
            for i, name in enumerate(("L1_xattn_bq", "L1_xattn_bk", "L1_xattn_bv")):
                act_e.dma_start(vrows[16 + i:17 + i, :], v[name].unsqueeze(0)).then_inc(ld_rows, 16)
            act_e.dma_start(wk0[:], v["L0_xattn_Wk"]).then_inc(ld_w0, 16)
            act_e.dma_start(wv0[:], v["L0_xattn_Wv"]).then_inc(ld_w0, 16)
            act_e.dma_start(wq0[:], v["L0_xattn_Wq"]).then_inc(ld_w0, 16)
            act_e.dma_start(bv0[:], v["L0_xattn_bv"].unsqueeze(0).broadcast_to([SC, D])).then_inc(ld_w0, 16)
            for i, name in enumerate(("L1_xattn_Wq", "L1_xattn_Wk", "L1_xattn_Wv", "L1_xattn_W0")):
                act_e.dma_start(w1raw[:, i, :], v[name]).then_inc(ld_w1, 16)

            for i in range(3):
                n = min(6, B - 6 * i)
                act_e.wait_ge(ctxT_lo, i + 1)
                src = bank[i][:, 0:n * SC].rearrange("p (b s) -> p b s", s=SC)[:, :, SA:SC]
                nc.scalar.copy(ctxT[:, 6 * i:6 * i + n, 2 * SA:CT].rearrange("p b (r s) -> p b r s", r=E),
                               src.unsqueeze(2).broadcast_to([P, n, E, SB])).then_inc(ctxT_hi, 1)
            act_e.wait_ge(vc_done, 1)
            for i in range(3):
                n = min(6, B - 6 * i)
                act_e.wait_ge(k_ps, i + 1)
                fn(k0T[:, 6 * SC * i:6 * SC * i + n * SC], bank[4 + i][:, 0:n * SC], ACT.Identity,
                   bias=col("bk0")).then_inc(k0_done, 1)

            def ln_copy(n, read, count, bk=7):
                act_e.wait_ge(xnT_ps, n + 1)
                since(act_e, read, count, 0)
                nc.scalar.copy(xnT[:], bank[bk][:]).then_inc(xnT_done, 1)

            def exp0(g):
                act_e.wait_ge(s0_shifted, g + 1)
                fn(e0[:], e0[:], ACT.Exp).then_inc(e0_done, 1)

            def q0_copy(g):
                act_e.wait_ge(q0_ps, g + 1)
                since(act_e, s0_ps, g, 0)
                fn(q0T[:], bank[1][:], ACT.Identity, bias=bqs[:, 0:1], scale=float(D) ** -0.5).then_inc(q0_done, 1)

            def weights0_copy(g):
                act_e.wait_ge(at0_ps, g + 1)
                since(act_e, o0_ps, g, 0)
                nc.scalar.copy(at0T[:], bank[3][0:SC, :]).then_inc(at0_done, 1)

            act_e.wait_ge(bqs_done, 2)
            for k in range(G + 1):
                if k < G:
                    ln_copy(LN_A + k, q0_ps, k)
                if k >= 1:
                    exp0(k - 1)
                if k < G:
                    q0_copy(k)
                if k >= 1:
                    weights0_copy(k - 1)

            act_e.wait_ge(w1T_ps, 1)
            nc.scalar.copy(w1T[:].rearrange("p i d -> p (i d)"), bank[6][:]).then_inc(w1T_done, 1)
            for i, bk in enumerate((5, 0, 6)):
                n = min(6, B - 6 * i)
                act_e.wait_ge(k_ps, 4 + i)
                fn(k1T[:, 6 * i:6 * i + n, :].rearrange("p b s -> p (b s)"), bank[bk][:, 0:n * SC], ACT.Identity,
                   bias=col("bk1")).then_inc(k1_done, 1)
            act_e.wait_ge(c_zero, 1)
            for i in range(G):
                act_e.wait_ge(v1_ps, i + 1)
                src = bank[1 + i][SA:P, :].rearrange("p (t c r d) -> p t c r d", t=TPG, r=2, d=DH)
                nc.scalar.copy(v1a[SA:P, TPG * i:TPG * (i + 1), :, 1, 0:DH], src[:, :, :, 1, :]).then_inc(v1_odd, 1)
            act_e.wait_ge(c_esel, 3)
            for r in (32, 64):
                nc.scalar.copy(esel[r:r + 32, :], esel[0:32, :]).then_inc(c_esel, 1)

            def sigmoid_enc(g):
                for k in range(2):
                    act_e.wait_ge(enc_ps, 2 * g + k + 1)
                    since(act_e, cont_ps, g, 0)
                    fn(spT[:, k, :], bank[1 + k][:], ACT.Sigmoid, bias=col(f"enc{k}")).then_inc(sp_done, 1)

            def tanh_router(g):
                act_e.wait_ge(r1_ps, g + 1)
                since(act_e, lg_ps, g, 0)
                act_e.wait_ge(c_misc, 1)
                fn(tT[0:M0, :], bank[4][0:M0, :], ACT.Tanh, bias=col("rb1", M0)).then_inc(t_done, 1)

            def gate_weights(k):
                act_e.wait_ge(gd_done, k + 1)
                fn(gw[:, 0, :], gd[:], ACT.Sigmoid, scale=-1.0).then_inc(gw_done, 1)
                fn(gw[:, 1, :], gd[:], ACT.Sigmoid).then_inc(gw_done, 1)

            ln_copy(LN_B, q0_ps, G)
            sigmoid_enc(0)
            def router0(k):
                ln_copy(k + LN_B, enc_ps, k * 2)
                tanh_router(k - 1)
                sigmoid_enc(k)

            router0(1)
            with act_e.Fori(2, G) as k:
                router0(k)
            tanh_router(G - 1)

            def relu0(g, e):
                act_e.wait_ge(h_ps, g * E + e + 1)
                since(act_e, y_ps, g * E, e - 3)
                fn(hT[:, e % 4, :], bank[4][:], ACT.Relu, bias=col(f"be1_{e}")).then_inc(h_act, 1)

            def mix_copy(g):
                act_e.wait_ge(acc_ps, g * TPG + TPG)
                since(act_e, c2s_ps, g * 2, 0)
                nc.scalar.copy(oT[:], bank[6][:]).then_inc(oT_done, 1)

            def sigmoid_c2s(g):
                since(act_e, dec_ps, g, 0)
                for k in range(2):
                    act_e.wait_ge(c2s_ps, g * 2 + k + 1)
                    fn(sp2T[:, k, :], bank[7 - k][:], ACT.Sigmoid, bias=col(f"c2s{k}")).then_inc(sp2_done, 1)

            def sigmoid_dec(g):
                act_e.wait_ge(dec_ps, g + 1)
                since(act_e, dn_done, g * TPG, 0)
                fn(dc[:].rearrange("p t d -> p (t d)"), bank[7][:], ACT.Sigmoid).then_inc(dc_done, 1)

            def mixture0(g, before):
                for e in range(0, E, 2):
                    relu0(g, e)
                    if before and e == 2:
                        mix_copy(g - 1)
                    if before and e == 4:
                        sigmoid_c2s(g - 1)
                if before:
                    sigmoid_dec(g - 1)

            relu0(0, 0)
            relu0(0, 2)
            gate_weights(0)
            relu0(0, 4)
            relu0(0, 6)
            mixture0(1, True)
            with act_e.Fori(2, G) as g:
                mixture0(g, True)

            def q1_copy(g, bank_t, bank_q):
                ln_copy(LN_C + g, q1_ps if g else enc_ps, g or 2 * G, bank_t)
                act_e.wait_ge(q1_ps, g + 1)
                fn(wideT[:, N * g:N * (g + 1)], bank[bank_q][:], ACT.Identity, bias=bqs[:, 1:2],
                   scale=float(DH) ** -0.5).then_inc(q1_done, 1)

            mix_copy(G - 1)
            q1_copy(0, 4, 5)
            sigmoid_c2s(G - 1)
            q1_copy(1, 4, 5)
            sigmoid_dec(G - 1)
            q1_copy(2, 4, 5)

            def weights_copy(b, j):
                act_e.wait_ge(pTa_ps, b + 1)
                since(act_e, o1_ps, b, -1)
                for k in range(2):
                    last = nc.scalar.copy(pTa[:, j % 2, 512 * k:512 * (k + 1)], bank[3 + k][:])
                last.then_inc(pTa_done, 1)
                act_e.wait_ge(pTb_ps, b + 1)
                nc.scalar.copy(pTb[:, j % 2, :], bank[5][0:RB, 0:2 * P]).then_inc(pTb_done, 1)

            def heads_copy(b):
                act_e.wait_ge(at1T_ps, b + 1)
                act_e.wait_ge(y1_ps, b)
                fn(at1T[:], bank[7][:, 0:P], ACT.Identity, bias=col("bv1")).then_inc(at1T_done, 1)

            def exp1(b, j):
                act_e.wait_ge(s1_shifted, b * 3 + 3)
                fn(e1[:, j % 2, :], e1[:, j % 2, :], ACT.Exp).then_inc(e1_done, 1)

            def attention1(b, j, first):
                if first >= 3:
                    heads_copy(b - 3)
                if first < B:
                    exp1(b, j)
                if 1 <= first < B + 1:
                    weights_copy(b - 1, j - 1)

            for b in range(4):
                if b == 2:
                    q1_copy(G - 1, 7, 6)
                attention1(b, b, b)
            act_e.wait_ge(q1_ps, G)
            with act_e.Fori(1, G) as i:
                for j in range(4):
                    attention1(i * 4 + j, j, 4)
                ln_copy(i + (LN_D - 1), lg_ps, i + (G - 1))
            for b in range(B, B + 3):
                attention1(b, b, b)
            act_e.wait_ge(wide_done, G - 1)
            ln_copy(LN_D + G - 1, lg_ps, 2 * G - 1)

            gate_weights(1)

            def silu(g, j):
                act_e.wait_ge(fh_ps, g * NB + j + 1)
                since(act_e, u1_done, g * NB, j - 1)
                fn(sil[:, j % 2, :], bank[j % 2][:], ACT.Silu).then_inc(sil_done, 1)

            for j in range(NB):
                silu(0, j)
            with act_e.Fori(1, G) as g:
                for j in range(NB):
                    silu(g, j)

        @block.vector
        def _(dve):
            v = nc.vector
            dve.wait_ge(vc_ps, 1)
            v.tensor_copy(vcols[:], bank[7][:, 0:NR]).then_inc(vc_done, 1)
            dve.wait_ge(c_id, 2)
            v.tensor_copy(ident_h[:], ident[:]).then_inc(c_idh, 1)
            for i, (name, scale) in enumerate((("bq0", float(D) ** -0.5), ("bq1", float(DH) ** -0.5))):
                dve.wait_ge(vc_done, 1)
                v.tensor_scalar(bqs[:, i:i + 1], col(name), scale, None, ALU.mult).then_inc(bqs_done, 1)

            def moments(st, mom, cols, read, steps, base_steps, done):
                m = lambda i: mom[:, i, cols]
                v.tensor_tensor(m(0), st(1), st(4), ALU.add).then_inc(steps, 1)
                v.tensor_tensor(m(1), st(1), st(4), ALU.subtract).then_inc(steps, 1)
                v.scalar_tensor_tensor(out=m(2), in0=st(2), scalar=D * EPS, in1=st(5),
                                       op0=ALU.add, op1=ALU.add).then_inc(steps, 1)
                dve.wait_ge(steps, base_steps + 3)
                v.tensor_scalar(m(3), m(0), 0.5, None, ALU.mult).then_inc(steps, 1)
                v.scalar_tensor_tensor(out=m(4), in0=m(1), scalar=0.25, in1=m(1),
                                       op0=ALU.mult, op1=ALU.mult).then_inc(steps, 1)
                dve.wait_ge(steps, base_steps + 5)
                v.scalar_tensor_tensor(out=m(5), in0=m(2), scalar=1.0 / D, in1=m(4),
                                       op0=ALU.mult, op1=ALU.add).then_inc(done, 1)

            def ln_stats_of(n, b):
                v.bn_stats(stats[:, ds(b, 1), :].rearrange("p o s -> p (o s)"), x[:, ds(b * D, D)]).then_inc(ln_stats, 1)

            def ln_moments_of(n, g):
                dve.wait_ge(ln_stats, n * TPG + TPG)
                since(dve, ln_applied, n * TPG, (1 - G) * TPG)
                moments(lambda k: stats[:, ds(g * TPG, TPG), k], mom, ds(g * TPG, TPG), ln_stats, ln_steps,
                        n * 5, ln_moments)

            def ln_apply(n, g):
                dve.wait_ge(ln_rstd, n + 1)
                dve.wait_ge(ln_steps, n * 5 + 4)
                since(dve, xnT_ps, n, 0)
                for t in range(TPG):
                    v.tensor_scalar(xn[:, t, :], x[:, ds(g * N + t * D, D)], mom[:, 3, ds(g * TPG + t, 1)],
                                    rstd[:, ds(g * TPG + t, 1)], ALU.subtract, ALU.mult).then_inc(ln_applied, 1)

            for g in range(G):
                dve.wait_ge(ld_x[g], 16)
                for t in range(TPG):
                    ln_stats_of(LN_A + g, TPG * g + t)
                ln_moments_of(LN_A + g, g)
                if g == 0:
                    dve.wait_ge(ctxT_ps, 1)
                for i in range(3):
                    if g == (0, 1, 1)[i]:
                        n = min(6, B - 6 * i)
                        dve.wait_ge(ctxT_ps, i + 1)
                        src = bank[i][:, 0:n * SC].rearrange("p (b s) -> p b s", s=SC)[:, :, 0:SA]
                        v.tensor_copy(ctxT[:, 6 * i:6 * i + n, 0:2 * SA].rearrange("p b (r s) -> p b r s", r=2),
                                      src.unsqueeze(2).broadcast_to([P, n, 2, SA])).then_inc(ctxT_lo, 1)
            ln_apply(LN_A, 0)
            dve.wait_ge(ld_w0, 16 * N_W0)
            for i in range(G):
                dve.wait_ge(v0_ps, i + 1)
                v.tensor_tensor(v0[:, N * i:N * (i + 1)].rearrange("p (t d) -> p t d", d=D),
                                bank[i][0:SC, :].rearrange("p (t d) -> p t d", d=D),
                                bv0[:].unsqueeze(1).broadcast_to([SC, TPG, D]), ALU.add).then_inc(v0_done, 1)

            def shift0(g):
                dve.wait_ge(s0_ps, g + 1)
                since(dve, at0_ps, g, 0)
                since(dve, sum0_done, g, 0)
                v.scalar_tensor_tensor(out=e0[:].rearrange("p t s -> p (t s)"),
                                       in0=mask0[:, TPG * SC * g:TPG * SC * (g + 1)], scalar=-1e9,
                                       in1=bank[2][:, 0:TPG * SC], op0=ALU.mult, op1=ALU.add).then_inc(s0_masked, 1)
                dve.wait_ge(s0_masked, g + 1)
                since(dve, s0_shifted, g, 0)
                v.tensor_reduce(m0[:], e0[:], AX.X, ALU.max).then_inc(m0_done, 1)
                dve.wait_ge(m0_done, g + 1)
                v.tensor_tensor(e0[:], e0[:], m0[:].unsqueeze(2).broadcast_to([P, TPG, SC]),
                                ALU.subtract).then_inc(s0_shifted, 1)

            def sums0(g):
                dve.wait_ge(e0_done, g + 1)
                since(dve, r0_done, g, 0)
                v.tensor_reduce(sum0[:], e0[:], AX.X, ALU.add).then_inc(sum0_done, 1)
                dve.wait_ge(sum0_done, g + 1)
                since(dve, x1_done, g * TPG, 0)
                v.reciprocal(r0[:], sum0[:]).then_inc(r0_done, 1)

            def add0(g):
                dve.wait_ge(r0_done, g + 1)
                dve.wait_ge(o0_ps, g + 1)
                dve.wait_ge(ln_applied, TPG * (g + 1))
                for t in range(TPG):
                    xt = x[:, N * g + D * t:N * g + D * (t + 1)]
                    v.scalar_tensor_tensor(out=xt, in0=bank[4][:, D * t:D * (t + 1)], scalar=r0[:, t:t + 1],
                                           in1=xt, op0=ALU.mult, op1=ALU.add).then_inc(x1_done, 1)
                for t in range(TPG):
                    dve.wait_ge(x1_done, TPG * g + t + 1)
                    ln_stats_of(LN_B + g, TPG * g + t)
                ln_moments_of(LN_B + g, g)

            dve.wait_ge(ld_m0, 16)
            for k in range(G + 2):
                if 1 <= k <= G:
                    shift0(k - 1)
                if k + 1 < G:
                    ln_apply(LN_A + k + 1, k + 1)
                if k >= 2:
                    add0(k - 2)
                if 1 <= k <= G:
                    sums0(k - 1)

            dve.wait_ge(ld_bias, 16 * N_BIAS)
            left = [brow[:], bres[:, 0, :], bres[:, 1, :]]
            for i in range(3):
                v.tensor_copy(bpart[:, i, :], left[i]).then_inc(c_step, 1)
                dve.wait_ge(c_step, 2 * i + 1)
                if i < 2:
                    v.tensor_tensor(left[i + 1], left[i], bpart[:, i, :], ALU.subtract).then_inc(c_step, 1)
                    dve.wait_ge(c_step, 2 * i + 2)
            v.tensor_scalar(bsel[:, 0, :], bpart[:, 0, :], ident[0:3, 0:1], None, ALU.mult).then_inc(c_step, 1)
            dve.wait_ge(c_step, 6)
            v.scalar_tensor_tensor(out=bsel[:, 1, :], in0=bpart[:, 1, :], scalar=ident[0:3, 1:2], in1=bsel[:, 0, :],
                                   op0=ALU.mult, op1=ALU.add).then_inc(c_step, 1)
            dve.wait_ge(c_step, 7)
            v.scalar_tensor_tensor(out=bsplit[:], in0=bpart[:, 2, :], scalar=ident[0:3, 2:3], in1=bsel[:, 1, :],
                                   op0=ALU.mult, op1=ALU.add).then_inc(c_split, 1)

            ln_apply(LN_B, 0)
            dve.wait_ge(c_ones, 3)
            for i in range(G):
                dve.wait_ge(v1_ps, i + 1)
                src = bank[1 + i][0:SA, :].rearrange("p (t c r d) -> p t c r d", t=TPG, r=2, d=DH)
                v.tensor_copy(v1a[0:SA, TPG * i:TPG * (i + 1), :, 0, 0:DH], src[:, :, :, 0, :]).then_inc(v1_even, 1)
                v.tensor_tensor(v1b[:, TPG * i:TPG * (i + 1), :, 0:DH],
                                bank[(0, 5, 6, 7)[i]][0:RB, :].rearrange("p (t h d) -> p t h d", t=TPG, d=DH),
                                slot_of[:].rearrange("p c e -> p (c e)").unsqueeze(1).unsqueeze(3)
                                .broadcast_to([RB, TPG, NH, DH]), ALU.mult).then_inc(v1_b, 1)

            def continuous(g):
                dve.wait_ge(cont_ps, g + 1)
                v.tensor_scalar(wideT[:, ds(g * N, N)], bank[3][:], col("s2c"), None, ALU.add).then_inc(cont_done, 1)

            ln_apply(LN_B + 1, 1)
            with dve.Fori(1, G - 1) as k:
                continuous(k - 1)
                ln_apply(k + (LN_B + 1), k + 1)
            continuous(G - 2)
            continuous(G - 1)

            def gate_tokens(k, logits, between):
                n = [k * 13]

                def step(op):
                    n[0] += 1
                    op.then_inc(g_step, 1)
                    dve.wait_ge(g_step, n[0])

                dve.wait_ge(lg_ps, G * (k + 1))
                step(v.tensor_copy(lg[:].rearrange("p b e -> p (b e)"), logits))
                for i, l in enumerate((lg, lg2)):
                    wide = lambda y: y[:, i, :].unsqueeze(2).broadcast_to([P, B, E])
                    step(v.tensor_reduce(gmx[:, i, :], l[:], AX.X, ALU.max))
                    step(v.tensor_tensor(geq[:, i], l[:], wide(gmx), ALU.is_equal))
                    step(v.tensor_tensor(gkey[:, i], geq[:, i], rank[:].unsqueeze(1).broadcast_to([P, B, E]), ALU.mult))
                    step(v.tensor_reduce(gkx[:, i, :], gkey[:, i], AX.X, ALU.max))
                    step(v.tensor_tensor(goh[:, i], gkey[:, i], wide(gkx), ALU.is_equal))
                    if i == 0:
                        step(v.scalar_tensor_tensor(out=lg2[:], in0=goh[:, 0], scalar=NEG_BIG, in1=lg[:],
                                                    op0=ALU.mult, op1=ALU.add))
                v.tensor_tensor(gd[:], gmx[:, 1, :], gmx[:, 0, :], ALU.subtract).then_inc(gd_done, 1)
                between()
                for i in range(2):
                    dve.wait_ge(gw_done, 2 * k + i + 1)
                    last = v.tensor_tensor(gwo[:, i], goh[:, i], gw[:, i, :].unsqueeze(2).broadcast_to([P, B, E]), ALU.mult)
                step(last)
                v.tensor_tensor(gates[:], gwo[:, 0], gwo[:, 1], ALU.add).then_inc(gates_done, 1)

            def relu0(g, e):
                dve.wait_ge(h_ps, g * E + e + 1)
                since(dve, y_ps, g * E, e - 3)
                v.tensor_scalar(hT[:, e % 4, :], bank[5][:], col(f"be1_{e}"), 0.0, ALU.add, ALU.max).then_inc(h_dve, 1)

            def gate_outputs(g):
                dve.wait_ge(y_ps, g * E + E)
                for t in range(TPG):
                    since(dve, gh_done, g * TPG, t - 1)
                    v.tensor_tensor(gy[:, t % 2, :].rearrange("p (e m) -> p e m", e=E),
                                    bank[t][:].rearrange("p (e m) -> p e m", e=E),
                                    gates[:, ds(g * TPG + t, 1), :].rearrange("p o e -> p (o e)").unsqueeze(2)
                                    .broadcast_to([P, E, M0]), ALU.mult).then_inc(gy_done, 1)

            def decoded_moments(g):
                dve.wait_ge(dc_done, g + 1)
                since(dve, lo_moments, g, 0)
                for t in range(TPG):
                    v.bn_stats(stats2[:, t, :], dc[:, t, :]).then_inc(lo_stats, 1)
                dve.wait_ge(lo_stats, g * TPG + TPG)
                since(dve, dn_done, g * TPG, 0)
                since(dve, lo_rstd, g, 0)
                moments(lambda k: stats2[:, :, k], mom2, slice(0, TPG), lo_stats, lo_steps, g * 5, lo_moments)

            def decoded_norm(g):
                dve.wait_ge(lo_rstd, g + 1)
                dve.wait_ge(lo_steps, g * 5 + 4)
                since(dve, dg_done, g, 0)
                for t in range(TPG):
                    v.tensor_scalar(dn[:, t, :], dc[:, t, :], mom2[:, 3, t:t + 1], rstd2[:, t:t + 1],
                                    ALU.subtract, ALU.mult).then_inc(dn_done, 1)
                dve.wait_ge(dn_done, g * TPG + TPG)
                since(dve, x2_done, g, 0)
                v.tensor_tensor(dg[:], dn[:], ln_g[:].unsqueeze(1).broadcast_to([P, TPG, D]), ALU.mult).then_inc(dg_done, 1)
                dve.wait_ge(dg_done, g + 1)
                dve.wait_ge(xb_done, g + 1)
                v.tensor_tensor(x[:, ds(g * N, N)], dg[:].rearrange("p t d -> p (t d)"), xb[:], ALU.add).then_inc(x2_done, 1)
                dve.wait_ge(x2_done, g + 1)
                for t in range(TPG):
                    ln_stats_of(g + LN_C, g * TPG + t)
                ln_moments_of(g + LN_C, g)

            def mixture0(g, before):
                for e in range(1, E, 2):
                    relu0(g, e)
                if before:
                    decoded_moments(g - 1)
                gate_outputs(g)
                if before:
                    decoded_norm(g - 1)

            gate_tokens(0, bank[5][:, 0:B * E], lambda: relu0(0, 1))
            for e in range(3, E, 2):
                relu0(0, e)
            dve.wait_ge(gates_done, 1)
            gate_outputs(0)
            mixture0(1, True)
            with dve.Fori(2, G) as g:
                mixture0(g, True)
            for g in range(G - 1):
                ln_apply(LN_C + g, g)
            decoded_moments(G - 1)
            decoded_norm(G - 1)

            def shift1(b, j, between):
                for k in range(3):
                    dve.wait_ge(s1_ps, b * 3 + k + 1)
                    if k == 0:
                        dve.wait_ge(mx_done, b)
                    if k < 2:
                        v.tensor_reduce(mxa[:, 8 * k:8 * (k + 1)], bank[k][:].rearrange("p (h s) -> p h s", s=SA),
                                        AX.X, ALU.max).then_inc(mxab_done, 1)
                    else:
                        v.tensor_reduce(mxb[:], bank[2][:, 0:CB].rearrange("p (h s) -> p h s", h=NH),
                                        AX.X, ALU.max).then_inc(mxab_done, 1)
                dve.wait_ge(mxab_done, b * 3 + 3)
                dve.wait_ge(s1_shifted, b * 3)
                v.tensor_tensor(mx[:], mxa[:], mxb[:], ALU.max).then_inc(mx_done, 1)
                dve.wait_ge(mx_done, b + 1)
                since(dve, pTb_ps, b, -1)
                for k in range(2):
                    v.tensor_tensor(e1[:, j % 2, 512 * k:512 * (k + 1)].rearrange("p (h s) -> p h s", s=SA),
                                    bank[k][:].rearrange("p (h s) -> p h s", s=SA),
                                    mx[:, 8 * k:8 * (k + 1)].unsqueeze(2).broadcast_to([P, 8, SA]),
                                    ALU.subtract).then_inc(s1_shifted, 1)
                    if k == 0:
                        between()
                v.tensor_tensor(e1[:, j % 2, CA:CA + CB].rearrange("p (h s) -> p h s", s=SB),
                                bank[2][:, 0:CB].rearrange("p (h s) -> p h s", s=SB),
                                mx[:].unsqueeze(2).broadcast_to([P, NH, SB]), ALU.subtract).then_inc(s1_shifted, 1)

            def normalize1(b, j):
                dve.wait_ge(o1_ps, b + 1)
                dve.wait_ge(at1_done, b)
                o = bank[6][:, 0:NH * DV].rearrange("p (h v) -> p h v", v=DV)
                v.reciprocal(rs1[:], o[:, :, DH]).then_inc(rs1_done, 1)
                dve.wait_ge(rs1_done, b + 1)
                since(dve, at1T_ps, b, -1)
                v.tensor_tensor(at1[:, j % 2, :, :], o[:, :, 0:DH], rs1[:].unsqueeze(2).broadcast_to([P, NH, DH]),
                                ALU.mult).then_inc(at1_done, 1)

            def add1(b):
                dve.wait_ge(y1_ps, b + 1)
                v.tensor_tensor(x[:, ds(b * D, D)], bank[7][:, P:2 * P], x[:, ds(b * D, D)], ALU.add).then_inc(x3_done, 1)
                dve.wait_ge(x3_done, b + 1)
                ln_stats_of(LN_D, b)

            def attention1(b, j, first, between=lambda: None):
                def add():
                    if first >= 3:
                        add1(b - 3)
                    between()
                if first < B:
                    shift1(b, j, add)
                else:
                    add()
                if 2 <= first < B + 2:
                    normalize1(b - 2, j - 2)

            def wide_copy(g):
                dve.wait_ge(xnT_done, g + (LN_D + 1))
                v.tensor_copy(wideT[:, ds(g * N, N)], xnT[:]).then_inc(wide_done, 1)

            for b in range(4):
                attention1(b, b, b)
                if b == 0:
                    ln_apply(LN_C + G - 1, G - 1)
            with dve.Fori(1, G) as i:
                attention1(i * 4, 0, 4)
                attention1(i * 4 + 1, 1, 4)
                attention1(i * 4 + 2, 2, 4, lambda: ln_moments_of(i + (LN_D - 1), i - 1))
                attention1(i * 4 + 3, 3, 4, lambda: ln_apply(i + (LN_D - 1), i - 1))
                wide_copy(i - 1)
            for b in range(B, B + 3):
                attention1(b, b, b)
            ln_moments_of(LN_D + G - 1, G - 1)
            ln_apply(LN_D + G - 1, G - 1)
            wide_copy(G - 1)

            dve.wait_ge(c_misc, 5)
            gate_tokens(1, bank[6][:, LG1:LG1 + B * E], lambda: None)
            dve.wait_ge(gates_done, 2)
            v.tensor_copy(gsp[:, :, 0:E], gates[:]).then_inc(gsp_done, 1)
            dve.wait_ge(gsp_done, 1)
            v.tensor_tensor(gres[:, 0], gates[:], gsp[:, :, 0:E], ALU.subtract).then_inc(c_split, 1)
            dve.wait_ge(c_split, 2)
            v.tensor_copy(gsp[:, :, 32:32 + E], gres[:, 0]).then_inc(gsp_done, 1)
            dve.wait_ge(gsp_done, 2)
            v.tensor_tensor(gres[:, 1], gres[:, 0], gsp[:, :, 32:32 + E], ALU.subtract).then_inc(c_split, 1)
            dve.wait_ge(c_split, 3)
            v.tensor_copy(gsp[:, :, 64:64 + E], gres[:, 1]).then_inc(gsp_done, 1)
            for i in range(2):
                dve.wait_ge(gT_ps, i + 1)
                v.tensor_copy(gT[:, 8 * P * i:8 * P * (i + 1)], bank[3 + i][:].bitcast(BF16)[0:96, :]).then_inc(gT_done, 1)

            def gated(g, j):
                dve.wait_ge(sil_done, g * NB + j + 1)
                dve.wait_ge(fg_ps, g * NB + j + 1)
                since(dve, act_done, g * NB, j - 1)
                v.tensor_tensor(u1[:, j % 2, :], bank[2 + j % 2][:], sil[:, j % 2, :], ALU.mult).then_inc(u1_done, 1)
                dve.wait_ge(u1_done, g * NB + j + 1)
                dve.wait_ge(gb_ps, g * NB + j + 1)
                since(dve, fy_ps, g * NB, j - 2)
                v.tensor_tensor(act[:, j % 3, :], bank[4 + j % 2][:], u1[:, j % 2, :], ALU.mult).then_inc(act_done, 1)

            def result(g):
                dve.wait_ge(fy_ps, g * NB + NB)
                v.tensor_tensor(x[:, ds(g * N, N)], bank[6][:], x[:, ds(g * N, N)], ALU.add).then_inc(res_done, 1)

            for j in range(NB):
                gated(0, j)
            with dve.Fori(1, G) as g:
                for j in range(NB):
                    if j == 2:
                        result(g - 1)
                    gated(g, j)
            result(G - 1)


def since(eng, signal, base, k):
    if not (isinstance(base, int) and base + k <= 0):
        eng.wait_ge(signal, base + k)


_INS = ["x", "ctx_1024", "mask_BxSxS2_fk0", "mask_Bx1xSxS2_bf1",
        "L0_xattn_Wq", "L0_xattn_bq", "L0_xattn_Wk", "L0_xattn_bk", "L0_xattn_Wv", "L0_xattn_bv",
        "L0_ffn_enc_W", "L0_ffn_enc_b", "L0_ffn_s2c_W", "L0_ffn_s2c_b", "L0_ffn_rW1", "L0_ffn_rb1",
        "L0_ffn_rW2", "L0_ffn_rb2", "L0_ffn_We1", "L0_ffn_be1", "L0_ffn_We2", "L0_ffn_be2",
        "L0_ffn_c2s_W", "L0_ffn_c2s_b", "L0_ffn_dec_W", "L0_ffn_dec_b", "L0_ffn_ln_g", "L0_ffn_ln_b",
        "L1_xattn_Wq", "L1_xattn_bq", "L1_xattn_Wk", "L1_xattn_bk", "L1_xattn_Wv", "L1_xattn_bv",
        "L1_xattn_W0", "L1_xattn_b0", "L1_ffn_Wr", "L1_ffn_W1", "L1_ffn_W2", "L1_ffn_W3"]


def kernel(**inputs):
    import concourse.bacc as _bacc
    from concourse.bass_utils import run_bass_kernel_spmd as _run

    nc = _bacc.Bacc("TRN2", target_bir_lowering=False, num_devices=1)
    arrays, aps = {}, {}
    for name in _INS:
        v = np.ascontiguousarray(inputs[name])
        if v.dtype == np.bool_:
            v = v.view(np.uint8)
        arrays[f"in_{name}"] = v
        aps[name] = nc.dram_tensor(f"in_{name}", v.shape, mybir.dt.from_np(v.dtype), kind="ExternalInput").ap()
    out = nc.dram_tensor("out", (B, S, D), F32, kind="ExternalOutput").ap()
    xattn_ffn_program(nc, aps, out)
    return _run(nc, [arrays], core_ids=[0]).results[0]["out"]
```

```python
from contextlib import ExitStack

import concourse.bass as bass
import numpy as np
from concourse import mybir
from concourse.alu_op_type import AluOpType as ALU

F32 = mybir.dt.float32
BF16 = mybir.dt.bfloat16
F32R = mybir.dt.float32r
ACT = mybir.ActivationFunctionType
AX = mybir.AxisListType
ds = bass.ds

P = 128
B, S, D = 16, 128, 128
SC = 77
TPG = 4
G = B // TPG
N = TPG * S
NH, DH = 16, 8
E = 8
H0, M0 = 256, 64
HX = H0 // 2
H1 = 192
NB = E * H1 // P
SA = 64
SB = SC - SA
NA = NH // 2
RB = E * SB
CA, CB = NH * SA, NH * SB
DV = DH + 1
CT = 2 * SA + RB
HIDDEN = -float(2 ** 100)
EPS = 1e-5
NEG_BIG = -1e38


def xattn_ffn_program(nc, a, out):
    ctx = ExitStack()
    with ctx:
        def sb(name, shape, dt=F32):
            return ctx.enter_context(nc.sbuf_tensor(name, shape, dt))

        def sem(name):
            return ctx.enter_context(nc.semaphore(name))

        def room(*uses):
            size = lambda use: sum(int(np.prod(t[1][1:])) * (2 if t[2:] == (BF16,) else 4) for t in use)
            tensors = []
            for n, use in enumerate(uses):
                with ExitStack() as use_of_room:
                    keep = ctx if n == len(uses) - 1 else use_of_room
                    tensors += [keep.enter_context(nc.sbuf_tensor(*t[:2], *(t[2:] or (F32,)))) for t in use]
                    rest = max(map(size, uses)) - size(use)
                    if keep is ctx and rest:
                        ctx.enter_context(nc.sbuf_tensor(f"rest_{use[0][0]}", [P, rest // 4], F32))
            return tensors

        x = sb("x", [P, B * D])
        room_a = sb("room_a", [P, B * D])
        w3_hi, = room([("w3_hi", [P, E * H1], F32R)])
        room_c = sb("room_c", [P, 2, B * SC])
        v0_room, w3_lo = room([("v0", [P, B * D])], [("w3_lo", [P, E * H1], F32R)])
        ctx_in = room_a[0:SC, :].rearrange("p (b d) -> p b d", b=B)
        ctxT, w1_hi, w1_lo = room([("ctxT", [P, B, CT])],
                                  [("w1_hi", [P, E * H1], F32R), ("w1_lo", [P, E * H1], F32R)])
        k0T = room_c[:, 0, :]
        v0 = v0_room[0:SC, :]
        k1T = sb("k1T", [P, B, SC])
        v1, act_lo, act = room([("v1", [P, B, 2, NH * DV])],
                               [("act_lo", [P, 4, N], F32R), ("act", [P, 2, N])])
        v1a = v1[:, :, 0, :].rearrange("p b (c r v) -> p b c r v", r=2, v=DV)
        v1b = v1[0:RB, :, 1, :].rearrange("p b (h v) -> p b h v", v=DV)
        kblk, gh_hi, gh_lo, gh2, act_hi, sil, u1 = room([("kblk", [P, 4, CA + CB])],
                                     [("gh_hi", [P, 4, N], F32R), ("gh_lo", [P, 4, N], F32R), ("gh2", [P, N])],
                                     [("act_hi", [P, 4, N], F32R), ("sil", [P, 2, N]), ("u1", [P, 2, N])])
        mask0 = room_c[:, 1, :]
        mask1 = sb("mask1", [P, B, SC], mybir.dt.uint8)
        hide1 = sb("hide1", [P, B, SC], BF16)

        enc_w = sb("enc_w", [P, H0])
        s2c_w = sb("s2c_w", [P, 2, 2, M0])
        r_w1 = sb("r_w1", [P, 2, M0])
        r_w2 = sb("r_w2", [M0 + 1, E])
        c2s_w = sb("c2s_w", [P, H0])
        we1, gT = room([("we1", [P, E, HX])], [("gT", [96, B * P], BF16)])
        we2, xb = room([("we2", [P, E, M0])], [("xb", [P, TPG * D])])
        r_w1_hi, r_w1_lo = (sb(f"r_w1_{i}", [P, 2 * M0], F32R) for i in ("hi", "lo"))
        we1_hi, we1_lo = (sb(f"we1_{i}", [P, E, HX], F32R) for i in ("hi", "lo"))
        we2_hi, we2_lo = (sb(f"we2_{i}", [P, E, 2, M0], F32R) for i in ("hi", "lo"))
        c2s_hi, c2s_lo = (sb(f"c2s_{i}", [P, H0], F32R) for i in ("hi", "lo"))
        be2 = sb("be2", [E, 2, M0])
        sel8 = sb("sel8", [E, 96])
        be2_x, be2_p, be2_s, geq, gkey, lg2 = room(
            [("be2_x", [96, 2, P]), ("be2_p", [96, 3, P], BF16), ("be2_s", [96, 2, P])],
            [("geq", [P, 2, B, E]), ("gkey", [P, 2, B, E]), ("lg2", [P, B, E])])
        be2_w = sb("be2_w", [96, P], BF16)
        part_of = sb("part_of", [96, 4])
        dec_w = sb("dec_w", [P, 2, D])
        ln_g = sb("ln_g", [P, D])
        ln_b = sb("ln_b", [P, D])
        w1raw, gwo, gres = room([("w1raw", [P, 4, D])], [("gwo", [P, 2, B, E]), ("gres", [P, 2, B, E])])
        w1T = sb("w1T", [P, 4, D])
        wr = sb("wr", [P, E])
        f_w1, w2_hi = room([("f_w1", [P, E * H1])], [("w2_hi", [P, NB, D], F32R)])
        f_w3, w2_lo = room([("f_w3", [P, E * H1])], [("w2_lo", [P, NB, D], F32R)])
        f_w2 = sb("f_w2", [P, NB, D])

        ROWS = ["bq0", "bk0", "enc0", "enc1", "rb1", "s2c"] + [f"be1_{e}" for e in range(E)] + \
               ["c2s0", "c2s1", "bq1", "bk1", "bv1"]
        NR = len(ROWS)
        vrows = sb("vrows", [NR, P])
        vcols = sb("vcols", [P, NR])

        def col(name, rows=P):
            i = ROWS.index(name)
            return vcols[0:rows, i:i + 1]

        NBR = 2 * D
        brow = sb("brow", [3, NBR])
        early = kblk[0:3, :, :].rearrange("p r c -> p (r c)")
        bres = early[:, 0:2 * NBR].rearrange("p (i n) -> p i n", i=2)
        bsel = early[:, 2 * NBR:4 * NBR].rearrange("p (i n) -> p i n", i=2)
        bpart = early[:, 4 * NBR:4 * NBR + 3 * NBR // 2].bitcast(BF16).rearrange("p (i n) -> p i n", i=3)
        bsplit = sb("bsplit", [3, NBR], BF16)
        ones3 = sb("ones3", [3, P], BF16)

        ident = sb("ident", [P, P])
        ident_h = sb("ident_h", [P, P], BF16)
        head_of = sb("head_of", [P, NH])
        slot_of = sb("slot_of", [RB, 2, E])
        rank = sb("rank", [P, E])
        half = sb("half", [P, TPG])
        esel = sb("esel", [96, E * P], BF16)

        stats = sb("stats", [P, B, 6])
        mom = sb("mom", [P, 6, B])
        rstd = sb("rstd", [P, B])
        bqs = sb("bqs", [P, 2])
        xn = sb("xn", [P, TPG, D])
        xnT = sb("xnT", [P, N])
        cont, wideT, wide_hi = room([("cont", [P, G * N], F32R)], [("wideT", [P, G * N])],
                                    [("wide_hi", [P, G * N], F32R)])
        e0, at0T, wq0, wk0, wv0, bv0, dg, qt = room(
            [("e0", [P, TPG, SC]), ("at0T", [SC, N]), ("wq0", [P, D]), ("wk0", [P, D]), ("wv0", [P, D]),
             ("bv0", [SC, D])],
            [("dg", [P, TPG, D]), ("qt", [P, 2, P])])
        q0T, oS, yT = room([("q0T", [P, N])], [("oS", [P, N], F32R)], [("yT", [P, N])])
        m0 = sb("m0", [P, TPG])
        sum0 = sb("sum0", [P, TPG])
        r0 = sb("r0", [P, TPG])
        spT, pTb, at1 = room([("spT", [P, 2, N])],
                             [("pTb", [RB, 2, 2 * P]), ("at1", [P, 2, NH, DH])])
        tT, vt = room([("tT", [M0 + 1, N])], [("vt", [P, 2, 2, NH * DV])])
        hid, gh01, wide_lo = room([("hid", [P, 2, N]), ("gh01", [P, 2, N])], [("wide_lo", [P, G * N], F32R)])
        gh = [gh01[:, 0, :], gh01[:, 1, :], gh2[:]]
        sp2T = spT
        dc, dn, gsp = room([("dc", [P, TPG, D]), ("dn", [P, TPG, D])], [("gsp", [P, B, 96], BF16)])
        stats2 = sb("stats2", [P, TPG, 6])
        mom2 = sb("mom2", [P, 6, TPG])
        rstd2 = sb("rstd2", [P, TPG])
        lg = sb("lg", [P, B, E])
        goh = sb("goh", [P, 2, B, E])
        gmx = sb("gmx", [P, 2, B])
        gkx = sb("gkx", [P, 2, B])
        gd = sb("gd", [P, B])
        gw = sb("gw", [P, 2, B])
        gates = sb("gates", [P, B, E])
        e1 = room_c
        mxa = sb("mxa", [P, NH])
        mxb = sb("mxb", [P, NH])
        mx = sb("mx", [P, NH])
        pTa = room_a[:].rearrange("p (i n) -> p i n", i=2)
        rs1 = sb("rs1", [P, NH])
        at1T = sb("at1T", [P, P])

        bank = [ctx.enter_context(nc.psum_tensor(f"bank{i}", [P, 512], F32)) for i in range(8)]

        ld_x = [sem(f"ld_x{g}") for g in range(G)]
        ld_ctx = sem("ld_ctx")
        ld_rows = sem("ld_rows")
        ld_w0 = sem("ld_w0")
        ld_m0 = sem("ld_m0")
        ld_m1 = sem("ld_m1")
        ld_w1 = sem("ld_w1")
        ld_bias = sem("ld_bias")
        ld_f0 = sem("ld_f0")
        ld_f1 = sem("ld_f1")
        stored = sem("stored")
        c_id = sem("c_id")
        c_idh = sem("c_idh")
        c_sel = sem("c_sel")
        c_esel = sem("c_esel")
        c_esel_all = sem("c_esel_all")
        c_zero = sem("c_zero")
        c_ones = sem("c_ones")
        c_misc = sem("c_misc")
        c_step = sem("c_step")
        c_split = sem("c_split")
        vc_ps = sem("vc_ps")
        vc_done = sem("vc_done")
        w1T_ps = sem("w1T_ps")
        w1T_done = sem("w1T_done")
        ctxT_ps = sem("ctxT_ps")
        ctxT_lo = sem("ctxT_lo")
        ctxT_hi = sem("ctxT_hi")
        bqs_done = sem("bqs_done")
        k_ps = sem("k_ps")
        k0_done = sem("k0_done")
        k1_done = sem("k1_done")
        v0_ps = sem("v0_ps")
        v0_done = sem("v0_done")
        v1_ps = sem("v1_ps")
        v1_even = sem("v1_even")
        v1_odd = sem("v1_odd")
        v1_b = sem("v1_b")
        hide_done = sem("hide_done")
        kb_done = sem("kb_done")
        ln_stats = sem("ln_stats")
        ln_moments = sem("ln_moments")
        ln_steps = sem("ln_steps")
        ln_rstd = sem("ln_rstd")
        ln_applied = sem("ln_applied")
        xnT_ps = sem("xnT_ps")
        xnT_done = sem("xnT_done")
        q0_ps = sem("q0_ps")
        q0_done = sem("q0_done")
        s0_ps = sem("s0_ps")
        s0_masked = sem("s0_masked")
        m0_done = sem("m0_done")
        s0_shifted = sem("s0_shifted")
        e0_done = sem("e0_done")
        sum0_done = sem("sum0_done")
        r0_done = sem("r0_done")
        at0_ps = sem("at0_ps")
        at0_done = sem("at0_done")
        o0_ps = sem("o0_ps")
        x1_done = sem("x1_done")
        enc_ps = sem("enc_ps")
        sp_done = sem("sp_done")
        cont_ps = sem("cont_ps")
        cont_hi = sem("cont_hi")
        cont_lo = sem("cont_lo")
        be2_ps = sem("be2_ps")
        be2_step = sem("be2_step")
        be2_sum = sem("be2_sum")
        w0_split = sem("w0_split")
        relu_done = sem("relu_done")
        gb0_ps = sem("gb0_ps")
        gh_done = sem("gh_done")
        gh_hi_done = sem("gh_hi_done")
        gh_lo_done = sem("gh_lo_done")
        oS_hi = sem("oS_hi")
        oS_lo = sem("oS_lo")
        r1_ps = sem("r1_ps")
        t_done = sem("t_done")
        lg_ps = sem("lg_ps")
        lg_done = sem("lg_done")
        g_step = sem("g_step")
        gd_done = sem("gd_done")
        gw_done = sem("gw_done")
        gates_done = sem("gates_done")
        h_ps = sem("h_ps")
        y_ps = sem("y_ps")
        c2s_ps = sem("c2s_ps")
        sp2_done = sem("sp2_done")
        dec_ps = sem("dec_ps")
        dc_done = sem("dc_done")
        lo_stats = sem("lo_stats")
        lo_moments = sem("lo_moments")
        lo_steps = sem("lo_steps")
        lo_rstd = sem("lo_rstd")
        dn_done = sem("dn_done")
        dg_done = sem("dg_done")
        xb_done = sem("xb_done")
        x2_done = sem("x2_done")
        q1_ps = sem("q1_ps")
        q1_done = sem("q1_done")
        qt_done = sem("qt_done")
        vt_done = sem("vt_done")
        s1_ps = sem("s1_ps")
        mxab_done = sem("mxab_done")
        mx_done = sem("mx_done")
        s1_shifted = sem("s1_shifted")
        e1_done = sem("e1_done")
        pTa_ps = sem("pTa_ps")
        pTb_ps = sem("pTb_ps")
        pTa_done = sem("pTa_done")
        pTb_done = sem("pTb_done")
        o1_ps = sem("o1_ps")
        rs1_done = sem("rs1_done")
        at1_done = sem("at1_done")
        at1T_ps = sem("at1T_ps")
        at1T_done = sem("at1T_done")
        y1_ps = sem("y1_ps")
        x3_done = sem("x3_done")
        wide_done = sem("wide_done")
        gsp_done = sem("gsp_done")
        gres_done = sem("gres_done")
        gT_ps = sem("gT_ps")
        gT_done = sem("gT_done")
        fh_ps = sem("fh_ps")
        fg_ps = sem("fg_ps")
        gb_ps = sem("gb_ps")
        sil_done = sem("sil_done")
        u1_done = sem("u1_done")
        act_done = sem("act_done")
        act_hi_done = sem("act_hi_done")
        act_lo_done = sem("act_lo_done")
        f_split = sem("f_split")
        fy_ps = sem("fy_ps")
        yT_done = sem("yT_done")
        y_tok_ps = sem("y_tok_ps")
        res_done = sem("res_done")

        N_ROWS = 12
        N_W0 = 4
        N_W1 = 4
        N_F0 = 16
        N_BIAS = 2
        N_F1 = 4
        RUN_TILES = ((0, 2 * TPG), (2 * TPG, B)) * 2
        RUN_LOGITS = (2, G, G + 2, 2 * G)
        RUN_BANKS = (((7, 0, 8),), ((7, 8, B),), ((4, 0, 8),), ((7, 8, B),))
        transposes = lambda k: sum(len(b) for b in RUN_BANKS[:k + 1])
        ACTS = NB + NB // 3
        acts = lambda j: j + 1 + (j + 2) // 3
        LG1 = 256
        LN_A, LN_B, LN_C, LN_D = 0, G, 2 * G, 3 * G

        block = ctx.enter_context(nc.Block())

        @block.sync
        def _(sp):
            sp.dma_start(ctx_in[:], a["ctx_1024"].rearrange("b s d -> s b d")).then_inc(ld_ctx, 16)

            def load_tokens(g):
                sp.dma_start(x[:, N * g:N * (g + 1)].rearrange("p (b d) -> p b d", b=TPG),
                             a["x"].rearrange("b s d -> s b d")[:, TPG * g:TPG * (g + 1), :]).then_inc(ld_x[g], 16)

            load_tokens(0)
            for i, name in enumerate(("L0_xattn_bq", "L0_xattn_bk")):
                sp.dma_start(vrows[i:i + 1, :], a[name].unsqueeze(0)).then_inc(ld_rows, 16)
            sp.dma_start(vrows[2:4, :], a["L0_ffn_enc_b"].rearrange("(k p) -> k p", k=2)).then_inc(ld_rows, 16)
            for r in range(2):
                sp.dma_start(vrows[4:5, M0 * r:M0 * (r + 1)], a["L0_ffn_rb1"].unsqueeze(0)).then_inc(ld_rows, 16)
                sp.dma_start(vrows[5:6, M0 * r:M0 * (r + 1)], a["L0_ffn_s2c_b"].unsqueeze(0)).then_inc(ld_rows, 16)
            sp.dma_start(vrows[6:6 + E, :], a["L0_ffn_be1"]).then_inc(ld_rows, 16)
            sp.dma_start(vrows[14:16, :], a["L0_ffn_c2s_b"].rearrange("(k p) -> k p", k=2)).then_inc(ld_rows, 16)
            for i, name in enumerate(("L1_xattn_bq", "L1_xattn_bk", "L1_xattn_bv")):
                sp.dma_start(vrows[16 + i:17 + i, :], a[name].unsqueeze(0)).then_inc(ld_rows, 16)
            for g in range(1, G):
                load_tokens(g)
            sp.dma_start(mask0[:, :].rearrange("p (b s) -> p b s", b=B),
                         a["mask_BxSxS2_fk0"].rearrange("b t s -> t b s")).then_inc(ld_m0, 16)
            for i, name in enumerate(("L1_xattn_Wq", "L1_xattn_Wk", "L1_xattn_Wv", "L1_xattn_W0")):
                sp.dma_start(w1raw[:, i, :], a[name]).then_inc(ld_w1, 16)
            sp.dma_start(mask1[:], a["mask_Bx1xSxS2_bf1"].rearrange("b o t s -> t (b o) s")).then_inc(ld_m1, 16)
            for i, name in enumerate(("L0_ffn_dec_b", "L1_xattn_b0")):
                sp.dma_start(brow[:, D * i:D * (i + 1)],
                             a[name].unsqueeze(0).broadcast_to([3, D])).then_inc(ld_bias, 16)
            sp.dma_start(enc_w[:], a["L0_ffn_enc_W"]).then_inc(ld_f0, 16)
            for r in range(2):
                sp.dma_start(s2c_w[:, :, r, :],
                             a["L0_ffn_s2c_W"].rearrange("(k p) m -> p k m", p=P)).then_inc(ld_f0, 16)
            for r in range(2):
                sp.dma_start(r_w1[M0 * r:M0 * (r + 1)],
                             a["L0_ffn_rW1"].unsqueeze(1).broadcast_to([M0, 2, M0])).then_inc(ld_f0, 16)
            sp.dma_start(r_w2[0:M0, :], a["L0_ffn_rW2"]).then_inc(ld_f0, 16)
            sp.dma_start(r_w2[M0:M0 + 1, :], a["L0_ffn_rb2"].unsqueeze(0)).then_inc(ld_f0, 16)
            for r in range(2):
                sp.dma_start(we1[M0 * r:M0 * (r + 1)], a["L0_ffn_We1"].rearrange("e m h -> m e h")).then_inc(ld_f0, 16)
            sp.dma_start(be2[:], a["L0_ffn_be2"].unsqueeze(1).broadcast_to([E, 2, M0])).then_inc(ld_f0, 16)
            sp.dma_start(we2[:], a["L0_ffn_We2"].rearrange("e h m -> h e m")).then_inc(ld_f0, 16)
            for r in range(2):
                sp.dma_start(c2s_w[M0 * r:M0 * (r + 1), :], a["L0_ffn_c2s_W"]).then_inc(ld_f0, 16)
            sp.dma_start(dec_w[:], a["L0_ffn_dec_W"].rearrange("(k p) m -> p k m", p=P)).then_inc(ld_f0, 16)
            sp.dma_start(ln_g[:], a["L0_ffn_ln_g"].unsqueeze(0).broadcast_to([P, D])).then_inc(ld_f0, 16)
            sp.dma_start(ln_b[:], a["L0_ffn_ln_b"].unsqueeze(0).broadcast_to([P, D])).then_inc(ld_f0, 16)
            sp.dma_start(wr[:], a["L1_ffn_Wr"]).then_inc(ld_f1, 16)
            sp.dma_start(f_w1[:, :].rearrange("p (e h) -> p e h", e=E),
                         a["L1_ffn_W1"].rearrange("e c h -> c e h")).then_inc(ld_f1, 16)
            sp.dma_start(f_w3[:, :].rearrange("p (e h) -> p e h", e=E),
                         a["L1_ffn_W3"].rearrange("e c h -> c e h")).then_inc(ld_f1, 16)
            sp.dma_start(f_w2[:], a["L1_ffn_W2"].rearrange("e h c -> (e h) c")
                         .rearrange("(j p) c -> p j c", p=P)).then_inc(ld_f1, 16)
            out_v = out.rearrange("b s d -> s b d")
            for g in range(G):
                sp.wait_ge(res_done, g + 1)
                sp.dma_start(out_v[:, TPG * g:TPG * (g + 1), :],
                             x[:, N * g:N * (g + 1)].rearrange("p (b d) -> p b d", d=D)).then_inc(stored, 16)
            sp.wait_ge(stored, 16 * G)

        @block.gpsimd
        def _(pool):
            pool.memset(ident[:], 0.0).then_inc(c_id, 1)
            pool.wait_ge(c_id, 1)
            pool.affine_select(out=ident[:], in_=ident[:], compare_op=ALU.not_equal, fill=1.0, base=0,
                               pattern=[[-1, P]], channel_multiplier=1).then_inc(c_id, 1)
            pool.memset(half[:], -0.5).then_inc(c_sel, 1)

            def ln_scale(n, s, back=G - 1):
                pool.wait_ge(ln_moments, n + 1)
                since(pool, ln_applied, n * TPG, -back * TPG)
                pool.tensor_tensor(rstd[:, ds(s * TPG, TPG)], mom[:, 5, ds(s * TPG, TPG)], half[:],
                                   ALU.pow).then_inc(ln_rstd, 1)

            pool.wait_ge(c_sel, 1)
            for g in range(G):
                ln_scale(LN_A + g, g)
            for e in range(E):
                pool.memset(rank[:, e:e + 1], float(E - e)).then_inc(c_sel, 1)
            pool.memset(head_of[:], 1.0).then_inc(c_sel, 1)
            pool.memset(slot_of[:], 1.0).then_inc(c_sel, 1)
            pool.wait_ge(c_sel, E + 3)
            pool.memset(tT[M0:M0 + 1, :], 1.0).then_inc(c_misc, 1)
            pool.wait_ge(c_misc, 1)
            pool.memset(ones3[:], 1.0).then_inc(c_misc, 1)
            pool.wait_ge(c_misc, 2)
            for i, (m, w) in enumerate(((head_of, DH), (slot_of, SB))):
                steps = lambda k: [[k, NH]] if i == 0 else [[0, 2], [k, E]]
                pool.wait_ge(c_sel, E + 3 + 2 * i)
                pool.affine_select(out=m[:], in_=m[:], compare_op=ALU.is_ge, fill=0.0, base=0,
                                   pattern=steps(-w), channel_multiplier=1).then_inc(c_sel, 1)
                pool.wait_ge(c_sel, E + 4 + 2 * i)
                pool.affine_select(out=m[:], in_=m[:], compare_op=ALU.is_ge, fill=0.0, base=w - 1,
                                   pattern=steps(w), channel_multiplier=-1).then_inc(c_sel, 1)
            pool.memset(gsp[:], 0.0).then_inc(c_misc, 1)
            pool.memset(v1[:].rearrange("p b k n -> p (b k n)"), 0.0).then_inc(c_zero, 1)
            pool.wait_ge(c_zero, 1)
            pool.wait_ge(c_sel, E + 7)
            pool.memset(v1a[0:SA, :, :, 0, DH], 1.0).then_inc(c_ones, 1)
            pool.wait_ge(c_ones, 1)
            pool.memset(v1a[SA:P, :, :, 1, DH], 1.0).then_inc(c_ones, 1)
            pool.wait_ge(c_ones, 2)
            pool.tensor_copy(v1b[:, :, :, DH], slot_of[:].rearrange("p c e -> p (c e)").unsqueeze(1)
                             .broadcast_to([RB, B, NH])).then_inc(c_ones, 1)

            pool.wait_ge(ld_m1, 16)
            pool.tensor_scalar(hide1[:], mask1[:], -HIDDEN, HIDDEN, ALU.mult, ALU.add).then_inc(hide_done, 1)

            pool.wait_ge(ld_f0, 16 * N_F0)
            flat = lambda w: w[:].rearrange("p a b -> p (a b)")
            twice = we2[:].unsqueeze(2).broadcast_to([P, E, 2, M0])
            for i, (whole, hi, lo) in enumerate(((flat(r_w1), r_w1_hi[:], r_w1_lo[:]), (c2s_w[:], c2s_hi[:], c2s_lo[:]),
                                                 (we1[:], we1_hi[:], we1_lo[:]), (twice, we2_hi[:], we2_lo[:]))):
                pool.tensor_copy(hi, whole).then_inc(w0_split, 1)
                pool.wait_ge(w0_split, 2 * i + 1)
                pool.tensor_tensor(lo, whole, hi.bitcast(F32), ALU.subtract).then_inc(w0_split, 1)

            for g in range(G):
                ln_scale(LN_B + g, g)

            pool.memset(esel[0:32, :], 1.0).then_inc(c_esel, 1)
            pool.wait_ge(c_esel, 1)
            pool.affine_select(out=esel[0:32, :], in_=esel[0:32, :], compare_op=ALU.is_ge, fill=0.0, base=0,
                               pattern=[[1, E * P]], channel_multiplier=-P).then_inc(c_esel, 1)
            pool.wait_ge(c_esel, 2)
            pool.affine_select(out=esel[0:32, :], in_=esel[0:32, :], compare_op=ALU.is_ge, fill=0.0, base=P - 1,
                               pattern=[[-1, E * P]], channel_multiplier=P).then_inc(c_esel, 1)

            def key_block(b, slot):
                for lo, n_s, off in ((0, SA, 0), (SA, SB, CA)):
                    pool.tensor_tensor(
                        kblk[:, slot, off:off + NH * n_s].rearrange("p (h s) -> p h s", h=NH),
                        k1T[:, ds(b, 1), lo:lo + n_s].broadcast_to([P, NH, n_s]),
                        head_of[:].unsqueeze(2).broadcast_to([P, NH, n_s]), ALU.mult).then_inc(kb_done, 1)

            def gated_low(g, e):
                pool.wait_ge(gh_hi_done, g * E + e + 1)
                since(pool, y_ps, g * E, e - 3)
                pool.tensor_tensor(gh_lo[:, e % 4, :], gh[(g * E + e) % 3], gh_hi[:, e % 4, :].bitcast(F32),
                                   ALU.subtract).then_inc(gh_lo_done, 1)

            def add_bias(g):
                since(pool, x2_done, g, 0)
                pool.tensor_tensor(xb[:].rearrange("p (t d) -> p t d", t=TPG),
                                   x[:, ds(g * N, N)].rearrange("p (t d) -> p t d", t=TPG),
                                   ln_b[:].unsqueeze(1).broadcast_to([P, TPG, D]), ALU.add).then_inc(xb_done, 1)

            def decoded_scale(g):
                pool.wait_ge(lo_moments, g + 1)
                since(pool, x2_done, g, 0)
                pool.tensor_tensor(rstd2[:], mom2[:, 5, :], half[:], ALU.pow).then_inc(lo_rstd, 1)

            pool.wait_ge(c_split, 1)
            for g in range(G):
                for e in range(E):
                    gated_low(g, e)
                    if g >= 1 and e == 5:
                        add_bias(g - 1)
                    if g >= 1 and e == 7:
                        decoded_scale(g - 1)
                    if g >= 2 and e == 7:
                        ln_scale(LN_C + g - 2, g - 2)

            def queries(b, j):
                since(pool, s1_ps, b * 3, -3)
                pool.tensor_copy(qt[:, j % 2, :], wideT[:, ds(b * P, P)]).then_inc(qt_done, 1)

            def values(b, j):
                since(pool, o1_ps, b, -1)
                pool.tensor_copy(vt[:, j % 2, :, :].rearrange("p k n -> p (k n)"),
                                 v1[:, ds(b, 1), :, :].rearrange("p o k n -> p (o k n)")).then_inc(vt_done, 1)

            def attention1(b, j, first):
                if first + 1 < B:
                    queries(b + 1, j + 1)
                if first + 2 < B:
                    key_block(b + 2, (j + 2) % 4)
                if first >= 1:
                    values(b - 1, j - 1)

            pool.wait_ge(k1_done, 3)
            pool.wait_ge(y_ps, G * E)
            key_block(0, 0)
            pool.wait_ge(q1_done, 1)
            queries(0, 0)
            ln_scale(LN_C + 2, 2)
            key_block(1, 1)
            add_bias(G - 1)
            attention1(0, 0, 0)
            decoded_scale(G - 1)
            for b in range(1, 4):
                if b == 3:
                    pool.wait_ge(dn_done, G * TPG)
                    pool.wait_ge(dg_done, G)
                    pool.memset(gsp[:], 0.0).then_inc(c_misc, 1)
                    pool.wait_ge(q1_done, 2)
                attention1(b, b, b)
                if b == 1:
                    ln_scale(LN_C + G - 1, G - 1)
            pool.wait_ge(q1_done, G)
            with pool.Fori(1, G - 1) as i:
                for j in range(4):
                    attention1(i * 4 + j, j, 4)
                    if j == 2:
                        ln_scale(i + (LN_D - 1), 0, 0)
            for b in range(B - 4, B + 1):
                attention1(b, b, b)
                if b == B - 2:
                    ln_scale(LN_D + G - 2, 0, 0)
            ln_scale(LN_D + G - 1, 0, 0)

            def act_low(g, j):
                pool.wait_ge(act_hi_done, g * NB + j + 1)
                since(pool, fy_ps, g * NB, j - 3)
                pool.tensor_tensor(act_lo[:, j % 4, :], act[:, j % 2, :], act_hi[:, j % 4, :].bitcast(F32),
                                   ALU.subtract).then_inc(act_lo_done, 1)

            pool.wait_ge(vt_done, B)
            for j in range(NB):
                act_low(0, j)
            with pool.Fori(1, G) as g:
                for j in range(NB):
                    act_low(g, j)

        @block.tensor
        def _(pe):
            mm, tr = nc.tensor.matmul, nc.tensor.transpose
            pe.wait_ge(c_id, 2)
            pe.wait_ge(ld_ctx, 16)
            for i in range(3):
                for r in range(min(6, B - 6 * i)):
                    last = tr(bank[i][:, SC * r:SC * (r + 1)], ctx_in[:, 6 * i + r, :], ident[0:SC, 0:SC])
                last.then_inc(ctxT_ps, 1)

            def keys(w, i, bk):
                n = min(6, B - 6 * i)
                mm(bank[bk][:, 0:n * SC], w, ctxT[:, 6 * i:6 * i + n, SA:SA + SC],
                   start=True, stop=True).then_inc(k_ps, 1)

            pe.wait_ge(ld_rows, 16 * N_ROWS)
            tr(bank[7][:, 0:NR], vrows[:], ident[0:NR, 0:NR]).then_inc(vc_ps, 1)
            pe.wait_ge(ld_w0, 16 * N_W0)
            for i in range(3):
                pe.wait_ge(ctxT_lo, i + 1)
                pe.wait_ge(ctxT_hi, i + 1)
                keys(wk0[:], i, 4 + i)
            for i in range(G):
                for t in range(TPG):
                    last = mm(bank[i][0:SC, D * t:D * (t + 1)], ctxT[:, TPG * i + t, SA:SA + SC], wv0[:],
                              start=True, stop=True)
                last.then_inc(v0_ps, 1)

            def ln_transpose(n, bk=7):
                pe.wait_ge(ln_applied, n * TPG + TPG)
                since(pe, xnT_done, n, 0)
                for t in range(TPG):
                    last = tr(bank[bk][:, P * t:P * (t + 1)], xn[:, t, :], ident[:])
                last.then_inc(xnT_ps, 1)

            def q0(g):
                pe.wait_ge(xnT_done, g + 1)
                since(pe, q0_done, g, 0)
                mm(bank[1][:], wq0[:], xnT[:], start=True, stop=True).then_inc(q0_ps, 1)

            def scores0(g):
                pe.wait_ge(q0_done, g + 1)
                since(pe, s0_masked, g, 0)
                for t in range(TPG):
                    last = mm(bank[2][:, SC * t:SC * (t + 1)], q0T[:, P * t:P * (t + 1)],
                              k0T[:, SC * (TPG * g + t):SC * (TPG * g + t + 1)], start=True, stop=True)
                last.then_inc(s0_ps, 1)

            def weights0(g):
                pe.wait_ge(e0_done, g + 1)
                since(pe, at0_done, g, 0)
                for t in range(TPG):
                    last = tr(bank[3][0:SC, P * t:P * (t + 1)], e0[:, t, :], ident[:])
                last.then_inc(at0_ps, 1)

            def values0(g):
                pe.wait_ge(at0_done, g + 1)
                since(pe, x1_done, TPG * g, 0)
                for t in range(TPG):
                    last = mm(bank[4][:, P * t:P * (t + 1)], at0T[:, P * t:P * (t + 1)],
                              v0[:, N * g + P * t:N * g + P * (t + 1)], start=True, stop=True)
                last.then_inc(o0_ps, 1)

            for k in range(G + 2):
                if k == 1:
                    pe.wait_ge(k0_done, 3)
                    pe.wait_ge(v0_done, G)
                if 1 <= k <= G:
                    scores0(k - 1)
                if k == 0:
                    pe.wait_ge(vc_done, 1)
                if k < G:
                    ln_transpose(LN_A + k)
                if k >= 2:
                    values0(k - 2)
                if k == 0:
                    pe.wait_ge(v0_done, 2)
                if k < G:
                    q0(k)
                if 1 <= k <= G:
                    weights0(k - 1)

            pe.wait_ge(ld_w1, 16 * N_W1)
            for i in range(4):
                last = tr(bank[6][:, P * i:P * (i + 1)], w1raw[:, i, :], ident[:])
            last.then_inc(w1T_ps, 1)
            pe.wait_ge(ld_f0, 16 * N_F0)
            pe.wait_ge(be2_step, 1)
            pe.wait_ge(xnT_done, G)
            mm(bank[7][0:96, 0:P], sel8[:], be2[:].rearrange("p r m -> p (r m)"), start=True, stop=True).then_inc(be2_ps, 1)
            pe.wait_ge(w1T_done, 1)
            for i, bk in enumerate((5, 0, 6)):
                keys(w1T[:, 1, :], i, bk)
            pe.wait_ge(q0_done, G)
            pe.wait_ge(s0_masked, G)
            pe.wait_ge(at0_done, G)
            for i in range(G):
                if i == 3:
                    pe.wait_ge(x1_done, B)
                if i < 3:
                    pe.wait_ge(k1_done, (2, 1, 3)[i])
                else:
                    pe.wait_ge(be2_step, 3)
                for t in range(TPG):
                    b, o = TPG * i + t, D * t
                    mm(bank[1 + i][:, o:o + D], ctxT[:, b, 0:2 * SA], w1T[:, 2, :], start=True, stop=True)
                    last = mm(bank[(0, 5, 6, 7)[i]][0:RB, o:o + D], ctxT[:, b, 2 * SA:CT], w1T[:, 2, :],
                              start=True, stop=True)
                last.then_inc(v1_ps, 1)
            pe.wait_ge(v1_b, G)
            pe.wait_ge(v1_even, G)
            pe.wait_ge(v1_odd, G)

            pe.wait_ge(ld_f0, 16 * N_F0)
            pe.wait_ge(c_misc, 2)
            pe.wait_ge(w0_split, 8)

            def encode(g):
                pe.wait_ge(xnT_done, g + (LN_B + 1))
                since(pe, sp_done, g * 2, 0)
                for k in range(2):
                    mm(bank[1 + k][:], enc_w[:, P * k:P * (k + 1)], xnT[:], start=True, stop=True).then_inc(enc_ps, 1)

            def to_continuous(g):
                pe.wait_ge(sp_done, g * 2 + 2)
                since(pe, cont_lo, g, 0)
                for k in range(2):
                    last = mm(bank[3][:], s2c_w[:, k, :, :].rearrange("p r m -> p (r m)"), spT[:, k, :],
                              start=(k == 0), stop=(k == 1))
                last.then_inc(cont_ps, 1)

            def router_hidden(g):
                pe.wait_ge(cont_lo, g + 1)
                since(pe, t_done, g, 0)
                for k, w in enumerate((r_w1_hi, r_w1_lo)):
                    last = mm(bank[4][:], w[:], cont[:, ds(g * N, N)], start=(k == 0), stop=(k == 1))
                last.then_inc(r1_ps, 1)

            def logits0(g):
                pe.wait_ge(t_done, g + 1)
                since(pe, lg_done, g, 0)
                for t in range(TPG):
                    last = mm(bank[5][:, t * E:(t + 1) * E], tT[:, P * t:P * (t + 1)], r_w2[:],
                              start=True, stop=True)
                last.then_inc(lg_ps, 1)

            for k in range(G + 1):
                if 1 <= k <= G:
                    to_continuous(k - 1)
                if k < G:
                    ln_transpose(LN_B + k)
                if k >= 2:
                    logits0(k - 2)
                if k < G:
                    encode(k)
                if 1 <= k <= G:
                    router_hidden(k - 1)

            def hidden0(g, e):
                since(pe, relu_done, g * E, e - 1)
                for k, w in enumerate((we1_hi, we1_lo)):
                    last = mm(bank[e % 2][:], w[:, e, :], cont[:, ds(g * N, N)], start=(k == 0), stop=(k == 1))
                last.then_inc(h_ps, 1)

            def gate0(g, e):
                since(pe, gh_done, g * E, e - 1)
                mm(bank[2 + e % 2][:], esel[:, P * e:P * (e + 1)], gT[:, ds(g * N, N)],
                   start=True, stop=True).then_inc(gb0_ps, 1)

            def expert0(g, e):
                pe.wait_ge(gh_lo_done, g * E + e + 1)
                if e == 0:
                    since(pe, oS_lo, g, 0)
                    mm(bank[4][:], be2_w[:], gT[:, ds(g * N, N)], start=True, stop=False, skip_group_check=True)
                for k, (w, h) in enumerate(((we2_hi, gh_hi), (we2_hi, gh_lo), (we2_lo, gh_hi))):
                    last = mm(bank[4][:], w[:, e, :, :].rearrange("p r m -> p (r m)"), h[:, e % 4, :],
                              start=False, stop=(e == E - 1 and k == 2), skip_group_check=True)
                last.then_inc(y_ps, 1)

            def spikes(g):
                pe.wait_ge(oS_lo, g + 1)
                since(pe, sp2_done, g * 2, 0)
                for k in range(2):
                    for i, w in enumerate((c2s_hi, c2s_lo)):
                        last = mm(bank[5 + k][:], w[:, P * k:P * (k + 1)], oS[:], start=(i == 0), stop=(i == 1))
                    last.then_inc(c2s_ps, 1)

            def decode(g):
                pe.wait_ge(sp2_done, g * 2 + 2)
                since(pe, dc_done, g, 0)
                mm(bank[7][:], ones3[:], bsplit[:, 0:D].unsqueeze(1).broadcast_to([3, TPG, D]),
                   start=True, stop=False, skip_group_check=True)
                for t in range(TPG):
                    for k in range(2):
                        last = mm(bank[7][:, D * t:D * (t + 1)], sp2T[:, k, P * t:P * (t + 1)], dec_w[:, k, :],
                                  start=False, stop=(k == 1), skip_group_check=True)
                last.then_inc(dec_ps, 1)

            LAG = 3

            def gates_T(k):
                pe.wait_ge(gsp_done, 3 * k + 3)
                for bk, lo, hi in RUN_BANKS[k]:
                    for b in range(lo, hi):
                        last = tr(bank[bk][:].bitcast(BF16)[0:96, P * (b - lo):P * (b - lo + 1)], gsp[:, b, :],
                                  ident_h[:])
                    last.then_inc(gT_ps, 1)

            pe.wait_ge(c_split, 1)
            pe.wait_ge(be2_step, 9)
            pe.wait_ge(c_idh, 1)
            hidden0(0, 0)
            hidden0(0, 1)
            pe.wait_ge(xnT_done, LN_B + G)
            gates_T(0)
            logits0(G - 1)
            pe.wait_ge(c_esel_all, 2)
            pe.wait_ge(gT_done, transposes(0))
            for g in range(G):
                for e in range(E):
                    if g or e >= 2:
                        hidden0(g, e)
                    gate0(g, e)
                    if e >= LAG:
                        expert0(g, e - LAG)
                    elif g:
                        expert0(g - 1, E - LAG + e)
                    if g == 0 and e == 7:
                        gates_T(1)
                        pe.wait_ge(gT_done, transposes(1))
                    if g and e == 3:
                        spikes(g - 1)
                    if g and e == 6:
                        decode(g - 1)

            def q1(g, bank_t, bank_q):
                ln_transpose(LN_C + g, bank_t)
                pe.wait_ge(xnT_done, LN_C + g + 1)
                since(pe, q1_done, g, 0)
                mm(bank[bank_q][:], w1T[:, 0, :], xnT[:], start=True, stop=True).then_inc(q1_ps, 1)

            pe.wait_ge(gh_done, G * E)
            q1(0, 3, 2)
            for e in range(E - LAG, E):
                expert0(G - 1, e)
            q1(1, 3, 2)
            spikes(G - 1)
            decode(G - 1)
            q1(2, 3, 2)

            pe.wait_ge(hide_done, 1)
            pe.wait_ge(c_idh, 1)
            pe.wait_ge(c_ones, 3)
            pe.wait_ge(relu_done, G * E)
            pe.wait_ge(q1_done, G - 1)
            pe.wait_ge(xnT_done, LN_C + G - 1)
            pe.wait_ge(sp2_done, 2 * G)

            def scores1(b, j, between):
                hide = hide1[:, ds(b, 1), :]
                for bk, lo, n_s, nh, o in ((0, 0, SA, NH // 2, 0), (1, 0, SA, NH // 2, CA // 2), (2, SA, SB, NH, CA)):
                    since(pe, s1_shifted, b * 3, bk - 2)
                    mm(bank[bk][:, 0:nh * n_s], ident_h[:], hide[:, :, lo:lo + n_s].broadcast_to([P, nh, n_s]),
                       start=True, stop=False, skip_group_check=True)
                    if bk == 0:
                        pe.wait_ge(qt_done, b + 1)
                        pe.wait_ge(kb_done, b * 2 + 2)
                    mm(bank[bk][:, 0:nh * n_s], qt[:, j % 2, :], kblk[:, j % 4, o:o + nh * n_s],
                       start=False, stop=True, skip_group_check=True).then_inc(s1_ps, 1)
                    if bk == 0:
                        between()

            def weights_T(b, j):
                pe.wait_ge(e1_done, b + 1)
                pe.wait_ge(pTa_done, b)
                for c in range(NA):
                    last = tr(bank[3 + c // 4][:, P * (c % 4):P * (c % 4 + 1)], e1[:, j % 2, P * c:P * (c + 1)], ident[:])
                last.then_inc(pTa_ps, 1)
                pe.wait_ge(pTb_done, b)
                for c in range(2):
                    last = tr(bank[5][0:RB, P * c:P * (c + 1)], e1[:, j % 2, CA + RB * c:CA + RB * (c + 1)], ident[:])
                last.then_inc(pTb_ps, 1)

            def values1(b, j):
                pe.wait_ge(at1_done, b)
                pe.wait_ge(vt_done, b + 1)
                pe.wait_ge(pTb_done, b + 1)
                for c in range(2):
                    mm(bank[6][:, E * DV * c:E * DV * (c + 1)], pTb[:, j % 2, P * c:P * (c + 1)],
                       vt[0:RB, j % 2, 1, E * DV * c:E * DV * (c + 1)], start=(c == 0), stop=False, skip_group_check=True)
                pe.wait_ge(pTa_done, b + 1)
                for c in range(NA):
                    last = mm(bank[6][:, 2 * DV * c:2 * DV * (c + 1)], pTa[:, j % 2, P * c:P * (c + 1)],
                              vt[:, j % 2, 0, 2 * DV * c:2 * DV * (c + 1)], start=False, stop=True, skip_group_check=True)
                last.then_inc(o1_ps, 1)

            def heads_T(b, j):
                pe.wait_ge(at1_done, b + 1)
                pe.wait_ge(x3_done, b)
                tr(bank[7][:, 0:P], at1[:, j % 2, :, :].rearrange("p h d -> p (h d)"), ident[:]).then_inc(at1T_ps, 1)

            def project1(b):
                pe.wait_ge(at1T_done, b + 1)
                mm(bank[7][:, P:2 * P], ones3[:], bsplit[:, D:2 * D], start=True, stop=False,
                   skip_group_check=True)
                mm(bank[7][:, P:2 * P], at1T[:], w1T[:, 3, :], start=False, stop=True,
                   skip_group_check=True).then_inc(y1_ps, 1)

            def logits1(g, bk=6, o=LG1):
                pe.wait_ge(xnT_done, g + (LN_D + 1))
                for t in range(TPG):
                    last = mm(bank[bk][:, o + t * E:o + (t + 1) * E], xnT[:, P * t:P * (t + 1)], wr[:],
                              start=True, stop=True)
                last.then_inc(lg_ps, 1)


            def product(to, w_hi, w_lo, g):
                for k, (w, t) in enumerate(((w_hi, wide_hi), (w_hi, wide_lo), (w_lo, wide_hi))):
                    last = mm(to, w, t[:, ds(g * N, N)], start=(k == 0), stop=(k == 2))
                return last

            def hidden_half(g, j):
                c = slice(P * j, P * (j + 1))
                since(pe, sil_done, g * NB, j - 1)
                product(bank[j % 2][:], w1_hi[:, c], w1_lo[:, c], g).then_inc(fh_ps, 1)

            def other_half(g, j):
                c = slice(P * j, P * (j + 1))
                since(pe, u1_done, g * NB, j - 1)
                product(bank[2 + j % 2][:], w3_hi[:, c], w3_lo[:, c], g).then_inc(fg_ps, 1)

            def gate1(g, j):
                if j % 3 < 2:
                    e = 2 * (j // 3) + j % 3
                    since(pe, act_done, g * ACTS, acts(j - 2))
                    mm(bank[4 + j % 3][:], esel[:, P * e:P * (e + 1)], gT[:, ds(g * N, N)],
                       start=True, stop=True).then_inc(gb_ps, 1)

            def attention1(b, j, first, logits_before=None, before_weights=lambda: None):
                turn = lambda: heads_T(b - 3, j - 3) if first >= 3 else None
                if first < B:
                    scores1(b, j, turn)
                else:
                    turn()
                if first >= 3:
                    project1(b - 3)
                if logits_before is not None:
                    pe.wait_ge(lg_done, logits_before)
                if 2 <= first < B + 2:
                    values1(b - 2, j - 2)
                before_weights()
                if 1 <= first < B + 1:
                    weights_T(b - 1, j - 1)

            for b in range(4):
                if b == 3:
                    pe.wait_ge(ld_f1, 16 * N_F1)
                    pe.wait_ge(dc_done, G)
                    q1(G - 1, 7, 7)
                    pe.wait_ge(q1_done, G)
                attention1(b, b, b)
            with pe.Fori(1, G) as i:
                def router_T():
                    pe.wait_ge(x3_done, i * 4 + 1)
                    ln_transpose(i + (LN_D - 1))

                for j in range(4):
                    attention1(i * 4 + j, j, 4, i + (G - 1) if j == 0 else None,
                               router_T if j == 3 else lambda: None)
                pe.wait_ge(at1_done, i * 4 + 2)
                logits1(i - 1)
            pe.wait_ge(f_split, 6)
            pe.wait_ge(wide_done, 2)
            pe.wait_ge(s1_shifted, 3 * B)
            hidden_half(0, 0)
            other_half(0, 0)
            attention1(B, B, B, 2 * G - 1)
            hidden_half(0, 1)
            attention1(B + 1, B + 1, B + 1)
            pe.wait_ge(pTa_done, B)
            other_half(0, 1)
            attention1(B + 2, B + 2, B + 2)

            gates_T(2)

            def output1(g, j):
                pe.wait_ge(act_lo_done, g * NB + j + 1)
                if j == 0:
                    since(pe, yT_done, g, 0)
                for k, (w, h) in enumerate(((w2_hi, act_hi), (w2_hi, act_lo), (w2_lo, act_hi))):
                    last = mm(bank[6][:], w[:, j, :], h[:, j % 4, :], start=(j == 0 and k == 0),
                              stop=(j == NB - 1 and k == 2), skip_group_check=True)
                last.then_inc(fy_ps, 1)

            def result(g):
                pe.wait_ge(yT_done, g + 1)
                since(pe, res_done, g, 0)
                for t in range(TPG):
                    last = tr(bank[7][:, P * t:P * (t + 1)], yT[:, P * t:P * (t + 1)], ident[:])
                last.then_inc(y_tok_ps, 1)

            def mixture1(g, before):
                for j in range(NB):
                    if before or j >= 2:
                        hidden_half(g, j)
                        other_half(g, j)
                    gate1(g, j)
                    if j >= LAG:
                        output1(g, j - LAG)
                    elif before:
                        output1(g - 1, NB - LAG + j)
                    if before and j == 4:
                        result(g - 1)
                    if not before and j == 1:
                        pe.wait_ge(x3_done, B)
                        ln_transpose(LN_D + G - 1)
                    if not before and j == 2:
                        logits1(G - 1, 7, 0)
                    if not before and j == 7:
                        gates_T(3)

            pe.wait_ge(wide_done, 2 * (G - 1))
            pe.wait_ge(gT_done, transposes(2))
            mixture1(0, False)
            pe.wait_ge(gT_done, transposes(3))
            with pe.Fori(1, G) as g:
                mixture1(g, True)
            for j in range(NB - LAG, NB):
                output1(G - 1, j)
            result(G - 1)

        @block.scalar
        def _(act_e):
            fn = nc.scalar.activation
            v = a
            act_e.dma_start(wk0[:], v["L0_xattn_Wk"]).then_inc(ld_w0, 16)
            act_e.dma_start(wv0[:], v["L0_xattn_Wv"]).then_inc(ld_w0, 16)
            act_e.dma_start(wq0[:], v["L0_xattn_Wq"]).then_inc(ld_w0, 16)
            act_e.dma_start(bv0[:], v["L0_xattn_bv"].unsqueeze(0).broadcast_to([SC, D])).then_inc(ld_w0, 16)

            for i in range(3):
                n = min(6, B - 6 * i)
                act_e.wait_ge(ctxT_lo, i + 1)
                src = bank[i][:, 0:n * SC].rearrange("p (b s) -> p b s", s=SC)[:, :, SA:SC]
                nc.scalar.copy(ctxT[:, 6 * i:6 * i + n, 2 * SA:CT].rearrange("p b (r s) -> p b r s", r=E),
                               src.unsqueeze(2).broadcast_to([P, n, E, SB])).then_inc(ctxT_hi, 1)
            act_e.wait_ge(vc_done, 1)
            for i in range(3):
                n = min(6, B - 6 * i)
                act_e.wait_ge(k_ps, i + 1)
                fn(k0T[:, 6 * SC * i:6 * SC * i + n * SC], bank[4 + i][:, 0:n * SC], ACT.Identity,
                   bias=col("bk0")).then_inc(k0_done, 1)

            def ln_copy(n, read, count, bk=7):
                act_e.wait_ge(xnT_ps, n + 1)
                since(act_e, read, count, 0)
                nc.scalar.copy(xnT[:], bank[bk][:]).then_inc(xnT_done, 1)

            def exp0(g):
                act_e.wait_ge(s0_shifted, g + 1)
                fn(e0[:], e0[:], ACT.Exp).then_inc(e0_done, 1)

            def q0_copy(g):
                act_e.wait_ge(q0_ps, g + 1)
                since(act_e, s0_ps, g, 0)
                fn(q0T[:], bank[1][:], ACT.Identity, bias=bqs[:, 0:1], scale=float(D) ** -0.5).then_inc(q0_done, 1)

            def weights0_copy(g):
                act_e.wait_ge(at0_ps, g + 1)
                since(act_e, o0_ps, g, 0)
                nc.scalar.copy(at0T[:], bank[3][0:SC, :]).then_inc(at0_done, 1)

            act_e.wait_ge(bqs_done, 2)
            for k in range(G + 1):
                if k < G:
                    ln_copy(LN_A + k, q0_ps, k)
                if k >= 1:
                    exp0(k - 1)
                if k < G:
                    q0_copy(k)
                if k >= 1:
                    weights0_copy(k - 1)

            act_e.wait_ge(w1T_ps, 1)
            nc.scalar.copy(w1T[:].rearrange("p i d -> p (i d)"), bank[6][:]).then_inc(w1T_done, 1)
            for i, bk in enumerate((5, 0, 6)):
                n = min(6, B - 6 * i)
                act_e.wait_ge(k_ps, 4 + i)
                fn(k1T[:, 6 * i:6 * i + n, :].rearrange("p b s -> p (b s)"), bank[bk][:, 0:n * SC], ACT.Identity,
                   bias=col("bk1")).then_inc(k1_done, 1)
            act_e.wait_ge(c_zero, 1)
            for i in range(G):
                act_e.wait_ge(v1_ps, i + 1)
                src = bank[1 + i][SA:P, :].rearrange("p (t c r d) -> p t c r d", t=TPG, r=2, d=DH)
                nc.scalar.copy(v1a[SA:P, TPG * i:TPG * (i + 1), :, 1, 0:DH], src[:, :, :, 1, :]).then_inc(v1_odd, 1)

            def sigmoid_enc(g):
                for k in range(2):
                    act_e.wait_ge(enc_ps, 2 * g + k + 1)
                    since(act_e, cont_ps, g, 0)
                    fn(spT[:, k, :], bank[1 + k][:], ACT.Sigmoid, bias=col(f"enc{k}")).then_inc(sp_done, 1)

            def tanh_router(g):
                act_e.wait_ge(r1_ps, g + 1)
                since(act_e, lg_ps, g, 0)
                act_e.wait_ge(c_misc, 1)
                fn(tT[0:M0, :], bank[4][0:M0, :], ACT.Tanh, bias=col("rb1", M0)).then_inc(t_done, 1)

            def gate_weights(k):
                act_e.wait_ge(gd_done, k + 1)
                t = slice(*RUN_TILES[k])
                fn(gw[:, 0, t], gd[:, t], ACT.Sigmoid, scale=-1.0).then_inc(gw_done, 1)
                fn(gw[:, 1, t], gd[:, t], ACT.Sigmoid).then_inc(gw_done, 1)

            def cont_high(g):
                act_e.wait_ge(cont_ps, g + 1)
                fn(cont[:, N * g:N * (g + 1)], bank[3][:], ACT.Identity, bias=col("s2c")).then_inc(cont_hi, 1)

            for k in range(G + 1):
                if k == G:
                    gate_weights(0)
                if k >= 1:
                    cont_high(k - 1)
                if k < G:
                    ln_copy(LN_B + k, enc_ps if k else q0_ps, 2 * k or G)
                    sigmoid_enc(k)
                if k >= 1:
                    tanh_router(k - 1)
                if k == 1:
                    act_e.wait_ge(c_esel, 3)
                    for r in (32, 64):
                        nc.scalar.copy(esel[r:r + 32, :], esel[0:32, :]).then_inc(c_esel_all, 1)

            def relu0(g, e):
                act_e.wait_ge(h_ps, g * E + e + 1)
                since(act_e, gh_done, g * E, e - 1)
                fn(hid[:, e % 2, :], bank[e % 2][:], ACT.Relu, bias=col(f"be1_{e}")).then_inc(relu_done, 1)

            def gated_high(g, e):
                act_e.wait_ge(gh_done, g * E + e + 1)
                since(act_e, y_ps, g * E, e - 3)
                nc.scalar.copy(gh_hi[:, e % 4, :], gh[(g * E + e) % 3]).then_inc(gh_hi_done, 1)

            def mix_high(g):
                act_e.wait_ge(y_ps, g * E + E)
                since(act_e, c2s_ps, g * 2, 0)
                nc.scalar.copy(oS[:], bank[4][:]).then_inc(oS_hi, 1)

            def sigmoid_c2s(g):
                since(act_e, dec_ps, g, 0)
                for k in range(2):
                    act_e.wait_ge(c2s_ps, g * 2 + k + 1)
                    fn(sp2T[:, k, :], bank[5 + k][:], ACT.Sigmoid, bias=col(f"c2s{k}")).then_inc(sp2_done, 1)

            def sigmoid_dec(g):
                act_e.wait_ge(dec_ps, g + 1)
                since(act_e, dn_done, g * TPG, 0)
                fn(dc[:].rearrange("p t d -> p (t d)"), bank[7][:], ACT.Sigmoid).then_inc(dc_done, 1)

            for g in range(G):
                for e in range(E):
                    if g and e == 3:
                        mix_high(g - 1)
                    relu0(g, e)
                    if e >= 1:
                        gated_high(g, e - 1)
                    elif g:
                        gated_high(g - 1, E - 1)
                    if g == 0 and e == 4:
                        gate_weights(1)
                    if g and e == 4:
                        sigmoid_c2s(g - 1)
                    if g and e == 7:
                        sigmoid_dec(g - 1)
            gated_high(G - 1, E - 1)

            def q1_copy(g, bank_t, bank_q):
                ln_copy(LN_C + g, q1_ps if g else enc_ps, g or 2 * G, bank_t)
                act_e.wait_ge(q1_ps, g + 1)
                fn(wideT[:, N * g:N * (g + 1)], bank[bank_q][:], ACT.Identity, bias=bqs[:, 1:2],
                   scale=float(DH) ** -0.5).then_inc(q1_done, 1)

            q1_copy(0, 3, 2)
            mix_high(G - 1)
            q1_copy(1, 3, 2)
            sigmoid_c2s(G - 1)
            sigmoid_dec(G - 1)
            q1_copy(2, 3, 2)

            def weights_copy(b, j):
                act_e.wait_ge(pTa_ps, b + 1)
                since(act_e, o1_ps, b, -1)
                for k in range(2):
                    last = nc.scalar.copy(pTa[:, j % 2, 512 * k:512 * (k + 1)], bank[3 + k][:])
                last.then_inc(pTa_done, 1)
                act_e.wait_ge(pTb_ps, b + 1)
                nc.scalar.copy(pTb[:, j % 2, :], bank[5][0:RB, 0:2 * P]).then_inc(pTb_done, 1)

            def heads_copy(b):
                act_e.wait_ge(at1T_ps, b + 1)
                act_e.wait_ge(y1_ps, b)
                fn(at1T[:], bank[7][:, 0:P], ACT.Identity, bias=col("bv1")).then_inc(at1T_done, 1)

            def exp1(b, j):
                act_e.wait_ge(s1_shifted, b * 3 + 3)
                fn(e1[:, j % 2, :], e1[:, j % 2, :], ACT.Exp).then_inc(e1_done, 1)

            def attention1(b, j, first, between=lambda: None):
                if first >= 3:
                    heads_copy(b - 3)
                between()
                if first < B:
                    exp1(b, j)
                if 1 <= first < B + 1:
                    weights_copy(b - 1, j - 1)

            for b in range(4):
                if b == 3:
                    q1_copy(G - 1, 7, 7)
                attention1(b, b, b)
            act_e.wait_ge(q1_ps, G)
            with act_e.Fori(1, G) as i:
                for j in range(4):
                    attention1(i * 4 + j, j, 4,
                               (lambda: ln_copy(i + (LN_D - 1), lg_ps, i + (G - 1))) if j == 3 else lambda: None)
            attention1(B, B, B)
            attention1(B + 1, B + 1, B + 1)
            gate_weights(2)
            attention1(B + 2, B + 2, B + 2)

            def silu(g, j):
                act_e.wait_ge(fh_ps, g * NB + j + 1)
                since(act_e, u1_done, g * NB, j - 1)
                fn(sil[:, j % 2, :], bank[j % 2][:], ACT.Silu).then_inc(sil_done, 1)

            def act_high(g, j):
                act_e.wait_ge(act_done, g * ACTS + acts(j))
                since(act_e, fy_ps, g * NB, j - 3)
                nc.scalar.copy(act_hi[:, j % 4, :], act[:, j % 2, :]).then_inc(act_hi_done, 1)

            def result(g):
                act_e.wait_ge(fy_ps, g * NB + NB)
                since(act_e, y_tok_ps, g, 0)
                nc.scalar.copy(yT[:], bank[6][:]).then_inc(yT_done, 1)

            def mixture1(g, before):
                for j in range(NB):
                    if before and j == 3:
                        result(g - 1)
                    silu(g, j)
                    if j >= 1:
                        act_high(g, j - 1)
                    elif before:
                        act_high(g - 1, NB - 1)
                    if not before and j == 1:
                        act_e.wait_ge(wide_done, 2 * (G - 1))
                        ln_copy(LN_D + G - 1, lg_ps, 2 * G - 1)
                    if not before and j == 4:
                        gate_weights(3)

            mixture1(0, False)
            with act_e.Fori(1, G) as g:
                mixture1(g, True)
            act_high(G - 1, NB - 1)
            result(G - 1)

        @block.vector
        def _(dve):
            v = nc.vector
            dve.wait_ge(c_id, 2)
            v.tensor_copy(ident_h[:], ident[:]).then_inc(c_idh, 1)

            v.tensor_copy(sel8[:].rearrange("p (k e) -> p k e", e=E),
                          ident[0:E, 0:E].unsqueeze(1).broadcast_to([E, 12, E])).then_inc(be2_step, 1)
            v.tensor_reduce(part_of[:], ident[0:96, 0:96].rearrange("p (k i e) -> p i k e", k=3, i=4),
                            AX.XY, ALU.add).then_inc(be2_step, 1)

            def columns():
                dve.wait_ge(vc_ps, 1)
                v.tensor_copy(vcols[:], bank[7][:, 0:NR]).then_inc(vc_done, 1)
                for i, (name, scale) in enumerate((("bq0", float(D) ** -0.5), ("bq1", float(DH) ** -0.5))):
                    dve.wait_ge(vc_done, 1)
                    v.tensor_scalar(bqs[:, i:i + 1], col(name), scale, None, ALU.mult).then_inc(bqs_done, 1)

            def moments(st, mom, cols, read, steps, base_steps, done):
                m = lambda i: mom[:, i, cols]
                v.tensor_tensor(m(0), st(1), st(4), ALU.add).then_inc(steps, 1)
                v.tensor_tensor(m(1), st(1), st(4), ALU.subtract).then_inc(steps, 1)
                v.scalar_tensor_tensor(out=m(2), in0=st(2), scalar=D * EPS, in1=st(5),
                                       op0=ALU.add, op1=ALU.add).then_inc(steps, 1)
                dve.wait_ge(steps, base_steps + 3)
                v.tensor_scalar(m(3), m(0), 0.5, None, ALU.mult).then_inc(steps, 1)
                v.scalar_tensor_tensor(out=m(4), in0=m(1), scalar=0.25, in1=m(1),
                                       op0=ALU.mult, op1=ALU.mult).then_inc(steps, 1)
                dve.wait_ge(steps, base_steps + 5)
                v.scalar_tensor_tensor(out=m(5), in0=m(2), scalar=1.0 / D, in1=m(4),
                                       op0=ALU.mult, op1=ALU.add).then_inc(done, 1)

            def ln_stats_of(b, s):
                v.bn_stats(stats[:, ds(s, 1), :].rearrange("p o s -> p (o s)"), x[:, ds(b * D, D)]).then_inc(ln_stats, 1)

            def ln_moments_of(n, s, back=G - 1):
                dve.wait_ge(ln_stats, n * TPG + TPG)
                since(dve, ln_applied, n * TPG, -back * TPG)
                moments(lambda k: stats[:, ds(s * TPG, TPG), k], mom, ds(s * TPG, TPG), ln_stats, ln_steps,
                        n * 5, ln_moments)

            def ln_apply(n, g, s):
                dve.wait_ge(ln_rstd, n + 1)
                dve.wait_ge(ln_steps, n * 5 + 4)
                since(dve, xnT_ps, n, 0)
                for t in range(TPG):
                    v.tensor_scalar(xn[:, t, :], x[:, ds(g * N + t * D, D)], mom[:, 3, ds(s * TPG + t, 1)],
                                    rstd[:, ds(s * TPG + t, 1)], ALU.subtract, ALU.mult).then_inc(ln_applied, 1)

            for g in range(G):
                dve.wait_ge(ld_x[g], 16)
                for t in range(TPG):
                    ln_stats_of(TPG * g + t, TPG * g + t)
                ln_moments_of(LN_A + g, g)
                if g == 2:
                    columns()
                for i in range(3):
                    if g == (0, 1, 1)[i]:
                        n = min(6, B - 6 * i)
                        dve.wait_ge(ctxT_ps, i + 1)
                        src = bank[i][:, 0:n * SC].rearrange("p (b s) -> p b s", s=SC)[:, :, 0:SA]
                        v.tensor_copy(ctxT[:, 6 * i:6 * i + n, 0:2 * SA].rearrange("p b (r s) -> p b r s", r=2),
                                      src.unsqueeze(2).broadcast_to([P, n, 2, SA])).then_inc(ctxT_lo, 1)
            ln_apply(LN_A, 0, 0)
            dve.wait_ge(ld_w0, 16 * N_W0)
            for i in range(G):
                dve.wait_ge(v0_ps, i + 1)
                v.tensor_tensor(v0[:, N * i:N * (i + 1)].rearrange("p (t d) -> p t d", d=D),
                                bank[i][0:SC, :].rearrange("p (t d) -> p t d", d=D),
                                bv0[:].unsqueeze(1).broadcast_to([SC, TPG, D]), ALU.add).then_inc(v0_done, 1)

            def shift0(g):
                dve.wait_ge(s0_ps, g + 1)
                since(dve, at0_ps, g, 0)
                since(dve, sum0_done, g, 0)
                v.scalar_tensor_tensor(out=e0[:].rearrange("p t s -> p (t s)"),
                                       in0=mask0[:, TPG * SC * g:TPG * SC * (g + 1)], scalar=-1e9,
                                       in1=bank[2][:, 0:TPG * SC], op0=ALU.mult, op1=ALU.add).then_inc(s0_masked, 1)
                dve.wait_ge(s0_masked, g + 1)
                since(dve, s0_shifted, g, 0)
                v.tensor_reduce(m0[:], e0[:], AX.X, ALU.max).then_inc(m0_done, 1)
                dve.wait_ge(m0_done, g + 1)
                v.tensor_tensor(e0[:], e0[:], m0[:].unsqueeze(2).broadcast_to([P, TPG, SC]),
                                ALU.subtract).then_inc(s0_shifted, 1)

            def sums0(g):
                dve.wait_ge(e0_done, g + 1)
                since(dve, r0_done, g, 0)
                v.tensor_reduce(sum0[:], e0[:], AX.X, ALU.add).then_inc(sum0_done, 1)
                dve.wait_ge(sum0_done, g + 1)
                since(dve, x1_done, g * TPG, 0)
                v.reciprocal(r0[:], sum0[:]).then_inc(r0_done, 1)

            def add0(g):
                dve.wait_ge(r0_done, g + 1)
                dve.wait_ge(o0_ps, g + 1)
                dve.wait_ge(ln_applied, TPG * (g + 1))
                for t in range(TPG):
                    xt = x[:, N * g + D * t:N * g + D * (t + 1)]
                    v.scalar_tensor_tensor(out=xt, in0=bank[4][:, D * t:D * (t + 1)], scalar=r0[:, t:t + 1],
                                           in1=xt, op0=ALU.mult, op1=ALU.add).then_inc(x1_done, 1)
                for t in range(TPG):
                    dve.wait_ge(x1_done, TPG * g + t + 1)
                    ln_stats_of(TPG * g + t, TPG * g + t)
                ln_moments_of(LN_B + g, g)

            dve.wait_ge(ld_m0, 16)
            for k in range(G + 2):
                if 1 <= k <= G:
                    shift0(k - 1)
                if k + 1 < G:
                    ln_apply(LN_A + k + 1, k + 1, k + 1)
                if k >= 2:
                    add0(k - 2)
                if 1 <= k <= G:
                    sums0(k - 1)

            dve.wait_ge(ld_bias, 16 * N_BIAS)
            left = [brow[:], bres[:, 0, :], bres[:, 1, :]]
            for i in range(3):
                v.tensor_copy(bpart[:, i, :], left[i]).then_inc(c_step, 1)
                dve.wait_ge(c_step, 2 * i + 1)
                if i < 2:
                    v.tensor_tensor(left[i + 1], left[i], bpart[:, i, :], ALU.subtract).then_inc(c_step, 1)
                    dve.wait_ge(c_step, 2 * i + 2)
            v.tensor_scalar(bsel[:, 0, :], bpart[:, 0, :], ident[0:3, 0:1], None, ALU.mult).then_inc(c_step, 1)
            dve.wait_ge(c_step, 6)
            v.scalar_tensor_tensor(out=bsel[:, 1, :], in0=bpart[:, 1, :], scalar=ident[0:3, 1:2], in1=bsel[:, 0, :],
                                   op0=ALU.mult, op1=ALU.add).then_inc(c_step, 1)
            dve.wait_ge(c_step, 7)
            v.scalar_tensor_tensor(out=bsplit[:], in0=bpart[:, 2, :], scalar=ident[0:3, 2:3], in1=bsel[:, 1, :],
                                   op0=ALU.mult, op1=ALU.add).then_inc(c_split, 1)

            dve.wait_ge(be2_ps, 1)
            dve.wait_ge(be2_step, 2)
            full, left1 = be2_x[:, 0, :], be2_x[:, 1, :]
            v.tensor_copy(full, bank[7][0:96, 0:P]).then_inc(be2_step, 1)
            dve.wait_ge(be2_step, 3)
            v.tensor_copy(be2_p[:, 0, :], full).then_inc(be2_step, 1)
            dve.wait_ge(be2_step, 4)
            v.tensor_tensor(left1, full, be2_p[:, 0, :], ALU.subtract).then_inc(be2_step, 1)
            dve.wait_ge(be2_step, 5)
            v.tensor_copy(be2_p[:, 1, :], left1).then_inc(be2_step, 1)
            dve.wait_ge(be2_step, 6)
            v.tensor_tensor(be2_p[:, 2, :], left1, be2_p[:, 1, :], ALU.subtract).then_inc(be2_step, 1)
            v.tensor_scalar(be2_s[:, 0, :], be2_p[:, 0, :], part_of[:, 0:1], None, ALU.mult).then_inc(be2_step, 1)
            dve.wait_ge(be2_step, 8)
            v.scalar_tensor_tensor(out=be2_s[:, 1, :], in0=be2_p[:, 1, :], scalar=part_of[:, 1:2],
                                   in1=be2_s[:, 0, :], op0=ALU.mult, op1=ALU.add).then_inc(be2_sum, 1)
            dve.wait_ge(be2_sum, 1)
            v.scalar_tensor_tensor(out=be2_w[:], in0=be2_p[:, 2, :], scalar=part_of[:, 2:3],
                                   in1=be2_s[:, 1, :], op0=ALU.mult, op1=ALU.add).then_inc(be2_step, 1)

            ln_apply(LN_B, 0, 0)
            dve.wait_ge(c_ones, 3)
            for i in range(G):
                dve.wait_ge(v1_ps, i + 1)
                src = bank[1 + i][0:SA, :].rearrange("p (t c r d) -> p t c r d", t=TPG, r=2, d=DH)
                v.tensor_copy(v1a[0:SA, TPG * i:TPG * (i + 1), :, 0, 0:DH], src[:, :, :, 0, :]).then_inc(v1_even, 1)
                v.tensor_tensor(v1b[:, TPG * i:TPG * (i + 1), :, 0:DH],
                                bank[(0, 5, 6, 7)[i]][0:RB, :].rearrange("p (t h d) -> p t h d", t=TPG, d=DH),
                                slot_of[:].rearrange("p c e -> p (c e)").unsqueeze(1).unsqueeze(3)
                                .broadcast_to([RB, TPG, NH, DH]), ALU.mult).then_inc(v1_b, 1)

            S2C = ROWS.index("s2c")

            def cont_low(g):
                dve.wait_ge(cont_hi, g + 1)
                c = slice(N * g, N * (g + 1))
                v.scalar_tensor_tensor(out=cont[M0:P, c], in0=bank[3][M0:P, :], scalar=vcols[M0:P, S2C:S2C + 1],
                                       in1=cont[M0:P, c].bitcast(F32), op0=ALU.add, op1=ALU.subtract).then_inc(cont_lo, 1)

            def logits0_copy(g):
                dve.wait_ge(lg_ps, g + 1)
                v.tensor_copy(lg[:, ds(g * TPG, TPG), :],
                              bank[5][:, 0:TPG * E].rearrange("p (t e) -> p t e", e=E)).then_inc(lg_done, 1)

            def step(n, op):
                op.then_inc(g_step, 1)
                dve.wait_ge(g_step, n)

            def choose(k, i):
                t, n, l = slice(*RUN_TILES[k]), 12 * k + 6 * i, (lg, lg2)[i]
                shape = [P, t.stop - t.start, E]
                wide = lambda y: y[:, i, t].unsqueeze(2).broadcast_to(shape)
                if i == 0:
                    dve.wait_ge(lg_done, RUN_LOGITS[k])
                step(n + 1, v.tensor_reduce(gmx[:, i, t], l[:, t], AX.X, ALU.max))
                step(n + 2, v.tensor_tensor(geq[:, i, t], l[:, t], wide(gmx), ALU.is_equal))
                step(n + 3, v.tensor_tensor(gkey[:, i, t], geq[:, i, t], rank[:].unsqueeze(1).broadcast_to(shape), ALU.mult))
                step(n + 4, v.tensor_reduce(gkx[:, i, t], gkey[:, i, t], AX.X, ALU.max))
                step(n + 5, v.tensor_tensor(goh[:, i, t], gkey[:, i, t], wide(gkx), ALU.is_equal))
                if i == 0:
                    step(n + 6, v.scalar_tensor_tensor(out=lg2[:, t], in0=goh[:, 0, t], scalar=NEG_BIG, in1=lg[:, t],
                                                       op0=ALU.mult, op1=ALU.add))
                else:
                    v.tensor_tensor(gd[:, t], gmx[:, 1, t], gmx[:, 0, t], ALU.subtract).then_inc(gd_done, 1)

            def weigh(k):
                t = slice(*RUN_TILES[k])
                for i in range(2):
                    dve.wait_ge(gw_done, 2 * k + i + 1)
                    last = v.tensor_tensor(gwo[:, i, t], goh[:, i, t],
                                           gw[:, i, t].unsqueeze(2).broadcast_to([P, t.stop - t.start, E]), ALU.mult)
                step(12 * k + 12, last)
                v.tensor_tensor(gates[:, t], gwo[:, 0, t], gwo[:, 1, t], ALU.add).then_inc(gates_done, 1)

            def split_gates(k):
                t = slice(*RUN_TILES[k])
                dve.wait_ge(gates_done, k + 1)
                dve.wait_ge(c_misc, k // 2 + 3)
                left = (gates[:, t], gres[:, 0, t], gres[:, 1, t])
                for p in range(3):
                    v.tensor_copy(gsp[:, t, 32 * p:32 * p + 3 * E].rearrange("p b (i e) -> p b i e", i=3),
                                  left[p].unsqueeze(2).broadcast_to([P, t.stop - t.start, 3, E])).then_inc(gsp_done, 1)
                    if p < 2:
                        dve.wait_ge(gsp_done, 3 * k + p + 1)
                        v.tensor_tensor(left[p + 1], left[p], gsp[:, t, 32 * p:32 * p + E],
                                        ALU.subtract).then_inc(gres_done, 1)
                        dve.wait_ge(gres_done, 2 * k + p + 1)

            def gT_copy(k):
                for i, (bk, lo, hi) in enumerate(RUN_BANKS[k]):
                    dve.wait_ge(gT_ps, transposes(k - 1) + i + 1)
                    v.tensor_copy(gT[:, P * lo:P * hi],
                                  bank[bk][:].bitcast(BF16)[0:96, 0:P * (hi - lo)]).then_inc(gT_done, 1)

            ln_apply(LN_B + 1, 1, 1)
            for k in range(1, G + 1):
                if k == G:
                    weigh(0)
                cont_low(k - 1)
                if k + 1 < G:
                    ln_apply(LN_B + k + 1, k + 1, k + 1)
                if k >= 2:
                    logits0_copy(k - 2)
                if k == G - 1:
                    choose(0, 0)
                    choose(0, 1)
                if k == G:
                    split_gates(0)

            def gate_hidden(g, e):
                dve.wait_ge(relu_done, g * E + e + 1)
                dve.wait_ge(gb0_ps, g * E + e + 1)
                since(dve, gh_lo_done, g * E, e - 2)
                v.tensor_tensor(gh[(g * E + e) % 3], bank[2 + e % 2][:], hid[:, e % 2, :], ALU.mult).then_inc(gh_done, 1)

            def mix_low(g):
                dve.wait_ge(oS_hi, g + 1)
                v.tensor_tensor(oS[M0:P, :], bank[4][M0:P, :], oS[M0:P, :].bitcast(F32), ALU.subtract).then_inc(oS_lo, 1)

            SPLITS = [(1, 0), (1, 1), (1, 3), (1, 5), (2, 3), (3, 3)]

            def split_weights(i):
                whole, hi, lo = ((f_w1[:], w1_hi[:], w1_lo[:]), (f_w3[:], w3_hi[:], w3_lo[:]),
                                 (f_w2[:], w2_hi[:], w2_lo[:]))[i // 2]
                if i == 0:
                    dve.wait_ge(ld_f1, 16 * N_F1)
                    dve.wait_ge(v1_ps, G)
                    dve.wait_ge(o0_ps, G)
                else:
                    dve.wait_ge(f_split, i)
                if i % 2 == 0:
                    v.tensor_copy(hi, whole).then_inc(f_split, 1)
                else:
                    v.tensor_tensor(lo, whole, hi.bitcast(F32), ALU.subtract).then_inc(f_split, 1)

            def decoded_moments(g):
                dve.wait_ge(dc_done, g + 1)
                since(dve, lo_moments, g, 0)
                for t in range(TPG):
                    v.bn_stats(stats2[:, t, :], dc[:, t, :]).then_inc(lo_stats, 1)
                dve.wait_ge(lo_stats, g * TPG + TPG)
                since(dve, dn_done, g * TPG, 0)
                since(dve, lo_rstd, g, 0)
                moments(lambda k: stats2[:, :, k], mom2, slice(0, TPG), lo_stats, lo_steps, g * 5, lo_moments)

            def decoded_apply(g):
                dve.wait_ge(lo_rstd, g + 1)
                dve.wait_ge(lo_steps, g * 5 + 4)
                since(dve, dg_done, g, 0)
                for t in range(TPG):
                    v.tensor_scalar(dn[:, t, :], dc[:, t, :], mom2[:, 3, t:t + 1], rstd2[:, t:t + 1],
                                    ALU.subtract, ALU.mult).then_inc(dn_done, 1)

            def decoded_gain(g):
                dve.wait_ge(dn_done, g * TPG + TPG)
                since(dve, x2_done, g, 0)
                v.tensor_tensor(dg[:], dn[:], ln_g[:].unsqueeze(1).broadcast_to([P, TPG, D]), ALU.mult).then_inc(dg_done, 1)

            def add2(g):
                dve.wait_ge(dg_done, g + 1)
                dve.wait_ge(xb_done, g + 1)
                v.tensor_tensor(x[:, N * g:N * (g + 1)], dg[:].rearrange("p t d -> p (t d)"), xb[:], ALU.add).then_inc(x2_done, 1)

            def stats2_of(g):
                dve.wait_ge(x2_done, g + 1)
                for t in range(TPG):
                    ln_stats_of(g * TPG + t, g * TPG + t)
                ln_moments_of(g + LN_C, g)

            gT_copy(0)
            logits0_copy(G - 1)
            for g in range(G):
                for e in range(E):
                    if g and e == 3:
                        mix_low(g - 1)
                    gate_hidden(g, e)
                    if g == 0 and e == 2:
                        choose(1, 0)
                    if g == 0 and e == 3:
                        choose(1, 1)
                    if g == 0 and e == 4:
                        weigh(1)
                    if g == 0 and e == 5:
                        split_gates(1)
                    if g == 0 and e == 7:
                        gT_copy(1)
                    if (g, e) in SPLITS:
                        split_weights(SPLITS.index((g, e)))
                    if g and e == 7:
                        decoded_moments(g - 1)
                    if g >= 2 and e == 1:
                        decoded_apply(g - 2)
                    if g >= 2 and e == 3:
                        decoded_gain(g - 2)
                    if g >= 2 and e == 4:
                        add2(g - 2)
                    if g >= 2 and e == 5:
                        stats2_of(g - 2)
            ln_apply(LN_C, 0, 0)
            decoded_apply(G - 2)
            decoded_gain(G - 2)
            add2(G - 2)
            ln_apply(LN_C + 1, 1, 1)
            stats2_of(G - 2)
            mix_low(G - 1)
            ln_apply(LN_C + 2, 2, 2)
            decoded_moments(G - 1)

            def shift1(b, j, between, b_added):
                for k in range(3):
                    dve.wait_ge(s1_ps, b * 3 + k + 1)
                    if k == 0:
                        dve.wait_ge(mx_done, b)
                    if k < 2:
                        v.tensor_reduce(mxa[:, 8 * k:8 * (k + 1)], bank[k][:].rearrange("p (h s) -> p h s", s=SA),
                                        AX.X, ALU.max).then_inc(mxab_done, 1)
                    else:
                        v.tensor_reduce(mxb[:], bank[2][:, 0:CB].rearrange("p (h s) -> p h s", h=NH),
                                        AX.X, ALU.max).then_inc(mxab_done, 1)
                dve.wait_ge(mxab_done, b * 3 + 3)
                dve.wait_ge(s1_shifted, b * 3)
                v.tensor_tensor(mx[:], mxa[:], mxb[:], ALU.max).then_inc(mx_done, 1)
                dve.wait_ge(mx_done, b + 1)
                since(dve, pTb_ps, b, -1)
                for k in range(2):
                    v.tensor_tensor(e1[:, j % 2, 512 * k:512 * (k + 1)].rearrange("p (h s) -> p h s", s=SA),
                                    bank[k][:].rearrange("p (h s) -> p h s", s=SA),
                                    mx[:, 8 * k:8 * (k + 1)].unsqueeze(2).broadcast_to([P, 8, SA]),
                                    ALU.subtract).then_inc(s1_shifted, 1)
                    if k == 0:
                        between()
                if b_added is not None:
                    dve.wait_ge(x3_done, b_added + 1)
                v.tensor_tensor(e1[:, j % 2, CA:CA + CB].rearrange("p (h s) -> p h s", s=SB),
                                bank[2][:, 0:CB].rearrange("p (h s) -> p h s", s=SB),
                                mx[:].unsqueeze(2).broadcast_to([P, NH, SB]), ALU.subtract).then_inc(s1_shifted, 1)

            def normalize1(b, j):
                dve.wait_ge(o1_ps, b + 1)
                dve.wait_ge(at1_done, b)
                o = bank[6][:, 0:NH * DV].rearrange("p (h v) -> p h v", v=DV)
                v.reciprocal(rs1[:], o[:, :, DH]).then_inc(rs1_done, 1)
                dve.wait_ge(rs1_done, b + 1)
                since(dve, at1T_ps, b, -1)
                v.tensor_tensor(at1[:, j % 2, :, :], o[:, :, 0:DH], rs1[:].unsqueeze(2).broadcast_to([P, NH, DH]),
                                ALU.mult).then_inc(at1_done, 1)

            def add1(b):
                dve.wait_ge(y1_ps, b + 1)
                v.tensor_tensor(x[:, ds(b * D, D)], bank[7][:, P:2 * P], x[:, ds(b * D, D)], ALU.add).then_inc(x3_done, 1)

            def attention1(b, j, first, after=lambda: None, after_add=lambda: None):
                def add():
                    if first >= 3:
                        add1(b - 3)
                    after_add()

                if first < B:
                    shift1(b, j, add, b - 3 if first >= 3 else None)
                else:
                    add()
                    dve.wait_ge(x3_done, b - 2)
                if first >= 3:
                    ln_stats_of(b - 3, (j - 3) % 4)
                after()
                if 2 <= first < B + 2:
                    normalize1(b - 2, j - 2)

            def wide_copy(g):
                dve.wait_ge(xnT_done, g + (LN_D + 1))
                v.tensor_copy(wide_hi[:, ds(g * N, N)], xnT[:]).then_inc(wide_done, 1)
                dve.wait_ge(wide_done, g * 2 + 1)
                v.tensor_tensor(wide_lo[:, ds(g * N, N)], xnT[:], wide_hi[:, ds(g * N, N)].bitcast(F32),
                                ALU.subtract).then_inc(wide_done, 1)

            def logits1_copy(g, bk=6, o=LG1):
                dve.wait_ge(lg_ps, g + (G + 1))
                v.tensor_copy(lg[:, ds(g * TPG, TPG), :],
                              bank[bk][:, o:o + TPG * E].rearrange("p (t e) -> p t e", e=E)).then_inc(lg_done, 1)

            for b in range(4):
                attention1(b, b, b)
                if b == 0:
                    decoded_apply(G - 1)
                    decoded_gain(G - 1)
                    add2(G - 1)
                    stats2_of(G - 1)
                if b == 1:
                    ln_apply(LN_C + G - 1, G - 1, G - 1)
            with dve.Fori(1, G) as i:
                attention1(i * 4, 0, 4)
                attention1(i * 4 + 1, 1, 4)
                attention1(i * 4 + 2, 2, 4, lambda: ln_moments_of(i + (LN_D - 1), 0, 0))
                attention1(i * 4 + 3, 3, 4, after_add=lambda: ln_apply(i + (LN_D - 1), i - 1, 0))
                wide_copy(i - 1)
                logits1_copy(i - 1)
            choose(2, 0)
            attention1(B, B, B)
            choose(2, 1)

            def gates_of_run():
                weigh(2)
                split_gates(2)

            attention1(B + 1, B + 1, B + 1, gates_of_run)
            attention1(B + 2, B + 2, B + 2)
            ln_moments_of(LN_D + G - 1, 0, 0)
            gT_copy(2)
            ln_apply(LN_D + G - 1, G - 1, 0)

            def gated(g, j):
                dve.wait_ge(sil_done, g * NB + j + 1)
                dve.wait_ge(fg_ps, g * NB + j + 1)
                since(dve, act_done, g * ACTS, acts(j - 2))
                v.tensor_tensor(u1[:, j % 2, :], bank[2 + j % 2][:], sil[:, j % 2, :], ALU.mult).then_inc(u1_done, 1)
                dve.wait_ge(u1_done, g * NB + j + 1)
                dve.wait_ge(gb_ps, g * E + 2 * (j // 3) + min(j % 3, 1) + 1)
                since(dve, act_lo_done, g * NB, j - 1)
                for bk, rows in (((4, slice(0, P)),), ((4, slice(0, P // 2)), (5, slice(P // 2, P))),
                                 ((5, slice(0, P)),))[j % 3]:
                    v.tensor_tensor(act[rows, j % 2, :], bank[bk][rows, :], u1[rows, j % 2, :],
                                    ALU.mult).then_inc(act_done, 1)

            def result(g):
                dve.wait_ge(y_tok_ps, g + 1)
                v.tensor_tensor(x[:, ds(g * N, N)], bank[7][:], x[:, ds(g * N, N)], ALU.add).then_inc(res_done, 1)

            for j in range(NB):
                gated(0, j)
                if j == 1:
                    wide_copy(G - 1)
                if j == 2:
                    logits1_copy(G - 1, 7, 0)
                    choose(3, 0)
                if j == 3:
                    choose(3, 1)
                if j == 4:
                    weigh(3)
                if j == 5:
                    split_gates(3)
                if j == 7:
                    gT_copy(3)
            with dve.Fori(1, G) as g:
                for j in range(NB):
                    if j == 5:
                        result(g - 1)
                    gated(g, j)
            result(G - 1)


def since(eng, signal, base, k):
    if not (isinstance(base, int) and base + k <= 0):
        eng.wait_ge(signal, base + k)


_INS = ["x", "ctx_1024", "mask_BxSxS2_fk0", "mask_Bx1xSxS2_bf1",
        "L0_xattn_Wq", "L0_xattn_bq", "L0_xattn_Wk", "L0_xattn_bk", "L0_xattn_Wv", "L0_xattn_bv",
        "L0_ffn_enc_W", "L0_ffn_enc_b", "L0_ffn_s2c_W", "L0_ffn_s2c_b", "L0_ffn_rW1", "L0_ffn_rb1",
        "L0_ffn_rW2", "L0_ffn_rb2", "L0_ffn_We1", "L0_ffn_be1", "L0_ffn_We2", "L0_ffn_be2",
        "L0_ffn_c2s_W", "L0_ffn_c2s_b", "L0_ffn_dec_W", "L0_ffn_dec_b", "L0_ffn_ln_g", "L0_ffn_ln_b",
        "L1_xattn_Wq", "L1_xattn_bq", "L1_xattn_Wk", "L1_xattn_bk", "L1_xattn_Wv", "L1_xattn_bv",
        "L1_xattn_W0", "L1_xattn_b0", "L1_ffn_Wr", "L1_ffn_W1", "L1_ffn_W2", "L1_ffn_W3"]


def kernel(**inputs):
    import concourse.bacc as _bacc
    from concourse.bass_utils import run_bass_kernel_spmd as _run

    nc = _bacc.Bacc("TRN2", target_bir_lowering=False, num_devices=1)
    arrays, aps = {}, {}
    for name in _INS:
        v = np.ascontiguousarray(inputs[name])
        if v.dtype == np.bool_:
            v = v.view(np.uint8)
        arrays[f"in_{name}"] = v
        aps[name] = nc.dram_tensor(f"in_{name}", v.shape, mybir.dt.from_np(v.dtype), kind="ExternalInput").ap()
    out = nc.dram_tensor("out", (B, S, D), F32, kind="ExternalOutput").ap()
    xattn_ffn_program(nc, aps, out)
    return _run(nc, [arrays], core_ids=[0]).results[0]["out"]
```
